# Optimizing a Trainium2 kernel written in Bass

```python
import numpy as np
import jax
import jax.numpy as jnp

def _softmax(x, axis=-1):
    return jax.nn.softmax(x, axis=axis)

def _gelu(x):
    return jax.nn.gelu(x, approximate=True)

def _silu(x):
    return jax.nn.silu(x)

def _sigmoid(x):
    return jax.nn.sigmoid(x)

def _layernorm(x, axis=-1, eps=1e-05):
    m = jnp.mean(x, axis=axis, keepdims=True)
    v = jnp.var(x, axis=axis, keepdims=True)
    return (x - m) / jnp.sqrt(v + eps)

def _scatter_add(tgt, idx, src, axis=0):
    return tgt.at[idx].add(src)

def _segment_sum(src, seg, n):
    return jax.ops.segment_sum(src, seg, n)
kernel_name = 'mk_xattn_seq_d4_seqx_r8_53e653'

def setup_inputs(seed: int=0):
    np.random.seed(seed)
    _w = jnp.asarray

    def _rec_inputs():
        import jax
        import jax.numpy as jnp
        _rk = jax.random.key(seed)
        x = -0.0002928 + 1 * jax.random.normal(jax.random.fold_in(_rk, 1), (32, 64, 256), jnp.float32)
        _lenS = 64 - jax.random.randint(jax.random.fold_in(_rk, 7), (32,), 0, max(1, 64 // 4) + 1, jnp.int32)
        _lenS2 = 64 - jax.random.randint(jax.random.fold_in(_rk, 8), (32,), 0, max(1, 64 // 4) + 1, jnp.int32)
        _ctx_2048P = jax.random.normal(jax.random.fold_in(_rk, 11), (32, 16, 256), jnp.float32)
        _ctx_2048c = jax.random.dirichlet(jax.random.fold_in(_rk, 511), 0.3 * jnp.ones((16,), jnp.float32), (32, 64))
        _ctx_2048t = jnp.einsum('bsk,bkd->bsd', _ctx_2048c, _ctx_2048P)
        _ctx_2048t = _ctx_2048t * jax.lax.rsqrt(jnp.mean(jnp.square(_ctx_2048t)) + 1e-12) * 0.953939
        ctx_2048 = -1.39393e-06 + 0.999914 * (_ctx_2048t + 0.3 * jax.random.normal(jax.random.fold_in(_rk, 611), (32, 64, 256), jnp.float32))
        _validS = jnp.arange(64)[None, :] < _lenS[:, None]
        _validS2 = jnp.arange(64)[None, :] < _lenS2[:, None]
        _causal = jnp.tril(jnp.ones((64, 64), dtype=bool))
        mask_Bx1xSxS2_ff0 = jnp.where(jnp.ones((32, 1, 64, 64), dtype=bool), 0.0, -1000000000.0).astype(jnp.float32)
        mask_BxS2_ik0 = jnp.where(jnp.broadcast_to(_validS2[:, :], (32, 64)), 0, 1).astype(jnp.int32)
        return (x, ctx_2048, mask_Bx1xSxS2_ff0, mask_BxS2_ik0)
    x, ctx_2048, mask_Bx1xSxS2_ff0, mask_BxS2_ik0 = _rec_inputs()

    def _L0_xattn_setup():
        import jax, jax.numpy as jnp
        import numpy as np
        EPS = 1e-05

        def _inorm(x):
            m = jnp.mean(x, axis=-1, keepdims=True)
            v = jnp.var(x, axis=-1, keepdims=True)
            return (x - m) * jax.lax.rsqrt(v + EPS)

        def _conv1x1(W, b, x):
            return jnp.einsum('oc,bct->bot', W, x) + b[None, :, None]
        key = jax.random.key(seed)
        ks = jax.random.split(key, 10)
        B, C, T = (4, 64, 256)
        s = 1.0 / np.sqrt(C)
        return {'x_c': jax.random.normal(ks[0], (B, C, T), jnp.float32), 'x_s': jax.random.normal(ks[1], (B, C, T), jnp.float32), 'Wn': jax.random.normal(ks[2], (C, C), jnp.float32) * s, 'bn': jax.random.normal(ks[3], (C,), jnp.float32) * s, 'Wm': jax.random.normal(ks[4], (C, C), jnp.float32) * s, 'bm': jax.random.normal(ks[5], (C,), jnp.float32) * s, 'Wl': jax.random.normal(ks[6], (C, C), jnp.float32) * s, 'bl': jax.random.normal(ks[7], (C,), jnp.float32) * s, 'Wo': jax.random.normal(ks[8], (C, C), jnp.float32) * s, 'bo': jax.random.normal(ks[9], (C,), jnp.float32) * s}
    _L0_xattn_all = _L0_xattn_setup()
    _L0_xattn_in = {k: v for k, v in _L0_xattn_all.items() if k in ('Wn', 'bn', 'Wm', 'bm', 'Wl', 'bl', 'Wo', 'bo')}
    del _L0_xattn_all

    def _L1_xattn_setup():
        import jax, jax.numpy as jnp
        import numpy as np
        B, Q, S1, S2 = (4, 32, 256, 256)
        D, H, K, F = (256, 16, 128, 1024)
        LN_EPS = 1e-05

        def _layer_norm(x, scale, offset):
            mu = jnp.mean(x, axis=-1, keepdims=True)
            var = jnp.var(x, axis=-1, keepdims=True)
            return (x - mu) * jax.lax.rsqrt(var + LN_EPS) * scale + offset

        def _cross_attention(q_in, kv_in, wq, bq, wk, bk, wv, bv, wo, bo, bias_k, bias_v):
            b, q_len, _ = q_in.shape
            t = kv_in.shape[1]
            qh = (q_in @ wq + bq).reshape(b, q_len, H, K)
            kh = (kv_in @ wk + bk).reshape(b, t, H, K)
            vh = (kv_in @ wv + bv).reshape(b, t, H, K)
            kh = jnp.concatenate([kh, jnp.broadcast_to(bias_k, (b, 1, H, K))], axis=1)
            vh = jnp.concatenate([vh, jnp.broadcast_to(bias_v, (b, 1, H, K))], axis=1)
            scale = jnp.sqrt(jnp.asarray(K, q_in.dtype))
            logits = jnp.einsum('bqhk,bthk->bhqt', qh, kh) / scale
            weights = jax.nn.softmax(logits, axis=-1)
            ctx = jnp.einsum('bhqt,bthk->bqhk', weights, vh).reshape(b, q_len, H * K)
            return ctx @ wo + bo

        def _forward(x, xf_1, xf_2, ln1_scale, ln1_offset, wq1, bq1, wk1, bk1, wv1, bv1, wo1, bo1, bias_k1, bias_v1, ln2_scale, ln2_offset, wq2, bq2, wk2, bk2, wv2, bv2, wo2, bo2, bias_k2, bias_v2, ln_mlp_scale, ln_mlp_offset, w_fc1, b_fc1, w_fc2, b_fc2):
            res = x
            h = _layer_norm(x, ln1_scale, ln1_offset)
            x = res + _cross_attention(h, xf_1, wq1, bq1, wk1, bk1, wv1, bv1, wo1, bo1, bias_k1, bias_v1)
            res = x
            h = _layer_norm(x, ln2_scale, ln2_offset)
            x = res + _cross_attention(h, xf_2, wq2, bq2, wk2, bk2, wv2, bv2, wo2, bo2, bias_k2, bias_v2)
            h = _layer_norm(x, ln_mlp_scale, ln_mlp_offset)
            h = jax.nn.gelu(h @ w_fc1 + b_fc1, approximate=False) @ w_fc2 + b_fc2
            return x + h
        key = jax.random.key(seed)
        ks = iter(jax.random.split(key, 64))

        def rn(shape, s=0.02):
            return jax.random.normal(next(ks), shape, jnp.float32) * s
        inp = {'x': rn((B, Q, D), 1.0), 'xf_1': rn((B, S1, D), 1.0), 'xf_2': rn((B, S2, D), 1.0)}
        for i in (1, 2):
            inp[f'ln{i}_scale'] = jnp.ones((D,), jnp.float32)
            inp[f'ln{i}_offset'] = jnp.zeros((D,), jnp.float32)
            inp[f'wq{i}'] = rn((D, H * K))
            inp[f'bq{i}'] = jnp.zeros((H * K,), jnp.float32)
            inp[f'wk{i}'] = rn((D, H * K))
            inp[f'bk{i}'] = jnp.zeros((H * K,), jnp.float32)
            inp[f'wv{i}'] = rn((D, H * K))
            inp[f'bv{i}'] = jnp.zeros((H * K,), jnp.float32)
            inp[f'wo{i}'] = rn((H * K, D))
            inp[f'bo{i}'] = jnp.zeros((D,), jnp.float32)
            inp[f'bias_k{i}'] = rn((1, 1, H, K))
            inp[f'bias_v{i}'] = rn((1, 1, H, K))
        inp['ln_mlp_scale'] = jnp.ones((D,), jnp.float32)
        inp['ln_mlp_offset'] = jnp.zeros((D,), jnp.float32)
        inp['w_fc1'] = rn((D, F))
        inp['b_fc1'] = jnp.zeros((F,), jnp.float32)
        inp['w_fc2'] = rn((F, D))
        inp['b_fc2'] = jnp.zeros((D,), jnp.float32)
        return inp
    _L1_xattn_all = _L1_xattn_setup()
    _L1_xattn_in = {k: v for k, v in _L1_xattn_all.items() if k in ('ln1_scale', 'ln1_offset', 'wq1', 'bq1', 'wk1', 'bk1', 'wv1', 'bv1', 'wo1', 'bo1', 'bias_k1', 'bias_v1', 'ln2_scale', 'ln2_offset', 'wq2', 'bq2', 'wk2', 'bk2', 'wv2', 'bv2', 'wo2', 'bo2', 'bias_k2', 'bias_v2', 'ln_mlp_scale', 'ln_mlp_offset', 'w_fc1', 'b_fc1', 'w_fc2', 'b_fc2')}
    del _L1_xattn_all

    def _L2_xattn_setup():
        import jax, jax.numpy as jnp
        import numpy as np
        H = 256
        NH = 32
        KVH = 8
        HD = H // NH
        GROUPS = NH // KVH
        EPS = 1e-06
        B, L, S = (4, 128, 128)

        def _gqa_forward(hidden_state, encoder_hidden_state, encoder_attention_mask, Wq, bq, Wk, bk, Wv, bv, Wo, bo, gamma, beta):
            b, l, _ = hidden_state.shape
            s = encoder_hidden_state.shape[1]
            q = hidden_state @ Wq + bq
            k = encoder_hidden_state @ Wk + bk
            v = encoder_hidden_state @ Wv + bv
            q = q.reshape(b, l, KVH, GROUPS, HD).transpose(0, 2, 3, 1, 4)
            k = k.reshape(b, s, KVH, HD).transpose(0, 2, 1, 3)
            v = v.reshape(b, s, KVH, HD).transpose(0, 2, 1, 3)
            scale = 1.0 / jnp.sqrt(jnp.asarray(HD, q.dtype))
            scores = jnp.einsum('bkgld,bksd->bkgls', q, k) * scale
            scores = scores + encoder_attention_mask[:, :, None, :, :]
            attn = jax.nn.softmax(scores, axis=-1)
            out = jnp.einsum('bkgls,bksd->bkgld', attn, v)
            out = out.transpose(0, 3, 1, 2, 4).reshape(b, l, H)
            out = out @ Wo + bo
            x = out + hidden_state
            mu = jnp.mean(x, axis=-1, keepdims=True)
            var = jnp.var(x, axis=-1, keepdims=True)
            return (x - mu) * jax.lax.rsqrt(var + EPS) * gamma + beta
        key = jax.random.key(seed)
        ks = jax.random.split(key, 12)
        sd = 0.02
        return {'hidden_state': jax.random.normal(ks[0], (B, L, H), jnp.float32), 'encoder_hidden_state': jax.random.normal(ks[1], (B, S, H), jnp.float32), 'encoder_attention_mask': jnp.zeros((B, 1, L, S), jnp.float32), 'Wq': jax.random.normal(ks[2], (H, H), jnp.float32) * sd, 'bq': jnp.zeros((H,), jnp.float32), 'Wk': jax.random.normal(ks[3], (H, KVH * HD), jnp.float32) * sd, 'bk': jnp.zeros((KVH * HD,), jnp.float32), 'Wv': jax.random.normal(ks[4], (H, KVH * HD), jnp.float32) * sd, 'bv': jnp.zeros((KVH * HD,), jnp.float32), 'Wo': jax.random.normal(ks[5], (H, H), jnp.float32) * sd, 'bo': jnp.zeros((H,), jnp.float32), 'gamma': jnp.ones((H,), jnp.float32), 'beta': jnp.zeros((H,), jnp.float32)}
    _L2_xattn_all = _L2_xattn_setup()
    _L2_xattn_in = {k: v for k, v in _L2_xattn_all.items() if k in ('Wq', 'bq', 'Wk', 'bk', 'Wv', 'bv', 'Wo', 'bo', 'gamma', 'beta')}
    del _L2_xattn_all

    def _L3_xattn_setup():
        import jax, jax.numpy as jnp
        import numpy as np
        B, P, K, H, NH = (4, 256, 32, 256, 16)
        DH = H // NH
        EPS = 1e-06

        def rmsnorm(x, w):
            var = jnp.mean(jnp.square(x), axis=-1, keepdims=True)
            return x * jax.lax.rsqrt(var + EPS) * w
        key = jax.random.key(seed)
        ks = jax.random.split(key, 12)
        s = 0.02
        return {'x': jax.random.normal(ks[0], (B, P, H), jnp.float32), 'latents': jax.random.normal(ks[1], (B, K, H), jnp.float32), 'attention_mask': jax.random.randint(ks[2], (B, P), 0, 2, jnp.int32), 'q_w': s * jax.random.normal(ks[3], (H, H), jnp.float32), 'q_b': jnp.zeros((H,), jnp.float32), 'kv_w': s * jax.random.normal(ks[4], (H, 2 * H), jnp.float32), 'kv_b': jnp.zeros((2 * H,), jnp.float32), 'out_w': s * jax.random.normal(ks[5], (H, H), jnp.float32), 'out_b': jnp.zeros((H,), jnp.float32), 'postnorm_w': jnp.ones((H,), jnp.float32), 'mlp_w1': s * jax.random.normal(ks[6], (H, 4 * H), jnp.float32), 'mlp_b1': jnp.zeros((4 * H,), jnp.float32), 'mlp_w2': s * jax.random.normal(ks[7], (4 * H, H), jnp.float32), 'mlp_b2': jnp.zeros((H,), jnp.float32)}
    _L3_xattn_all = _L3_xattn_setup()
    _L3_xattn_in = {k: v for k, v in _L3_xattn_all.items() if k in ('q_w', 'q_b', 'kv_w', 'kv_b', 'out_w', 'out_b', 'postnorm_w', 'mlp_w1', 'mlp_b1', 'mlp_w2', 'mlp_b2')}
    del _L3_xattn_all
    return {'x': x, 'ctx_2048': ctx_2048, 'mask_Bx1xSxS2_ff0': mask_Bx1xSxS2_ff0, 'mask_BxS2_ik0': mask_BxS2_ik0, 'L0_xattn_Wn': _L0_xattn_in['Wn'], 'L0_xattn_bn': _L0_xattn_in['bn'], 'L0_xattn_Wm': _L0_xattn_in['Wm'], 'L0_xattn_bm': _L0_xattn_in['bm'], 'L0_xattn_Wl': _L0_xattn_in['Wl'], 'L0_xattn_bl': _L0_xattn_in['bl'], 'L0_xattn_Wo': _L0_xattn_in['Wo'], 'L0_xattn_bo': _L0_xattn_in['bo'], 'L1_xattn_ln1_scale': _L1_xattn_in['ln1_scale'], 'L1_xattn_ln1_offset': _L1_xattn_in['ln1_offset'], 'L1_xattn_wq1': _L1_xattn_in['wq1'], 'L1_xattn_bq1': _L1_xattn_in['bq1'], 'L1_xattn_wk1': _L1_xattn_in['wk1'], 'L1_xattn_bk1': _L1_xattn_in['bk1'], 'L1_xattn_wv1': _L1_xattn_in['wv1'], 'L1_xattn_bv1': _L1_xattn_in['bv1'], 'L1_xattn_wo1': _L1_xattn_in['wo1'], 'L1_xattn_bo1': _L1_xattn_in['bo1'], 'L1_xattn_bias_k1': _L1_xattn_in['bias_k1'], 'L1_xattn_bias_v1': _L1_xattn_in['bias_v1'], 'L1_xattn_ln2_scale': _L1_xattn_in['ln2_scale'], 'L1_xattn_ln2_offset': _L1_xattn_in['ln2_offset'], 'L1_xattn_wq2': _L1_xattn_in['wq2'], 'L1_xattn_bq2': _L1_xattn_in['bq2'], 'L1_xattn_wk2': _L1_xattn_in['wk2'], 'L1_xattn_bk2': _L1_xattn_in['bk2'], 'L1_xattn_wv2': _L1_xattn_in['wv2'], 'L1_xattn_bv2': _L1_xattn_in['bv2'], 'L1_xattn_wo2': _L1_xattn_in['wo2'], 'L1_xattn_bo2': _L1_xattn_in['bo2'], 'L1_xattn_bias_k2': _L1_xattn_in['bias_k2'], 'L1_xattn_bias_v2': _L1_xattn_in['bias_v2'], 'L1_xattn_ln_mlp_scale': _L1_xattn_in['ln_mlp_scale'], 'L1_xattn_ln_mlp_offset': _L1_xattn_in['ln_mlp_offset'], 'L1_xattn_w_fc1': _L1_xattn_in['w_fc1'], 'L1_xattn_b_fc1': _L1_xattn_in['b_fc1'], 'L1_xattn_w_fc2': _L1_xattn_in['w_fc2'], 'L1_xattn_b_fc2': _L1_xattn_in['b_fc2'], 'L2_xattn_Wq': _L2_xattn_in['Wq'], 'L2_xattn_bq': _L2_xattn_in['bq'], 'L2_xattn_Wk': _L2_xattn_in['Wk'], 'L2_xattn_bk': _L2_xattn_in['bk'], 'L2_xattn_Wv': _L2_xattn_in['Wv'], 'L2_xattn_bv': _L2_xattn_in['bv'], 'L2_xattn_Wo': _L2_xattn_in['Wo'], 'L2_xattn_bo': _L2_xattn_in['bo'], 'L2_xattn_gamma': _L2_xattn_in['gamma'], 'L2_xattn_beta': _L2_xattn_in['beta'], 'L3_xattn_q_w': _L3_xattn_in['q_w'], 'L3_xattn_q_b': _L3_xattn_in['q_b'], 'L3_xattn_kv_w': _L3_xattn_in['kv_w'], 'L3_xattn_kv_b': _L3_xattn_in['kv_b'], 'L3_xattn_out_w': _L3_xattn_in['out_w'], 'L3_xattn_out_b': _L3_xattn_in['out_b'], 'L3_xattn_postnorm_w': _L3_xattn_in['postnorm_w'], 'L3_xattn_mlp_w1': _L3_xattn_in['mlp_w1'], 'L3_xattn_mlp_b1': _L3_xattn_in['mlp_b1'], 'L3_xattn_mlp_w2': _L3_xattn_in['mlp_w2'], 'L3_xattn_mlp_b2': _L3_xattn_in['mlp_b2']}

def reference(x, ctx_2048, mask_Bx1xSxS2_ff0, mask_BxS2_ik0, L0_xattn_Wn, L0_xattn_bn, L0_xattn_Wm, L0_xattn_bm, L0_xattn_Wl, L0_xattn_bl, L0_xattn_Wo, L0_xattn_bo, L1_xattn_ln1_scale, L1_xattn_ln1_offset, L1_xattn_wq1, L1_xattn_bq1, L1_xattn_wk1, L1_xattn_bk1, L1_xattn_wv1, L1_xattn_bv1, L1_xattn_wo1, L1_xattn_bo1, L1_xattn_bias_k1, L1_xattn_bias_v1, L1_xattn_ln2_scale, L1_xattn_ln2_offset, L1_xattn_wq2, L1_xattn_bq2, L1_xattn_wk2, L1_xattn_bk2, L1_xattn_wv2, L1_xattn_bv2, L1_xattn_wo2, L1_xattn_bo2, L1_xattn_bias_k2, L1_xattn_bias_v2, L1_xattn_ln_mlp_scale, L1_xattn_ln_mlp_offset, L1_xattn_w_fc1, L1_xattn_b_fc1, L1_xattn_w_fc2, L1_xattn_b_fc2, L2_xattn_Wq, L2_xattn_bq, L2_xattn_Wk, L2_xattn_bk, L2_xattn_Wv, L2_xattn_bv, L2_xattn_Wo, L2_xattn_bo, L2_xattn_gamma, L2_xattn_beta, L3_xattn_q_w, L3_xattn_q_b, L3_xattn_kv_w, L3_xattn_kv_b, L3_xattn_out_w, L3_xattn_out_b, L3_xattn_postnorm_w, L3_xattn_mlp_w1, L3_xattn_mlp_b1, L3_xattn_mlp_w2, L3_xattn_mlp_b2):
    import jax
    import jax.numpy as jnp

    def _L0_xattn_ref(x_c, x_s, Wn, bn, Wm, bm, Wl, bl, Wo, bo):
        import jax, jax.numpy as jnp
        import numpy as np
        EPS = 1e-05

        def _inorm(x):
            m = jnp.mean(x, axis=-1, keepdims=True)
            v = jnp.var(x, axis=-1, keepdims=True)
            return (x - m) * jax.lax.rsqrt(v + EPS)

        def _conv1x1(W, b, x):
            return jnp.einsum('oc,bct->bot', W, x) + b[None, :, None]
        Mn = _conv1x1(Wn, bn, _inorm(x_c))
        Mm = _conv1x1(Wm, bm, _inorm(x_s))
        A = jax.nn.softmax(jnp.einsum('bct,bcs->bts', Mn, Mm), axis=-1)
        Ml = _conv1x1(Wl, bl, x_s)
        Mo = jnp.einsum('bcs,bts->bct', Ml, A)
        return _conv1x1(Wo, bo, Mo) + x_c

    def _L1_xattn_ref(x, xf_1, xf_2, ln1_scale, ln1_offset, wq1, bq1, wk1, bk1, wv1, bv1, wo1, bo1, bias_k1, bias_v1, ln2_scale, ln2_offset, wq2, bq2, wk2, bk2, wv2, bv2, wo2, bo2, bias_k2, bias_v2, ln_mlp_scale, ln_mlp_offset, w_fc1, b_fc1, w_fc2, b_fc2):
        import jax, jax.numpy as jnp
        import numpy as np
        B, Q, S1, S2 = (4, 32, 256, 256)
        D, H, K, F = (256, 16, 128, 1024)
        LN_EPS = 1e-05

        def _layer_norm(x, scale, offset):
            mu = jnp.mean(x, axis=-1, keepdims=True)
            var = jnp.var(x, axis=-1, keepdims=True)
            return (x - mu) * jax.lax.rsqrt(var + LN_EPS) * scale + offset

        def _cross_attention(q_in, kv_in, wq, bq, wk, bk, wv, bv, wo, bo, bias_k, bias_v):
            b, q_len, _ = q_in.shape
            t = kv_in.shape[1]
            qh = (q_in @ wq + bq).reshape(b, q_len, H, K)
            kh = (kv_in @ wk + bk).reshape(b, t, H, K)
            vh = (kv_in @ wv + bv).reshape(b, t, H, K)
            kh = jnp.concatenate([kh, jnp.broadcast_to(bias_k, (b, 1, H, K))], axis=1)
            vh = jnp.concatenate([vh, jnp.broadcast_to(bias_v, (b, 1, H, K))], axis=1)
            scale = jnp.sqrt(jnp.asarray(K, q_in.dtype))
            logits = jnp.einsum('bqhk,bthk->bhqt', qh, kh) / scale
            weights = jax.nn.softmax(logits, axis=-1)
            ctx = jnp.einsum('bhqt,bthk->bqhk', weights, vh).reshape(b, q_len, H * K)
            return ctx @ wo + bo

        def _forward(x, xf_1, xf_2, ln1_scale, ln1_offset, wq1, bq1, wk1, bk1, wv1, bv1, wo1, bo1, bias_k1, bias_v1, ln2_scale, ln2_offset, wq2, bq2, wk2, bk2, wv2, bv2, wo2, bo2, bias_k2, bias_v2, ln_mlp_scale, ln_mlp_offset, w_fc1, b_fc1, w_fc2, b_fc2):
            res = x
            h = _layer_norm(x, ln1_scale, ln1_offset)
            x = res + _cross_attention(h, xf_1, wq1, bq1, wk1, bk1, wv1, bv1, wo1, bo1, bias_k1, bias_v1)
            res = x
            h = _layer_norm(x, ln2_scale, ln2_offset)
            x = res + _cross_attention(h, xf_2, wq2, bq2, wk2, bk2, wv2, bv2, wo2, bo2, bias_k2, bias_v2)
            h = _layer_norm(x, ln_mlp_scale, ln_mlp_offset)
            h = jax.nn.gelu(h @ w_fc1 + b_fc1, approximate=False) @ w_fc2 + b_fc2
            return x + h
        return _forward(x, xf_1, xf_2, ln1_scale, ln1_offset, wq1, bq1, wk1, bk1, wv1, bv1, wo1, bo1, bias_k1, bias_v1, ln2_scale, ln2_offset, wq2, bq2, wk2, bk2, wv2, bv2, wo2, bo2, bias_k2, bias_v2, ln_mlp_scale, ln_mlp_offset, w_fc1, b_fc1, w_fc2, b_fc2)

    def _L2_xattn_ref(hidden_state, encoder_hidden_state, encoder_attention_mask, Wq, bq, Wk, bk, Wv, bv, Wo, bo, gamma, beta):
        import jax, jax.numpy as jnp
        import numpy as np
        H = 256
        NH = 32
        KVH = 8
        HD = H // NH
        GROUPS = NH // KVH
        EPS = 1e-06
        B, L, S = (4, 128, 128)

        def _gqa_forward(hidden_state, encoder_hidden_state, encoder_attention_mask, Wq, bq, Wk, bk, Wv, bv, Wo, bo, gamma, beta):
            b, l, _ = hidden_state.shape
            s = encoder_hidden_state.shape[1]
            q = hidden_state @ Wq + bq
            k = encoder_hidden_state @ Wk + bk
            v = encoder_hidden_state @ Wv + bv
            q = q.reshape(b, l, KVH, GROUPS, HD).transpose(0, 2, 3, 1, 4)
            k = k.reshape(b, s, KVH, HD).transpose(0, 2, 1, 3)
            v = v.reshape(b, s, KVH, HD).transpose(0, 2, 1, 3)
            scale = 1.0 / jnp.sqrt(jnp.asarray(HD, q.dtype))
            scores = jnp.einsum('bkgld,bksd->bkgls', q, k) * scale
            scores = scores + encoder_attention_mask[:, :, None, :, :]
            attn = jax.nn.softmax(scores, axis=-1)
            out = jnp.einsum('bkgls,bksd->bkgld', attn, v)
            out = out.transpose(0, 3, 1, 2, 4).reshape(b, l, H)
            out = out @ Wo + bo
            x = out + hidden_state
            mu = jnp.mean(x, axis=-1, keepdims=True)
            var = jnp.var(x, axis=-1, keepdims=True)
            return (x - mu) * jax.lax.rsqrt(var + EPS) * gamma + beta
        return _gqa_forward(hidden_state, encoder_hidden_state, encoder_attention_mask, Wq, bq, Wk, bk, Wv, bv, Wo, bo, gamma, beta)

    def _L3_xattn_ref(x, latents, attention_mask, q_w, q_b, kv_w, kv_b, out_w, out_b, postnorm_w, mlp_w1, mlp_b1, mlp_w2, mlp_b2):
        import jax, jax.numpy as jnp
        import numpy as np
        B, P, K, H, NH = (4, 256, 32, 256, 16)
        DH = H // NH
        EPS = 1e-06

        def rmsnorm(x, w):
            var = jnp.mean(jnp.square(x), axis=-1, keepdims=True)
            return x * jax.lax.rsqrt(var + EPS) * w
        b, p, _ = x.shape
        k_len = latents.shape[1]
        residual = latents
        h = jnp.concatenate([x, latents], axis=1)
        q = (latents @ q_w + q_b).reshape(b, k_len, NH, DH)
        kv = (h @ kv_w + kv_b).reshape(b, p + k_len, NH, DH, 2)
        kmat, v = (kv[..., 0], kv[..., 1])
        attn = jnp.einsum('bkhd,bnhd->bhkn', q, kmat) / DH
        full_mask = jnp.concatenate([attention_mask.astype(bool), jnp.ones((b, k_len), bool)], axis=-1)
        attn = jnp.where(full_mask[:, None, None, :], attn, -jnp.inf)
        attn = jax.nn.softmax(attn.astype(jnp.float32), axis=-1).astype(q.dtype)
        attn_out = jnp.einsum('bhkn,bnhd->bkhd', attn, v).reshape(b, k_len, H)
        attn_out = attn_out @ out_w + out_b + residual
        out = rmsnorm(attn_out, postnorm_w)
        out = jax.nn.gelu(out @ mlp_w1 + mlp_b1) @ mlp_w2 + mlp_b2
        return out + residual
    x = _L0_xattn_ref(x, ctx_2048, L0_xattn_Wn, L0_xattn_bn, L0_xattn_Wm, L0_xattn_bm, L0_xattn_Wl, L0_xattn_bl, L0_xattn_Wo, L0_xattn_bo)
    x = _L1_xattn_ref(x, ctx_2048, ctx_2048, L1_xattn_ln1_scale, L1_xattn_ln1_offset, L1_xattn_wq1, L1_xattn_bq1, L1_xattn_wk1, L1_xattn_bk1, L1_xattn_wv1, L1_xattn_bv1, L1_xattn_wo1, L1_xattn_bo1, L1_xattn_bias_k1, L1_xattn_bias_v1, L1_xattn_ln2_scale, L1_xattn_ln2_offset, L1_xattn_wq2, L1_xattn_bq2, L1_xattn_wk2, L1_xattn_bk2, L1_xattn_wv2, L1_xattn_bv2, L1_xattn_wo2, L1_xattn_bo2, L1_xattn_bias_k2, L1_xattn_bias_v2, L1_xattn_ln_mlp_scale, L1_xattn_ln_mlp_offset, L1_xattn_w_fc1, L1_xattn_b_fc1, L1_xattn_w_fc2, L1_xattn_b_fc2)
    x = _L2_xattn_ref(x, ctx_2048, mask_Bx1xSxS2_ff0, L2_xattn_Wq, L2_xattn_bq, L2_xattn_Wk, L2_xattn_bk, L2_xattn_Wv, L2_xattn_bv, L2_xattn_Wo, L2_xattn_bo, L2_xattn_gamma, L2_xattn_beta)
    x = _L3_xattn_ref(ctx_2048, x, mask_BxS2_ik0, L3_xattn_q_w, L3_xattn_q_b, L3_xattn_kv_w, L3_xattn_kv_b, L3_xattn_out_w, L3_xattn_out_b, L3_xattn_postnorm_w, L3_xattn_mlp_w1, L3_xattn_mlp_b1, L3_xattn_mlp_w2, L3_xattn_mlp_b2)
    return x

_drawn_inputs = setup_inputs


def setup_inputs(seed=0):
    import zlib

    import numpy as np

    out = dict(_drawn_inputs(seed))
    spreads = {'L1_xattn_ln1_scale': (1.0, 0.6),
     'L1_xattn_ln1_offset': (0.0, 0.8),
     'L1_xattn_bq1': (0.0, 0.8),
     'L1_xattn_bk1': (0.0, 2.0),
     'L1_xattn_bv1': (0.0, 0.1),
     'L1_xattn_bo1': (0.0, 0.1),
     'L1_xattn_ln2_scale': (1.0, 0.6),
     'L1_xattn_ln2_offset': (0.0, 0.8),
     'L1_xattn_bq2': (0.0, 0.8),
     'L1_xattn_bk2': (0.0, 2.0),
     'L1_xattn_bv2': (0.0, 0.1),
     'L1_xattn_bo2': (0.0, 0.1),
     'L1_xattn_ln_mlp_scale': (1.0, 0.6),
     'L1_xattn_ln_mlp_offset': (0.0, 0.8),
     'L1_xattn_b_fc1': (0.0, 0.32),
     'L1_xattn_b_fc2': (0.0, 0.1),
     'L2_xattn_bq': (0.0, 2.0),
     'L2_xattn_bk': (0.0, 2.0),
     'L2_xattn_bv': (0.0, 0.343),
     'L2_xattn_bo': (0.0, 0.1),
     'L2_xattn_gamma': (1.0, 0.2),
     'L2_xattn_beta': (0.0, 0.1),
     'L3_xattn_q_b': (0.0, 0.8),
     'L3_xattn_kv_b': (0.0, 0.8),
     'L3_xattn_out_b': (0.0, 2.0),
     'L3_xattn_postnorm_w': (1.0, 0.6),
     'L3_xattn_mlp_b1': (0.0, 0.1),
     'L3_xattn_mlp_b2': (0.0, 0.1)}
    factors = {'L0_xattn_bm': 64.0,
     'L0_xattn_bl': 8.0,
     'L0_xattn_bo': 8.0,
     'L1_xattn_wq1': 8.0,
     'L1_xattn_wk1': 8.0,
     'L1_xattn_bias_k1': 64.0,
     'L1_xattn_bias_v1': 64.0,
     'L1_xattn_wq2': 8.0,
     'L1_xattn_wk2': 8.0,
     'L1_xattn_bias_k2': 64.0,
     'L1_xattn_bias_v2': 64.0,
     'L2_xattn_Wq': 8.0,
     'L2_xattn_Wk': 8.0,
     'L3_xattn_q_w': 8.0,
     'L3_xattn_kv_w': 8.0,
     'L3_xattn_out_w': 8.0}
    for name, (base, spread) in spreads.items():
        noise = np.random.default_rng([zlib.crc32(name.encode()), seed]).standard_normal(out[name].shape)
        drawn = base * np.exp(spread * noise) if base else spread * noise
        out[name] = jnp.asarray(drawn.astype(out[name].dtype))
    for name, factor in factors.items():
        out[name] = (out[name] * factor).astype(out[name].dtype)
    return out
```

```python
import concourse.bass as bass
from concourse import mybir
from contextlib import ExitStack
import numpy as np

F32 = mybir.dt.float32
F32R = mybir.dt.float32r
I32 = mybir.dt.int32
ALU = mybir.AluOpType
ACT = mybir.ActivationFunctionType
X_AXIS = mybir.AxisListType.X

B, T, D = 32, 64, 256
P = 128
PAIRS = B * T // P
KT = D // P
TOK = B * T
BLK = 512
NBLK = TOK // BLK
PPB = BLK // P
H1, K1 = 16, 128
HG = 4
NG = H1 // HG
FF = 1024
FT = FF // P
BANK, PSUM_BANKS = 512, 8
ds = bass.ds


class Mem:

    def __init__(self, nc, tag, psum=None):
        self.nc, self.tag, self.psum, self.stack, self.banks, self.sems = nc, tag, psum, ExitStack(), 0, []

    def __enter__(self):
        self.stack.__enter__()
        return self

    def __exit__(self, *a):
        numbers = sorted(s.num for s in self.sems)
        while numbers:
            run = [n for i, n in enumerate(numbers) if n == numbers[0] + i]
            self.nc.sync.sem_clear(range(run[0], run[-1] + 1))
            numbers = numbers[len(run):]
        return self.stack.__exit__(*a)

    def sb(self, name, shape, dt=F32):
        return self.stack.enter_context(self.nc.sbuf_tensor(f"{self.tag}_{name}", shape, dt))

    def ps(self, name, shape=(P, 512)):
        size, at = int(np.prod(shape[1:])), self.banks * BANK
        self.banks += -(-size // BANK)
        assert self.banks <= PSUM_BANKS, name
        view = self.psum[0:shape[0], at:at + size]
        dims = " ".join(f"d{n}" for n in range(len(shape) - 1))
        sizes = {f"d{n}": s for n, s in enumerate(shape[1:])}
        return view.rearrange(f"p ({dims}) -> p {dims}", **sizes) if len(shape) > 2 else view

    def sem(self, name):
        self.sems.append(self.stack.enter_context(self.nc.semaphore(f"{self.tag}_{name}")))
        return self.sems[-1]


def split_products(lhs_hi, lhs_lo, rhs_hi, rhs_lo):
    return [(lhs_hi, rhs_hi), (lhs_hi, rhs_lo), (lhs_lo, rhs_hi)]


def skewed(eng, n, body):
    body(0, True, False)
    with eng.Fori(1, n) as j:
        body(j, True, True)
    body(n, False, True)


def phase_setup(nc, A, G):
    with Mem(nc, "su", G.psum) as m:
        ctx_psum = [m.ps(f"ctx_psum{i}", (P, KT, P)) for i in range(2)]
        x_in, ctx_in = m.sem("x_in"), m.sem("ctx_in")
        ident_zero, ident_made = m.sem("ident_zero"), m.sem("ident_made")
        transposed, hi_done, lo_done = m.sem("transposed"), m.sem("hi_done"), m.sem("lo_done")
        x_dram = A["x"].rearrange("(p b) t d -> (b t) p d", b=2)
        c_dram = A["ctx_2048"].rearrange("(p b) t d -> (b t) p d", b=2)
        with nc.Block() as block:
            @block.sync
            def _(sp):
                for q in range(4):
                    sp.dma_start(G.ctx_tok[:, 4 * q:4 * q + 4, :], c_dram[:, 4 * q:4 * q + 4, :]).then_inc(ctx_in, 16)
                for q in range(4):
                    sp.dma_start(G.x_res[:, 4 * q:4 * q + 4, :], x_dram[:, 4 * q:4 * q + 4, :]).then_inc(x_in, 16)
                sp.wait_ge(x_in, 64)

            @block.gpsimd
            def _(pool):
                pool.memset(G.ident[:, :], 0.0).then_inc(ident_zero, 1)
                pool.wait_ge(ident_zero, 1)
                pool.affine_select(out=G.ident[:, :], in_=G.ident[:, :], compare_op=ALU.not_equal, fill=1.0,
                                   base=0, pattern=[[-1, P]], channel_multiplier=1).then_inc(ident_made, 1)
                pool.memset(G.minus_half[:, :], -0.5)

            @block.tensor
            def _(pe):
                pe.wait_ge(ident_made, 1)
                pe.wait_ge(ctx_in, 64)
                for p in range(PAIRS):
                    if p >= 2:
                        pe.wait_ge(lo_done, p - 1)
                    for k in range(KT):
                        mm = pe.transpose(ctx_psum[p % 2][:, k, :], G.ctx_tok[:, p, k * P:(k + 1) * P], G.ident[:, :])
                    mm.then_inc(transposed, 1)

            @block.scalar
            def _(act):
                for p in range(PAIRS):
                    act.wait_ge(transposed, p + 1)
                    act.activation(G.ctx_hi[:, :, p * P:(p + 1) * P], ctx_psum[p % 2][:, :, :], ACT.Copy).then_inc(hi_done, 1)

            @block.vector
            def _(dve):
                for p in range(PAIRS):
                    dve.wait_ge(hi_done, p + 1)
                    dve.tensor_tensor(G.ctx_lo[:, :, p * P:(p + 1) * P], ctx_psum[p % 2][:, :, :],
                                      G.ctx_hi[:, :, p * P:(p + 1) * P].bitcast(F32), ALU.subtract).then_inc(lo_done, 1)


def phase_layer0(nc, A, G):
    with Mem(nc, "l0", G.psum) as m:
        w_nat = m.sb("w_nat", [P, 4, P])
        w_t = m.sb("w_t", [P, 4, P])
        bias = m.sb("bias", [P, 4])
        obias = m.sb("obias", [P, 1])
        stats = m.sb("stats", [P, 2 * PAIRS, 6])
        mv = m.sb("mv", [P, 2 * PAIRS, 2])
        rstd = m.sb("rstd", [P, 2 * PAIRS])
        xn = m.sb("xn", [P, 2 * PAIRS, D])
        c_fix = [m.sb(f"c_fix{i}", [P, D]) for i in range(2)]
        mix = m.sb("mix", [P, 2, D])
        prob = [m.sb(f"prob{i}", [P, 2, 2, D]) for i in range(2)]
        prob_t = m.sb("prob_t", [P, 2, 2, D])
        y_sb = [m.sb(f"y{i}", [P, 2, P]) for i in range(2)]
        nmax = m.sb("nmax", [P, 2, 2])
        ssum = m.sb("ssum", [P, 2, 4])
        rsum = m.sb("rsum", [P, 4])
        mix_ps = m.ps("mix_ps", (P, 2, D))
        y_ps = m.ps("y_ps", (P, 2, P))
        s_ps = [m.ps(f"s_ps{i}", (P, 2, D)) for i in range(2)]
        t_ps = [m.ps(f"t_ps{i}", (P, 2, D)) for i in range(2)]
        o_ps = m.ps("o_ps", (P, D))
        w_zero, w_in, w_turned, w_kept = m.sem("w_zero"), m.sem("w_in"), m.sem("w_turned"), m.sem("w_kept")
        g_psum, w_ready = m.sem("g_psum"), m.sem("w_ready")
        stats_done, mv_done, eps_added, rstd_done, xn_done = (m.sem(n) for n in
            ("stats_done", "mv_done", "eps_added", "rstd_done", "xn_done"))
        c_fixed, mix_psum, mix_done, s_psum = (m.sem(n) for n in ("c_fixed", "mix_psum", "mix_done", "s_psum"))
        max_done, exp_done, rsum_done, prob_done = (m.sem(n) for n in ("max_done", "exp_done", "rsum_done", "prob_done"))
        t_psum, t_act, t_dve = (m.sem(n) for n in ("t_psum", "t_act", "t_dve"))
        y_psum, y_done, o_psum, x_done = (m.sem(n) for n in ("y_psum", "y_done", "o_psum", "x_done"))
        STEPS = PAIRS // 2
        with nc.Block() as block:
            @block.sync
            def _(sp):
                sp.wait_ge(w_zero, 1)
                for i, n in enumerate(("Wn", "Wm", "Wl", "Wo")):
                    for b in range(2):
                        sp.dma_start(w_nat[64 * b:64 * b + 64, i, 64 * b:64 * b + 64], A[f"L0_xattn_{n}"]).then_inc(w_in, 16)
                for i, n in enumerate(("bn", "bm", "bl", "bo")):
                    for b in range(2):
                        sp.dma_start(bias[64 * b:64 * b + 64, i:i + 1],
                                     A[f"L0_xattn_{n}"].rearrange("(p o) -> p o", o=1)).then_inc(w_in, 16)

            @block.gpsimd
            def _(pool):
                pool.wait_ge(mv_done, 2 * PAIRS)
                pool.tensor_scalar(rstd[:, :], mv[:, :, 1], 1e-5, None, ALU.add).then_inc(eps_added, 1)
                pool.wait_ge(eps_added, 1)
                pool.tensor_tensor(rstd[:, :], rstd[:, :], G.minus_half[:, 0:2 * PAIRS], ALU.pow).then_inc(rstd_done, 1)

                def body(j, front, back):
                    for q in range(2):
                        if front:
                            u = 2 * j + q
                            if back:
                                pool.wait_ge(y_psum, u - 1)
                            pool.tensor_copy(c_fix[q][:, :], G.ctx_tok[:, ds(u, 1), :]).then_inc(c_fixed, 1)
                body(0, True, False)
                with pool.Fori(1, STEPS) as j:
                    body(j, True, True)

            @block.tensor
            def _(pe):
                pe.wait_ge(w_in, 16 * 16)
                for i, src in enumerate((0, 1, 3)):
                    mm = pe.transpose(mix_ps[:, i // 2, (i % 2) * P:(i % 2) * P + P], w_nat[:, src, :], G.ident[:, :])
                mm.then_inc(w_turned, 1)
                pe.wait_ge(w_kept, 1)
                pe.matmul(y_ps[:, 0, :], w_nat[:, 2, :], w_t[:, 3, :], start=True, stop=True)
                pe.matmul(y_ps[:, 1, 0:1], w_t[:, 3, :], bias[:, 2:3], start=True, stop=True).then_inc(g_psum, 1)
                pe.wait_ge(w_ready, 2)
                pe.wait_ge(xn_done, 2 * PAIRS)

                def body(j, front, back):
                    for q in range(2):
                        u = 2 * j + q
                        if back:
                            r = u - 2
                            pe.wait_ge(prob_done, r + 1)
                            pe.wait_ge(t_act, r + 1)
                            pe.wait_ge(t_dve, r + 1)
                            for b in range(2):
                                for sh in range(2):
                                    for th in range(2):
                                        mm = pe.transpose(t_ps[b][:, sh, th * P:th * P + P],
                                                          prob[q][:, b, th, sh * P:sh * P + P], G.ident[:, :])
                                mm.then_inc(t_psum, 1)
                        if front:
                            if back or q:
                                pe.wait_ge(mix_done, u)
                            for i in range(2):
                                mm = pe.matmul(mix_ps[:, i, :], w_t[:, i, :], xn[:, ds(i * PAIRS + u, 1), :],
                                               start=True, stop=True)
                            mm.then_inc(mix_psum, 1)
                            pe.wait_ge(mix_done, u + 1)
                            if back or q:
                                pe.wait_ge(exp_done, 4 * u)
                            for b in range(2):
                                for th in range(2):
                                    mm = pe.matmul(s_ps[b][:, th, :], mix[64 * b:64 * b + 64, 0, th * P:th * P + P],
                                                   mix[64 * b:64 * b + 64, 1, :], start=True, stop=True)
                                mm.then_inc(s_psum, 1)
                        if back:
                            pe.wait_ge(t_act, r + 2)
                            pe.wait_ge(t_dve, r + 2)
                            pe.wait_ge(x_done, r + 1)
                            for b in range(2):
                                for sh in range(2):
                                    mm = pe.matmul(o_ps[64 * b:64 * b + 64, :], y_sb[q][:, sh, 64 * b:64 * b + 64],
                                                   prob_t[:, b, sh, :], start=(sh == 0), stop=(sh == 1))
                            mm.then_inc(o_psum, 1)
                        if front:
                            pe.wait_ge(c_fixed, u + 1)
                            if back or q:
                                pe.wait_ge(y_done, u)
                            for sh in range(2):
                                mm = pe.matmul(y_ps[:, sh, :], c_fix[q][:, sh * P:sh * P + P], w_t[:, 2, :],
                                               start=True, stop=True)
                            mm.then_inc(y_psum, 1)
                skewed(pe, STEPS, body)

            @block.scalar
            def _(act):
                def body(j, front, back):
                    for q in range(2):
                        u = 2 * j + q
                        if back:
                            r = u - 2
                            act.wait_ge(t_psum, 2 * r + 1)
                            act.activation(prob_t[:, 0, :, :], t_ps[0][:, :, :], ACT.Copy).then_inc(t_act, 1)
                        if front:
                            act.wait_ge(mix_psum, u + 1)
                            act.activation(mix[:, 0, :], mix_ps[:, 0, :], ACT.Identity, bias=bias[:, 0:1])
                            act.activation(mix[:, 1, :], mix_ps[:, 1, :], ACT.Identity, bias=bias[:, 1:2]).then_inc(mix_done, 1)
                            for b in range(2):
                                act.wait_ge(max_done, 2 * u + b + 1)
                                for th in range(2):
                                    act.activation(prob[q][:, b, th, :], s_ps[b][:, th, :], ACT.Exp,
                                                   bias=nmax[:, b, th:th + 1],
                                                   accum_out=ssum[:, q, 2 * b + th:2 * b + th + 1]).then_inc(exp_done, 1)
                act.wait_ge(w_in, 16 * 16)
                skewed(act, STEPS, body)

            @block.vector
            def _(dve):
                dve.memset(w_nat[:, :, :], 0.0).then_inc(w_zero, 1)
                dve.memset(nmax[:, :, :], 0.0).then_inc(t_act, 1)
                dve.memset(rsum[:, :], 0.0).then_inc(t_dve, 1)
                dve.memset(obias[:, :], 0.0).then_inc(x_done, 1)
                dve.wait_ge(w_turned, 1)
                dve.tensor_copy(w_t[:, 0:2, :], mix_ps[:, 0, :])
                dve.tensor_copy(w_t[:, 3, :], mix_ps[:, 1, 0:P]).then_inc(w_kept, 1)
                dve.wait_ge(g_psum, 1)
                dve.tensor_copy(w_t[:, 2, :], y_ps[:, 0, :]).then_inc(w_ready, 1)
                dve.wait_ge(x_done, 1)
                dve.tensor_tensor(obias[:, :], y_ps[:, 1, 0:1], bias[:, 3:4], ALU.add).then_inc(w_ready, 1)
                for i in range(2 * PAIRS):
                    src = G.x_res if i < PAIRS else G.ctx_tok
                    dve.bn_stats(stats[:, i, :], src[:, i % PAIRS, :]).then_inc(stats_done, 1)
                for i in range(2 * PAIRS):
                    dve.wait_ge(stats_done, i + 1)
                    dve.bn_aggr(mv[:, i, :], stats[:, i, :]).then_inc(mv_done, 1)
                dve.wait_ge(rstd_done, 1)
                dve.wait_ge(mv_done, 2 * PAIRS)
                for i in range(2 * PAIRS):
                    src = G.x_res if i < PAIRS else G.ctx_tok
                    dve.tensor_scalar(xn[:, i, :], src[:, i % PAIRS, :], mv[:, i, 0:1], rstd[:, i:i + 1],
                                      ALU.subtract, ALU.mult).then_inc(xn_done, 1)
                dve.wait_ge(w_ready, 2)
                dve.wait_ge(t_dve, 1)

                def body(j, front, back):
                    for q in range(2):
                        u = 2 * j + q
                        if back:
                            r = u - 2
                            dve.wait_ge(t_psum, 2 * r + 2)
                            dve.tensor_copy(prob_t[:, 1, :, :], t_ps[1][:, :, :]).then_inc(t_dve, 1)
                        if front:
                            if back or q:
                                dve.wait_ge(exp_done, 4 * u)
                            for b in range(2):
                                dve.wait_ge(s_psum, 2 * u + b + 1)
                                dve.tensor_reduce(nmax[:, b, :], s_ps[b][:, :, :], X_AXIS, ALU.max, negate=True).then_inc(max_done, 1)
                        if back:
                            dve.wait_ge(o_psum, r + 1)
                            dve.scalar_tensor_tensor(G.x_res[:, ds(r, 1), :], o_ps[:, :], obias[:, 0:1],
                                                     G.x_res[:, ds(r, 1), :], ALU.add, ALU.add).then_inc(x_done, 1)
                        if front:
                            dve.wait_ge(exp_done, 4 * u + 4)
                            if back or q:
                                dve.wait_ge(prob_done, u)
                            dve.reciprocal(rsum[:, :], ssum[:, q, :]).then_inc(rsum_done, 1)
                            dve.wait_ge(rsum_done, u + 1)
                            for i in range(4):
                                sc = dve.tensor_scalar(prob[q][:, i // 2, i % 2, :], prob[q][:, i // 2, i % 2, :],
                                                       rsum[:, i:i + 1], None, ALU.mult)
                            sc.then_inc(prob_done, 1)
                            dve.wait_ge(y_psum, u + 1)
                            dve.tensor_copy(y_sb[q][:, :, :], y_ps[:, :, :]).then_inc(y_done, 1)
                skewed(dve, STEPS, body)


def phase_features(nc, G, tag, src, dst_hi, dst_lo, kind, eps=0.0, scale=None, offset=None,
                   update=False):
    with Mem(nc, tag, G.psum) as m:
        affine = m.sb("affine", [P, 2, KT])
        row_in = m.sb("row_in", [2 * KT, P])
        stats = m.sb("stats", [P, PAIRS, 6])
        mv = m.sb("mv", [P, PAIRS, 2])
        rstd = m.sb("rstd", [P, PAIRS])
        normed = m.sb("normed", [P, PAIRS, D])
        raw = [m.sb(f"raw{i}", [P, BLK]) for i in range(2)]
        feat_ps = [m.ps(f"feat_ps{i}", (P, BLK)) for i in range(3)]
        affine_in, stats_done, mv_done, eps_added, rstd_done, normed_done = (m.sem(n) for n in
            ("affine_in", "stats_done", "mv_done", "eps_added", "rstd_done", "normed_done"))
        feat_psum, raw_done, hi_done, lo_done = (m.sem(n) for n in ("feat_psum", "raw_done", "hi_done", "lo_done"))
        affine_ps = m.ps("affine_ps", (P, 2 * KT))
        affine_psum, affine_done, rows_zero = m.sem("affine_psum"), m.sem("affine_done"), m.sem("rows_zero")
        if update:
            spread_affine = m.sb("spread_affine", [P, 2, D])
            spread_in, scaled = m.sem("spread_in"), m.sem("scaled")
        normalized = src if kind == "plain" else normed
        with nc.Block() as block:
            @block.sync
            def _(sp):
                if scale is not None:
                    sp.wait_ge(rows_zero, 1)
                    sp.dma_start(row_in[0:KT, :], scale.rearrange("(k p) -> k p", p=P)).then_inc(affine_in, 16)
                    if offset is not None:
                        sp.dma_start(row_in[KT:2 * KT, :], offset.rearrange("(k p) -> k p", p=P)).then_inc(affine_in, 16)
                if update:
                    for n, v in enumerate((scale, offset)):
                        sp.dma_start(spread_affine[:, n, :], v.rearrange("(o n) -> o n", o=1).partition_broadcast(P)).then_inc(spread_in, 16)

            @block.gpsimd
            def _(pool):
                if kind != "plain":
                    pool.wait_ge(mv_done, PAIRS)
                    if kind == "rms":
                        pool.tensor_tensor(rstd[:, :], mv[:, :, 0], mv[:, :, 0], ALU.mult).then_inc(eps_added, 1)
                        pool.wait_ge(eps_added, 1)
                        pool.tensor_tensor(rstd[:, :], rstd[:, :], mv[:, :, 1], ALU.add).then_inc(eps_added, 1)
                        pool.wait_ge(eps_added, 2)
                        pool.tensor_scalar(rstd[:, :], rstd[:, :], eps, None, ALU.add).then_inc(eps_added, 1)
                    else:
                        pool.tensor_scalar(rstd[:, :], mv[:, :, 1], eps, None, ALU.add).then_inc(eps_added, 3)
                    pool.wait_ge(eps_added, 3)
                    pool.tensor_tensor(rstd[:, :], rstd[:, :], G.minus_half[:, 0:PAIRS], ALU.pow).then_inc(rstd_done, 1)

            @block.tensor
            def _(pe):
                if scale is not None:
                    pe.wait_ge(affine_in, 16 if offset is None else 32)
                    pe.transpose(affine_ps[:, :], row_in[:, :], G.ident[0:2 * KT, 0:2 * KT]).then_inc(affine_psum, 1)
                for n in range(NBLK * KT):
                    b, k = n // KT, n % KT
                    if kind != "plain":
                        pe.wait_ge(normed_done, PPB * (b + 1))
                    if n >= 3:
                        pe.wait_ge(raw_done, n - 2)
                    for i in range(PPB):
                        mm = pe.transpose(feat_ps[n % 3][:, i * P:(i + 1) * P],
                                          normalized[:, PPB * b + i, k * P:(k + 1) * P], G.ident[:, :])
                    mm.then_inc(feat_psum, 1)

            @block.scalar
            def _(act):
                if scale is not None:
                    act.wait_ge(affine_psum, 1)
                    act.activation(affine[:, :, :].rearrange("p a k -> p (a k)"), affine_ps[:, :], ACT.Copy).then_inc(affine_done, 1)
                    act.wait_ge(affine_done, 1)
                for n in range(NBLK * KT):
                    k = n % KT
                    act.wait_ge(feat_psum, n + 1)
                    if n >= 2:
                        act.wait_ge(lo_done, n - 1)
                    if scale is not None:
                        act.activation(raw[n % 2][:, :], feat_ps[n % 3][:, :], ACT.Identity,
                                       bias=affine[:, 1, k:k + 1], scale=affine[:, 0, k:k + 1]).then_inc(raw_done, 1)
                    else:
                        act.activation(raw[n % 2][:, :], feat_ps[n % 3][:, :], ACT.Copy).then_inc(raw_done, 1)

            @block.vector
            def _(dve):
                dve.memset(row_in[:, :], 0.0).then_inc(rows_zero, 1)
                if kind != "plain":
                    for i in range(PAIRS):
                        dve.bn_stats(stats[:, i, :], src[:, i, :]).then_inc(stats_done, 1)
                    for i in range(PAIRS):
                        dve.wait_ge(stats_done, i + 1)
                        dve.bn_aggr(mv[:, i, :], stats[:, i, :]).then_inc(mv_done, 1)
                    dve.wait_ge(rstd_done, 1)
                    dve.wait_ge(mv_done, PAIRS)
                    for i in range(PAIRS):
                        if kind == "ln":
                            dve.tensor_scalar(normed[:, i, :], src[:, i, :], mv[:, i, 0:1], rstd[:, i:i + 1],
                                              ALU.subtract, ALU.mult).then_inc(normed_done, 1)
                        else:
                            dve.tensor_scalar(normed[:, i, :], src[:, i, :], rstd[:, i:i + 1], None,
                                              ALU.mult).then_inc(normed_done, 1)
                for n in range(NBLK * KT):
                    b, k = n // KT, n % KT
                    hi, lo = dst_hi[:, k, b * BLK:(b + 1) * BLK], dst_lo[:, k, b * BLK:(b + 1) * BLK]
                    dve.wait_ge(raw_done, n + 1)
                    dve.tensor_copy(hi, raw[n % 2][:, :]).then_inc(hi_done, 1)
                    dve.wait_ge(hi_done, n + 1)
                    dve.tensor_tensor(lo, raw[n % 2][:, :], hi.bitcast(F32), ALU.subtract).then_inc(lo_done, 1)
                if update:
                    dve.wait_ge(spread_in, 32)
                    dve.wait_ge(normed_done, PAIRS)
                    for p in range(PAIRS):
                        dve.tensor_tensor(src[:, p, :], normed[:, p, :], spread_affine[:, 0, :], ALU.mult).then_inc(scaled, 1)
                    for p in range(PAIRS):
                        dve.wait_ge(scaled, p + 1)
                        dve.tensor_tensor(src[:, p, :], src[:, p, :], spread_affine[:, 1, :], ALU.add)



CONST_ROWS = ("bq", "bk", "bias_k", "bias_v", "bv")


def phase_layer1_constants(nc, A, G):
    with Mem(nc, "l1c", G.psum) as m:
        rows = m.sb("rows", [5 * H1, 2, P])
        wo = [m.sb(f"wo{i}", [P, H1, D]) for i in range(2)]
        lhs = m.sb("lhs", [P, 2, H1, H1 + 1])
        unit = m.sb("unit", [1, H1 + 1])
        bo = m.sb("bo", [1, 2, D])
        cols_ps = m.ps("cols_ps", (P, 2, 5 * H1))
        bvo_ps = m.ps("bvo_ps", (H1 + 1, 2, D))
        rows_in, wo_in, cleared, unit_zero = (m.sem(n) for n in ("rows_in", "wo_in", "cleared", "unit_zero"))
        cols_psum, cols_done, hi_done, lhs_done, bvo_psum = (m.sem(n) for n in
            ("cols_psum", "cols_done", "hi_done", "lhs_done", "bvo_psum"))
        with nc.Block() as block:
            @block.sync
            def _(sp):
                for i in range(2):
                    for n, name in enumerate(CONST_ROWS):
                        src = A[f"L1_xattn_{name}{i + 1}"]
                        src = src.rearrange("a b h d -> (a b h) d") if len(src.shape) == 4 else src.rearrange("(h d) -> h d", d=K1)
                        sp.dma_start(rows[n * H1:(n + 1) * H1, i, :], src).then_inc(rows_in, 16)
                    sp.dma_start(bo[:, i, :], A[f"L1_xattn_bo{i + 1}"].rearrange("(o n) -> o n", o=1)).then_inc(rows_in, 16)
                for i in range(2):
                    sp.dma_start(wo[i][:, :, :], A[f"L1_xattn_wo{i + 1}"].rearrange("(h d) n -> d h n", d=K1)).then_inc(wo_in, 16)
                    sp.wait_ge(wo_in, 16 * (i + 1))

            @block.gpsimd
            def _(pool):
                pool.memset(lhs[:, :, :, :], 0.0).then_inc(cleared, 1)
                pool.memset(unit[:, :], 0.0).then_inc(unit_zero, 1)
                pool.wait_ge(unit_zero, 1)
                pool.memset(unit[:, H1:H1 + 1], 1.0).then_inc(cleared, 1)

            @block.tensor
            def _(pe):
                pe.wait_ge(rows_in, 16 * 12)
                for i in range(2):
                    mm = pe.transpose(cols_ps[:, i, :], rows[:, i, :], G.ident[0:5 * H1, 0:5 * H1])
                mm.then_inc(cols_psum, 1)
                pe.wait_ge(lhs_done, 2)
                pe.wait_ge(cleared, 2)
                for i in range(2):
                    pe.wait_ge(wo_in, 16 * (i + 1))
                    for h in range(H1):
                        pe.matmul(bvo_ps[:, i, :], lhs[:, i, h, :], wo[i][:, h, :], start=(h == 0), stop=False)
                    mm = pe.matmul(bvo_ps[:, i, :], unit[:, :], bo[:, i, :], start=False, stop=True)
                mm.then_inc(bvo_psum, 1)

            @block.vector
            def _(dve):
                dve.wait_ge(cols_psum, 1)
                dve.tensor_copy(G.cols[:, :, :], cols_ps[:, :, :]).then_inc(cols_done, 1)
                dve.wait_ge(cols_done, 1)
                bias_k, bias_v, bv = (G.cols[:, :, n * H1:(n + 1) * H1] for n in (2, 3, 4))
                dve.tensor_copy(G.bias_k_hi[:, :, :], bias_k).then_inc(hi_done, 1)
                dve.wait_ge(hi_done, 1)
                dve.tensor_tensor(G.bias_k_lo[:, :, :], bias_k, G.bias_k_hi[:, :, :].bitcast(F32), ALU.subtract)
                dve.wait_ge(cleared, 2)
                diagonal = lhs[:, :, :, :].rearrange("p i h c -> p i (h c)")[:, :, 0:H1 * (H1 + 1):H1 + 2]
                dve.tensor_tensor(diagonal, bias_v, bv, ALU.subtract).then_inc(lhs_done, 1)
                dve.tensor_copy(lhs[:, :, :, H1], bv).then_inc(lhs_done, 1)
                dve.wait_ge(bvo_psum, 1)
                dve.tensor_copy(G.bvo[:, :, :], bvo_ps[:, :, :])


def phase_layer1_attention(nc, A, G, i):
    tag = f"att{i}"
    NI = NG * NBLK
    KP = T + 1
    name = lambda n: A[f"L1_xattn_{n}{i}"]
    q_scale = float(K1) ** -0.5
    with Mem(nc, tag, G.psum) as m:
        q_hi, q_lo = (m.sb(n, [P, HG, BLK], F32R) for n in ("q_hi", "q_lo"))
        k_hi, k_lo = (m.sb(n, [P, HG, 2 * PPB, KP], F32R) for n in ("k_hi", "k_lo"))
        v_hi, v_lo = (m.sb(n, [P, PPB, HG * K1], F32R) for n in ("v_hi", "v_lo"))
        pt_hi, pt_lo = (m.sb(n, [P, BLK], F32R) for n in ("pt_hi", "pt_lo"))
        ot_hi, ot_lo = (m.sb(n, [P, HG, BLK], F32R) for n in ("ot_hi", "ot_lo"))
        wqk_hi, wqk_lo = (m.sb(n, [P, HG, 2, KT, K1], F32R) for n in ("wqk_hi", "wqk_lo"))
        wv_hi, wv_lo = (m.sb(n, [P, KT, HG * K1], F32R) for n in ("wv_hi", "wv_lo"))
        wo_hi, wo_lo = (m.sb(n, [P, HG, D], F32R) for n in ("wo_hi", "wo_lo"))
        cf_hi, cf_lo = (m.sb(n, [P, KT, BLK], F32R) for n in ("cf_hi", "cf_lo"))
        stage_qk = m.sb("stage_qk", [P, 2, 2, KT, K1])
        stage_vo = m.sb("stage_vo", [P, KT * HG * K1])
        soft = m.sb("soft", [P, PPB, KP])
        prob = m.sb("prob", [P, PPB, P])
        rmax = m.sb("rmax", [P, PPB])
        rsum = m.sb("rsum", [P, PPB])
        rinv = m.sb("rinv", [P, PPB])
        q_ps, k_ps = m.ps("q_ps"), m.ps("k_ps")
        s_ps = m.ps("s_ps", (P, PPB, 2 * P))
        t_ps, c_ps = m.ps("t_ps"), m.ps("c_ps")
        o_ps = [m.ps(f"o_ps{n}", (P, 2, D)) for n in range(2)]
        v_ps = [q_ps, k_ps]
        qk_in = [m.sem(f"qk_in{n}") for n in range(2)]
        vo_in, w_hi, wqk_ready, wv_ready, wo_ready, cf_ready, kb_ready = (m.sem(n) for n in
            ("vo_in", "w_hi", "wqk_ready", "wv_ready", "wo_ready", "cf_ready", "kb_ready"))
        q_psum, k_psum, v_psum, s_psum, t_psum, c_psum, o_psum = (m.sem(n) for n in
            ("q_psum", "k_psum", "v_psum", "s_psum", "t_psum", "c_psum", "o_psum"))
        q_high, k_high, v_high, pt_high, ot_high = (m.sem(n) for n in ("q_high", "k_high", "v_high", "pt_high", "ot_high"))
        q_ready, k_ready, v_ready, pt_ready, ot_ready, x_added = (m.sem(n) for n in
            ("q_ready", "k_ready", "v_ready", "pt_ready", "ot_ready", "x_added"))
        max_done, shifted, exp_done, sum_done, inv_done, prob_ready = (m.sem(n) for n in
            ("max_done", "shifted", "exp_done", "sum_done", "inv_done", "prob_ready"))

        qk_dram = [name(w).rearrange("(k p) n -> p k n", p=P) for w in ("wq", "wk")]
        v_dram = name("wv").rearrange("(k p) n -> p k n", p=P)
        o_dram = name("wo").rearrange("(h d) n -> d h n", d=K1)

        def score_item(j, h, front, back):
            if h < HG - 1:
                return (j - 1, h + 1) if back else None
            return (j, 0) if front else None

        with nc.Block() as block:
            @block.sync
            def _(sp):
                def group(g, first):
                    for h in range(HG):
                        if not (first and h < 2):
                            sp.wait_ge(wqk_ready, HG * g + h - 1)
                        for w in range(2):
                            sp.dma_start(stage_qk[:, h % 2, w, :, :],
                                         qk_dram[w][:, :, ds((HG * g + h) * K1, K1)]).then_inc(qk_in[h % 2], 16)
                    if not first:
                        sp.wait_ge(wo_ready, g)
                    sp.dma_start(stage_vo[:, :].rearrange("p (k n) -> p k n", k=KT),
                                 v_dram[:, :, ds(HG * K1 * g, HG * K1)]).then_inc(vo_in, 16)
                    sp.wait_ge(wv_ready, g + 1)
                    sp.dma_start(stage_vo[:, :].rearrange("p (h n) -> p h n", h=HG),
                                 o_dram[:, ds(HG * g, HG), :]).then_inc(vo_in, 16)
                group(0, True)
                with sp.Fori(1, NG) as g:
                    group(g, False)

            @block.gpsimd
            def _(pool):
                SPLITS = HG + 2

                def split(count, hi, lo, raw, ready):
                    pool.tensor_copy(hi, raw).then_inc(w_hi, 1)
                    pool.wait_ge(w_hi, count)
                    pool.tensor_tensor(lo, raw, hi.bitcast(F32), ALU.subtract).then_inc(ready, 1)

                def context_block(g, b, first):
                    if not (first and b == 0):
                        pool.wait_ge(v_psum, PPB * (NBLK * g + b))
                    pool.tensor_copy(cf_hi[:, :, :], G.ctx_hi[:, :, b * BLK:(b + 1) * BLK].bitcast(F32))
                    pool.tensor_copy(cf_lo[:, :, :], G.ctx_lo[:, :, b * BLK:(b + 1) * BLK].bitcast(F32)).then_inc(cf_ready, 1)

                def key_bias(g, b, first):
                    for h in range(HG):
                        pool.wait_ge(k_psum, HG * (NBLK * g + b) + h + 1)
                        for dst, src in ((k_hi, G.bias_k_hi), (k_lo, G.bias_k_lo)):
                            kb = pool.tensor_copy(dst[:, h, :, T:KP], src[:, i - 1, ds(HG * g + h, 1)].bitcast(F32)
                                                  .unsqueeze(1).to_broadcast([P, 2 * PPB, 1]))
                        kb.then_inc(kb_ready, 1)

                def group(g, first):
                    for h in range(HG):
                        pool.wait_ge(qk_in[h % 2], 32 * (HG // 2 * g + h // 2 + 1))
                        if not first:
                            pool.wait_ge(k_psum, HG * NBLK * g - HG + h + 1)
                        split(SPLITS * g + h + 1, wqk_hi[:, h, :, :, :], wqk_lo[:, h, :, :, :],
                              stage_qk[:, h % 2, :, :, :], wqk_ready)
                    pool.wait_ge(vo_in, 32 * g + 16)
                    if not first:
                        pool.wait_ge(v_psum, PPB * NBLK * g)
                    split(SPLITS * g + HG + 1, wv_hi[:, :, :], wv_lo[:, :, :],
                          stage_vo[:, :].rearrange("p (k n) -> p k n", k=KT), wv_ready)
                    context_block(g, 0, first)
                    key_bias(g, 0, first)
                    context_block(g, 1, first)
                    pool.wait_ge(vo_in, 32 * g + 32)
                    if not first:
                        pool.wait_ge(o_psum, 2 * NBLK * g)
                    split(SPLITS * g + HG + 2, wo_hi[:, :, :], wo_lo[:, :, :],
                          stage_vo[:, :].rearrange("p (h n) -> p h n", h=HG), wo_ready)
                    key_bias(g, 1, first)
                    for b in (2, 3):
                        context_block(g, b, first)
                        key_bias(g, b, first)
                for g in range(NG):
                    group(g, g == 0)

            @block.tensor
            def _(pe):
                def body(j, front, back):
                    if front:
                        g, off = j // NBLK, (j % NBLK) * BLK
                    for h in range(HG):
                        item = score_item(j, h, front, back)
                        if item:
                            js, hs = item
                            n = HG * js + hs
                            pe.wait_ge(q_ready, n + 1)
                            pe.wait_ge(k_ready, n + 1)
                            pe.wait_ge(kb_ready, n + 1)
                            if back:
                                pe.wait_ge(shifted, 2 * n)
                            for p in range(PPB):
                                cols = slice(p * P, (p + 1) * P)
                                prods = split_products(q_hi[:, hs, cols], q_lo[:, hs, cols],
                                                       k_hi[:, hs, 2 * p:2 * p + 2, :], k_lo[:, hs, 2 * p:2 * p + 2, :])
                                for t, (a, b) in enumerate(prods):
                                    mm = pe.matmul(s_ps[:, p, 0:2 * KP], a, b, start=(t == 0), stop=(t == 2))
                            mm.then_inc(s_psum, 1)
                        if back:
                            n = HG * (j - 1) + h
                            pe.wait_ge(prob_ready, 3 * n + 3)
                            pe.wait_ge(pt_ready, n + 1)
                            for p in range(PPB):
                                mm = pe.transpose(t_ps[:, p * P:(p + 1) * P], prob[:, p, :], G.ident[:, :])
                            mm.then_inc(t_psum, 1)
                        if front:
                            n = HG * j + h
                            pe.wait_ge(wqk_ready, HG * g + h + 1)
                            if back or h:
                                pe.wait_ge(q_ready, n)
                                pe.wait_ge(k_ready, n)
                            if back and h == 0:
                                pe.wait_ge(v_ready, PPB * j)
                            for w, dst, x_hi, x_lo, done in ((0, q_ps, G.feat_hi, G.feat_lo, q_psum),
                                                             (1, k_ps, G.ctx_hi, G.ctx_lo, k_psum)):
                                for k in range(KT):
                                    prods = split_products(wqk_hi[:, h, w, k, :], wqk_lo[:, h, w, k, :],
                                                           x_hi[:, k, ds(off, BLK)], x_lo[:, k, ds(off, BLK)])
                                    for t, (a, b) in enumerate(prods):
                                        mm = pe.matmul(dst[:, :], a, b, start=(k == 0 and t == 0),
                                                       stop=(k == KT - 1 and t == 2))
                                mm.then_inc(done, 1)
                        if back:
                            n = HG * (j - 1) + h
                            pe.wait_ge(pt_ready, n + 2)
                            pe.wait_ge(ot_ready, n + 1)
                            pe.wait_ge(v_ready, PPB * j)
                            for p in range(PPB):
                                cols, head = slice(p * P, (p + 1) * P), slice(h * K1, (h + 1) * K1)
                                for t, (a, b) in enumerate(split_products(v_hi[:, p, head], v_lo[:, p, head],
                                                                          pt_hi[:, cols], pt_lo[:, cols])):
                                    mm = pe.matmul(c_ps[:, cols], a, b, start=(t == 0), stop=(t == 2))
                            mm.then_inc(c_psum, 1)
                    if front:
                        pe.wait_ge(wv_ready, g + 1)
                        pe.wait_ge(cf_ready, j + 1)
                        pe.wait_ge(q_ready, HG * j + HG)
                        pe.wait_ge(k_ready, HG * j + HG)
                        for p in range(PPB):
                            if p >= 2:
                                pe.wait_ge(v_ready, PPB * j + p - 1)
                            for k in range(KT):
                                cols = slice(p * P, (p + 1) * P)
                                for t, (a, b) in enumerate(split_products(cf_hi[:, k, cols], cf_lo[:, k, cols],
                                                                          wv_hi[:, k, :], wv_lo[:, k, :])):
                                    mm = pe.matmul(v_ps[p % 2][:, :], a, b, start=(k == 0 and t == 0),
                                                   stop=(k == KT - 1 and t == 2))
                            mm.then_inc(v_psum, 1)
                    if back:
                        pe.wait_ge(ot_ready, HG * j + 1)
                        pe.wait_ge(wo_ready, (j - 1) // NBLK + 1)
                        pe.wait_ge(x_added, 2 * (j - 1) + 1)
                        for p in range(PPB):
                            cols = slice(p * P, (p + 1) * P)
                            for h in range(HG):
                                for t, (a, b) in enumerate(split_products(ot_hi[:, h, cols], ot_lo[:, h, cols],
                                                                          wo_hi[:, h, :], wo_lo[:, h, :])):
                                    mm = pe.matmul(o_ps[p // 2][:, p % 2, :], a, b, start=(h == 0 and t == 0),
                                                   stop=(h == HG - 1 and t == 2))
                            if p % 2:
                                mm.then_inc(o_psum, 1)
                skewed(pe, NI, body)

            @block.scalar
            def _(act):
                def body(j, front, back):
                    for h in range(HG):
                        if back:
                            n = HG * (j - 1) + h
                            act.wait_ge(t_psum, n + 1)
                            act.activation(pt_hi[:, :], t_ps[:, :], ACT.Copy).then_inc(pt_high, 1)
                        item = score_item(j, h, front, back)
                        if item:
                            n = HG * item[0] + item[1]
                            act.wait_ge(shifted, 2 * n + 2)
                            act.activation(soft[:, :, :], soft[:, :, :], ACT.Exp, scale=q_scale).then_inc(exp_done, 1)
                        if front:
                            n, head = HG * j + h, HG * (j // NBLK) + h
                            act.wait_ge(q_psum, n + 1)
                            act.activation(q_hi[:, h, :], q_ps[:, :], ACT.Identity,
                                           bias=G.cols[:, i - 1, ds(head, 1)]).then_inc(q_high, 1)
                            act.wait_ge(k_psum, n + 1)
                            act.activation(k_hi[:, h, :, 0:T], k_ps[:, :].rearrange("p (b t) -> p b t", t=T), ACT.Identity,
                                           bias=G.cols[:, i - 1, ds(H1 + head, 1)]).then_inc(k_high, 1)
                        if back:
                            act.wait_ge(c_psum, HG * (j - 1) + h + 1)
                            act.activation(ot_hi[:, h, :], c_ps[:, :], ACT.Copy).then_inc(ot_high, 1)
                    if front:
                        for p in range(PPB):
                            act.wait_ge(v_psum, PPB * j + p + 1)
                            act.activation(v_hi[:, p, :], v_ps[p % 2][:, :], ACT.Copy).then_inc(v_high, 1)
                skewed(act, NI, body)

            @block.vector
            def _(dve):
                dve.memset(prob[:, :, :], 0.0).then_inc(pt_ready, 1)
                dve.memset(G.bias_prob[:, :, H1:H1 + 1], 1.0).then_inc(ot_ready, 1)
                dve.memset(rmax[:, :], 0.0).then_inc(x_added, 1)
                dve.wait_ge(pt_ready, 1)
                dve.wait_ge(x_added, 1)
                halves = [slice(0, T), slice(T, 2 * T)]

                def low(dst, psum, high):
                    return dve.tensor_tensor(dst, psum, high.bitcast(F32), ALU.subtract)

                def body(j, front, back):
                    for h in range(HG):
                        item = score_item(j, h, front, back)
                        if item:
                            js, hs = item
                            n = HG * js + hs
                            dve.wait_ge(s_psum, n + 1)
                            for u, half in enumerate(halves):
                                dve.tensor_reduce(rmax[half, :], s_ps[half, :, u * KP:(u + 1) * KP], X_AXIS, ALU.max).then_inc(max_done, 1)
                            if back:
                                dve.wait_ge(prob_ready, 3 * n)
                            for u, half in enumerate(halves):
                                dve.wait_ge(max_done, 2 * n + u + 1)
                                dve.tensor_tensor(soft[half, :, :], s_ps[half, :, u * KP:(u + 1) * KP],
                                                  rmax[half, :].unsqueeze(2).to_broadcast([T, PPB, KP]), ALU.subtract).then_inc(shifted, 1)
                        if back:
                            m_ = HG * (j - 1) + h
                            dve.wait_ge(pt_high, m_ + 1)
                            low(pt_lo[:, :], t_ps[:, :], pt_hi[:, :]).then_inc(pt_ready, 1)
                        if item:
                            dve.wait_ge(exp_done, n + 1)
                            dve.tensor_reduce(rsum[:, :], soft[:, :, :], X_AXIS, ALU.add).then_inc(sum_done, 1)
                            dve.wait_ge(sum_done, n + 1)
                            dve.reciprocal(rinv[:, :], rsum[:, :]).then_inc(inv_done, 1)
                            dve.wait_ge(inv_done, n + 1)
                            if back:
                                dve.wait_ge(t_psum, n)
                            for half in halves:
                                dve.tensor_tensor(prob[half, :, half], soft[half, :, 0:T],
                                                  rinv[half, :].unsqueeze(2).to_broadcast([T, PPB, T]), ALU.mult).then_inc(prob_ready, 1)
                            dve.tensor_tensor(G.bias_prob[:, ds(PPB * (js % NBLK), PPB), ds(HG * (js // NBLK) + hs, 1)],
                                              soft[:, :, T:KP], rinv[:, :].unsqueeze(2), ALU.mult).then_inc(prob_ready, 1)
                        if front:
                            m_, head = HG * j + h, HG * (j // NBLK) + h
                            dve.wait_ge(q_high, m_ + 1)
                            dve.scalar_tensor_tensor(q_lo[:, h, :], q_ps[:, :], G.cols[:, i - 1, ds(head, 1)],
                                                     q_hi[:, h, :].bitcast(F32), ALU.add, ALU.subtract).then_inc(q_ready, 1)
                            dve.wait_ge(k_high, m_ + 1)
                            dve.scalar_tensor_tensor(k_lo[:, h, :, 0:T], k_ps[:, :].rearrange("p (b t) -> p b t", t=T),
                                                     G.cols[:, i - 1, ds(H1 + head, 1)],
                                                     k_hi[:, h, :, 0:T].bitcast(F32), ALU.add, ALU.subtract).then_inc(k_ready, 1)
                        if back:
                            dve.wait_ge(ot_high, HG * (j - 1) + h + 1)
                            low(ot_lo[:, h, :], c_ps[:, :], ot_hi[:, h, :]).then_inc(ot_ready, 1)
                    if front:
                        for p in range(PPB):
                            dve.wait_ge(v_high, PPB * j + p + 1)
                            low(v_lo[:, p, :], v_ps[p % 2][:, :], v_hi[:, p, :]).then_inc(v_ready, 1)
                    if back:
                        for p in range(2):
                            dve.wait_ge(o_psum, 2 * (j - 1) + p + 1)
                            x = G.x_res[:, ds(PPB * ((j - 1) % NBLK) + 2 * p, 2), :]
                            dve.tensor_tensor(x, o_ps[p][:, :, :], x, ALU.add).then_inc(x_added, 1)
                skewed(dve, NI, body)


def phase_bias_token(nc, G, i):
    with Mem(nc, f"bt{i}", G.psum) as m:
        bp_t = [m.sb(f"bp_t{n}", [H1 + 1, P]) for n in range(2)]
        t_ps = [m.ps(f"t_ps{n}", (H1 + 1, P)) for n in range(2)]
        o_ps = [m.ps(f"o_ps{n}", (P, D)) for n in range(2)]
        t_psum, t_done, o_psum, x_done = (m.sem(n) for n in ("t_psum", "t_done", "o_psum", "x_done"))
        with nc.Block() as block:
            @block.tensor
            def _(pe):
                for p in range(PAIRS + 1):
                    if p < PAIRS:
                        if p >= 2:
                            pe.wait_ge(t_done, p - 1)
                        pe.transpose(t_ps[p % 2][:, :], G.bias_prob[:, p, :], G.ident[:, :]).then_inc(t_psum, 1)
                    if p:
                        pe.wait_ge(t_done, p)
                        if p >= 3:
                            pe.wait_ge(x_done, p - 2)
                        pe.matmul(o_ps[(p - 1) % 2][:, :], bp_t[(p - 1) % 2][:, :], G.bvo[:, i - 1, :], start=True, stop=True).then_inc(o_psum, 1)

            @block.scalar
            def _(act):
                for p in range(PAIRS):
                    act.wait_ge(t_psum, p + 1)
                    if p >= 2:
                        act.wait_ge(o_psum, p - 1)
                    act.activation(bp_t[p % 2][:, :], t_ps[p % 2][:, :], ACT.Copy).then_inc(t_done, 1)

            @block.vector
            def _(dve):
                for p in range(PAIRS):
                    dve.wait_ge(o_psum, p + 1)
                    dve.tensor_tensor(G.x_res[:, p, :], o_ps[p % 2][:, :], G.x_res[:, p, :], ALU.add).then_inc(x_done, 1)


def phase_mlp(nc, A, G, tag, w1_dram, b1_dram, w2_dram, b2_dram, func):
    LAG, RING = 2, 4
    with Mem(nc, tag, G.psum) as m:
        w1_raw, w2_raw = m.sb("w1_raw", [P, KT, FF]), m.sb("w2_raw", [P, FT, D])
        w1_hi, w1_lo = (m.sb(n, [P, KT, FF], F32R) for n in ("w1_hi", "w1_lo"))
        w2_hi, w2_lo = (m.sb(n, [P, FT, D], F32R) for n in ("w2_hi", "w2_lo"))
        b1_rows, b1 = m.sb("b1_rows", [FT, P]), m.sb("b1", [P, FT])
        b2 = m.sb("b2", [P, D])
        act_raw = [m.sb(f"act_raw{n}", [P, BLK]) for n in range(2)]
        act_hi = [m.sb(f"act_hi{n}", [P, BLK], F32R) for n in range(RING)]
        act_lo = [m.sb(f"act_lo{n}", [P, BLK], F32R) for n in range(RING)]
        hid_ps = [m.ps(f"hid_ps{n}", (P, BLK)) for n in range(RING)]
        out_ps = [m.ps(f"out_ps{n}", (P, D)) for n in range(PPB)]
        w1_in, w2_in, b1_in, b2_in = (m.sem(n) for n in ("w1_in", "w2_in", "b1_in", "b2_in"))
        b1_psum, b1_done, b2_added, w_hi, w_ready = (m.sem(n) for n in ("b1_psum", "b1_done", "b2_added", "w_hi", "w_ready"))
        hid_psum, raw_done, hi_done, act_ready, out_psum, x_done = (m.sem(n) for n in
            ("hid_psum", "raw_done", "hi_done", "act_ready", "out_psum", "x_done"))
        with nc.Block() as block:
            @block.sync
            def _(sp):
                sp.dma_start(b1_rows[:, :], b1_dram.rearrange("(f p) -> f p", p=P)).then_inc(b1_in, 16)
                sp.dma_start(w1_raw[:, :, :], w1_dram.rearrange("(k p) n -> p k n", p=P)).then_inc(w1_in, 16)
                sp.dma_start(w2_raw[:, :, :], w2_dram.rearrange("(f p) n -> p f n", p=P)).then_inc(w2_in, 16)
                sp.dma_start(b2[:, :], b2_dram.rearrange("(o n) -> o n", o=1).partition_broadcast(P)).then_inc(b2_in, 16)

            @block.gpsimd
            def _(pool):
                pool.wait_ge(b2_in, 16)
                for p in range(PAIRS):
                    pool.tensor_tensor(G.x_res[:, p, :], G.x_res[:, p, :], b2[:, :], ALU.add).then_inc(b2_added, 1)

            @block.tensor
            def _(pe):
                pe.wait_ge(b1_in, 16)
                pe.transpose(hid_ps[0][:, 0:FT], b1_rows[:, :], G.ident[0:FT, 0:FT]).then_inc(b1_psum, 1)
                pe.wait_ge(b1_done, 1)

                def up(j, f, first):
                    n = FT * j + f
                    if first:
                        pe.wait_ge(w_ready, min(f, 1) + 1)
                    if not first or f >= RING:
                        pe.wait_ge(raw_done, n - RING + 1)
                    for k in range(KT):
                        cols = slice(f * P, (f + 1) * P)
                        for t, (a, b) in enumerate(split_products(w1_hi[:, k, cols], w1_lo[:, k, cols],
                                                                  G.feat_hi[:, k, ds(j * BLK, BLK)],
                                                                  G.feat_lo[:, k, ds(j * BLK, BLK)])):
                            mm = pe.matmul(hid_ps[f % RING][:, :], a, b, start=(k == 0 and t == 0),
                                           stop=(k == KT - 1 and t == 2))
                    mm.then_inc(hid_psum, 1)

                def down(j, f, first):
                    pe.wait_ge(act_ready, FT * j + f + 1)
                    for p in range(PPB):
                        if f == 0 and not first:
                            pe.wait_ge(x_done, PPB * (j - 1) + p + 1)
                        cols = slice(p * P, (p + 1) * P)
                        for t, (a, b) in enumerate(split_products(act_hi[f % RING][:, cols], act_lo[f % RING][:, cols],
                                                                  w2_hi[:, f, :], w2_lo[:, f, :])):
                            mm = pe.matmul(out_ps[p][:, :], a, b, start=(f == 0 and t == 0), stop=(f == FT - 1 and t == 2))
                        if f == FT - 1:
                            mm.then_inc(out_psum, 1)

                def block_of_tokens(j, first):
                    for f in range(FT):
                        up(j, f, first)
                        if f >= LAG:
                            down(j, f - LAG, first)
                    for f in range(FT - LAG, FT):
                        down(j, f, first)
                block_of_tokens(0, True)
                with pe.Fori(1, NBLK) as j:
                    block_of_tokens(j, False)

            @block.scalar
            def _(act):
                act.wait_ge(b1_psum, 1)
                act.activation(b1[:, :], hid_ps[0][:, 0:FT], ACT.Copy).then_inc(b1_done, 1)
                act.wait_ge(b1_done, 1)

                def block_of_tokens(j, first):
                    for f in range(FT):
                        n = FT * j + f
                        act.wait_ge(hid_psum, n + 1)
                        if not first or f >= 2:
                            act.wait_ge(act_ready, n - 1)
                        act.activation(act_raw[f % 2][:, :], hid_ps[f % RING][:, :], func, bias=b1[:, f:f + 1]).then_inc(raw_done, 1)
                block_of_tokens(0, True)
                with act.Fori(1, NBLK) as j:
                    block_of_tokens(j, False)

            @block.vector
            def _(dve):
                for n, (got, raw, hi, lo) in enumerate(((w1_in, w1_raw, w1_hi, w1_lo), (w2_in, w2_raw, w2_hi, w2_lo))):
                    dve.wait_ge(got, 16)
                    dve.tensor_copy(hi[:, :, :], raw[:, :, :]).then_inc(w_hi, 1)
                    dve.wait_ge(w_hi, n + 1)
                    dve.tensor_tensor(lo[:, :, :], raw[:, :, :], hi[:, :, :].bitcast(F32), ALU.subtract).then_inc(w_ready, 1)

                def block_of_tokens(j, first):
                    for f in range(FT):
                        n = FT * j + f
                        dve.wait_ge(raw_done, n + 1)
                        dve.tensor_copy(act_hi[f % RING][:, :], act_raw[f % 2][:, :]).then_inc(hi_done, 1)
                        dve.wait_ge(hi_done, n + 1)
                        dve.tensor_tensor(act_lo[f % RING][:, :], act_raw[f % 2][:, :], act_hi[f % RING][:, :].bitcast(F32),
                                          ALU.subtract).then_inc(act_ready, 1)
                    if first:
                        dve.wait_ge(b2_added, PAIRS)
                    for p in range(PPB):
                        dve.wait_ge(out_psum, PPB * j + p + 1)
                        x = G.x_res[:, ds(PPB * j + p, 1), :]
                        dve.tensor_tensor(x, out_ps[p][:, :], x, ALU.add).then_inc(x_done, 1)
                block_of_tokens(0, True)
                with dve.Fori(1, NBLK) as j:
                    block_of_tokens(j, False)


UNITS = 4


def wait(eng, sem, value):
    if not (isinstance(value, int) and value <= 0):
        eng.wait_ge(sem, value)


def pair_steps(j, front, back):
    for half in range(2):
        prep = 2 * j + half if front else None
        unit_pair = (2 * j - 1 if back else None) if half == 0 else (2 * j if front else None)
        for i in range(UNITS):
            if i < UNITS - 1:
                scores = (unit_pair, i + 1) if unit_pair is not None else None
            else:
                scores = (prep, 0) if prep is not None else None
            yield half, i, prep, unit_pair, scores


def phase_narrow_attention(nc, A, G, layer, dst):
    two = layer == 2
    GR, NK = (8, 64) if two else (4, 128)
    HD = 8 if two else 16
    score_scale = float(HD) ** -0.5 if two else 1.0 / HD
    eps_mask = -1e30
    VR = 64 if two else P
    with Mem(nc, f"l{layer}", G.psum) as m:
        wq_raw = m.sb("wq_raw", [P, KT, D])
        kv_cols = 64 if two else D
        wkv_raw = m.sb("wkv_raw", [P, KT, 2, kv_cols] if two else [P, KT, 2 * D])
        wq_hi, wq_lo = (m.sb(n, [P, KT, D], F32R) for n in ("wq_hi", "wq_lo"))
        KC = P if two else D
        wk_f = m.sb("wk_f", [P, KT, KC])
        wk_hi, wk_lo = (m.sb(n, [P, KT, KC], F32R) for n in ("wk_hi", "wk_lo"))
        wv = m.sb("wv", [P, KT, kv_cols])
        wo = m.sb("wo", [64, 4, D] if two else [P, KT, D])
        rows = m.sb("rows", [8, P])
        cols = m.sb("cols", [P, 8])
        o_bias = m.sb("o_bias", [P, D])
        mask = m.sb("mask", [P, B, NK])
        mask_int = None if two else m.sb("mask_int", [P, B * T], I32)
        spread = m.sb("spread", [P, 8])
        q_bd = [m.sb(f"q_bd{n}", [P, 2, 2, P] if two else [P, 2, 2, 8 * T]) for n in range(2)]
        k_bd = [m.sb(f"k_bd{n}", [P, 8, P] if two else [P, 2, 2 * P]) for n in range(2)]
        v_bd = [m.sb(f"v_bd{n}", [P, 2, 4, 64] if two else [P, 2, H1, P]) for n in range(2)]
        vx = m.sb("vx", [P, KT, 2, 2, T])
        soft = [m.sb(f"soft{n}", [P, GR, NK]) for n in range(2)]
        prob = m.sb("prob", [P, GR, NK])
        pt = m.sb("pt", [P, 4, P])
        ot = m.sb("ot", [64, 4, P] if two else [P, 2, P])
        rmax, rsum, rinv = (m.sb(n, [P, GR]) for n in ("rmax", "rsum", "rinv"))
        s_ps = [m.ps(f"s_ps{n}") for n in range(2)]
        t_ps, c_ps, o_ps = m.ps("t_ps"), m.ps("c_ps", (P, P)), m.ps("o_ps", (P, D))
        q_ps = m.ps("q_ps", (P, 2, P))
        k_ps = m.ps("k_ps", (P, P) if two else (P, 2, 2, P))
        v_ps = m.ps("v_ps", (P, 2, kv_cols))
        w_in, row_in, mask_in, spread_made, zeroed = (m.sem(n) for n in ("w_in", "row_in", "mask_in", "spread_made", "zeroed"))
        w_hi, w_ready, cols_psum, cols_done, mask_done, o_bias_added = (m.sem(n) for n in
            ("w_hi", "w_ready", "cols_psum", "cols_done", "mask_done", "o_bias_added"))
        vx_ready, q_psum, k_psum, v_psum, q_done, k_done, v_done = (m.sem(n) for n in
            ("vx_ready", "q_psum", "k_psum", "v_psum", "q_done", "k_done", "v_done"))
        s_psum, masked, max_done, shifted, exp_done, sum_done, inv_done, prob_ready = (m.sem(n) for n in
            ("s_psum", "masked", "max_done", "shifted", "exp_done", "sum_done", "inv_done", "prob_ready"))
        t_psum, pt_done, c_psum, ot_done, o_psum, x_done = (m.sem(n) for n in
            ("t_psum", "pt_done", "c_psum", "ot_done", "o_psum", "x_done"))
        STEPS = PAIRS // 2
        if two:
            name = lambda n: A[f"L2_xattn_{n}"]
            w_loads = [(wq_raw[:, :, :], name("Wq").rearrange("(k p) n -> p k n", p=P)),
                       (wkv_raw[:, :, 0, :], name("Wk").rearrange("(k p) n -> p k n", p=P)),
                       (wkv_raw[:, :, 1, :], name("Wv").rearrange("(k p) n -> p k n", p=P))] + \
                      [(wo[8 * v:8 * v + 8, :, :], name("Wo")[32 * v:32 * v + 32, :].rearrange("(g d) n -> d g n", d=8)) for v in range(8)]
            q_bias = name("bq").rearrange("(v c g d) -> c g v d", v=8, c=2, g=2)
            row_loads = [(rows[c:c + 1, 64 * g:64 * g + 64].rearrange("o (v d) -> o v d", d=8), q_bias[c:c + 1, g]) for c in range(2) for g in range(2)] + \
                        [(rows[r:r + 1, 64 * g:64 * g + 64], name(n).rearrange("(o n) -> o n", o=1)) for r, n in ((2, "bk"), (4, "bv")) for g in range(2)]
            o_bias_dram = name("bo")
            mask_dram = A["mask_Bx1xSxS2_ff0"].rearrange("b o q t -> q (b o) t")
            mask_loads = [(mask[64 * g:64 * g + 64, :, :], mask_dram) for g in range(2)]
        else:
            name = lambda n: A[f"L3_xattn_{n}"]
            w_loads = [(wq_raw[:, :, :], name("q_w").rearrange("(k p) n -> p k n", p=P)),
                       (wkv_raw[:, :, :], name("kv_w").rearrange("(k p) n -> p k n", p=P)),
                       (wo[:, :, :], name("out_w").rearrange("(k p) n -> p k n", p=P))]
            kv_bias = name("kv_b").rearrange("(c p w) -> w c p", c=2, w=2)
            row_loads = [(rows[0:2, :], name("q_b").rearrange("(c p) -> c p", p=P)),
                         (rows[2:4, :], kv_bias[0]), (rows[4:6, :], kv_bias[1])]
            o_bias_dram = name("out_b")
            mask_loads = [(mask_int[:, :], A["mask_BxS2_ik0"].rearrange("(o b) t -> o (b t)", o=1).partition_broadcast(P))]

        with nc.Block() as block:
            @block.sync
            def _(sp):
                sp.wait_ge(zeroed, 3)
                with nc.allow_non_contiguous_dma(reason="biases of interleaved keys and values: 512 words"):
                    for dst_, src in row_loads:
                        sp.dma_start(dst_, src).then_inc(row_in, 16)
                for dst_, src in w_loads:
                    sp.dma_start(dst_, src).then_inc(w_in, 16)
                sp.dma_start(o_bias[:, :], o_bias_dram.rearrange("(o n) -> o n", o=1).partition_broadcast(P)).then_inc(mask_in, 16)
                for dst_, src in mask_loads:
                    sp.dma_start(dst_, src).then_inc(mask_in, 16)

            @block.gpsimd
            def _(pool):
                pool.memset(spread[:, :], 1.0).then_inc(spread_made, 1)
                n = 1
                for base, width in ((0, 8 * HD), (64, 64))[:2 if two else 1]:
                    for cm, b0, pat in ((1, -base, -HD), (-1, base + HD - 1, HD)):
                        pool.wait_ge(spread_made, n)
                        rows_ = slice(base, base + (64 if two else P))
                        pool.affine_select(out=spread[rows_, :], in_=spread[rows_, :], compare_op=ALU.is_ge, fill=0.0,
                                           base=b0 + cm * base, pattern=[[pat, 8]], channel_multiplier=cm).then_inc(spread_made, 1)
                        n += 1
                pool.wait_ge(spread_made, n)

                def normalize(pair, i):
                    n = UNITS * pair + i
                    pool.wait_ge(inv_done, n + 1)
                    wait(pool, t_psum, n)
                    pool.tensor_tensor(prob[:, :, :], soft[i % 2][:, :, :],
                                       rinv[:, :].unsqueeze(2).to_broadcast([P, GR, NK]), ALU.mult).then_inc(prob_ready, 1)

                def body(j, front, back):
                    for half, i, prep, unit_pair, scores in pair_steps(j, front, back):
                        if i == 0 and prep is not None:
                            wait(pool, v_psum, prep)
                            for s in range(2):
                                hi, lo = (G.ctx_hi, G.ctx_lo) if two or s == 0 else (G.feat_hi, G.feat_lo)
                                for k in range(KT):
                                    vs = pool.tensor_tensor(vx[:, k, :, s, :],
                                                            hi[:, k, ds(prep * P, P)].bitcast(F32).rearrange("p (b t) -> p b t", b=2),
                                                            lo[:, k, ds(prep * P, P)].bitcast(F32).rearrange("p (b t) -> p b t", b=2), ALU.add)
                            vs.then_inc(vx_ready, 1)
                        if scores:
                            normalize(*scores)
                skewed(pool, STEPS, body)

            @block.tensor
            def _(pe):
                n_rows = len(row_loads)
                pe.wait_ge(row_in, 16 * n_rows)
                pe.transpose(c_ps[:, 0:8], rows[:, :], G.ident[0:8, 0:8]).then_inc(cols_psum, 1)
                pe.wait_ge(cols_done, 1)
                pe.wait_ge(w_ready, 3)
                pe.wait_ge(w_in, 16 * len(w_loads))

                def accumulate(out, products):
                    for n, (a, b) in enumerate(products):
                        mm = pe.matmul(out, a, b, start=(n == 0), stop=(n == len(products) - 1))
                    return mm

                def body(j, front, back):
                    for half, i, prep, unit_pair, scores in pair_steps(j, front, back):
                        if scores:
                            pair, c_i = scores
                            n, par = UNITS * pair + c_i, half if i < UNITS - 1 else 1 - half
                            par = 1 - half if i < UNITS - 1 else half
                            b, c = c_i // 2, c_i % 2
                            pe.wait_ge(q_done, pair + 1)
                            pe.wait_ge(k_done, pair + 1)
                            wait(pe, masked, n - 1)
                            out = s_ps[c_i % 2]
                            if two:
                                mm = accumulate(out[:, :], [(q_bd[par][:, c, b, :], k_bd[par][:, :, b * T:(b + 1) * T])])
                            else:
                                for h2 in range(4):
                                    mm = accumulate(out[:, h2 * P:(h2 + 1) * P],
                                                    [(q_bd[par][:, c, b, h2 * P:(h2 + 1) * P], k_bd[par][:, c, b * P:(b + 1) * P])])
                            mm.then_inc(s_psum, 1)
                        if prep is not None and i == 0:
                            x_hi, x_lo = (t[:, :, ds(prep * P, P)] for t in (G.feat_hi, G.feat_lo))
                            c_hi, c_lo = (t[:, :, ds(prep * P, P)] for t in (G.ctx_hi, G.ctx_lo))
                            wait(pe, q_done, prep)
                            for c in range(2):
                                cs = slice(c * P, (c + 1) * P)
                                mm = accumulate(q_ps[:, c, :], [ab for k in range(KT) for ab in
                                                split_products(wq_hi[:, k, cs], wq_lo[:, k, cs], x_hi[:, k], x_lo[:, k])])
                            mm.then_inc(q_psum, 1)
                            wait(pe, k_done, prep)
                            if two:
                                mm = accumulate(k_ps[:, :], [ab for k in range(KT) for ab in
                                                split_products(wk_hi[:, k, :], wk_lo[:, k, :], c_hi[:, k], c_lo[:, k])])
                            else:
                                for c in range(2):
                                    cs = slice(c * P, (c + 1) * P)
                                    for s, (t_hi, t_lo) in enumerate(((c_hi, c_lo), (x_hi, x_lo))):
                                        mm = accumulate(k_ps[:, c, :, s * T:(s + 1) * T], [ab for k in range(KT) for ab in
                                                        split_products(wk_hi[:, k, cs], wk_lo[:, k, cs], t_hi[:, k], t_lo[:, k])])
                            mm.then_inc(k_psum, 1)
                        if prep is not None and i == 1:
                            pe.wait_ge(vx_ready, prep + 1)
                            wait(pe, v_done, prep)
                            for b in range(2):
                                mm = accumulate(v_ps[:, b, :], [(vx[:, k, b, :, :], wv[:, k, :]) for k in range(KT)])
                            mm.then_inc(v_psum, 1)
                        if unit_pair is not None:
                            n, par, b, c = UNITS * unit_pair + i, 1 - half, i // 2, i % 2
                            pe.wait_ge(prob_ready, n + 1)
                            wait(pe, pt_done, n)
                            for q in range(4):
                                mm = pe.transpose(t_ps[:, q * P:(q + 1) * P],
                                                  prob[:, :, :].rearrange("p g t -> p (g t)")[:, q * P:(q + 1) * P], G.ident[:, :])
                            mm.then_inc(t_psum, 1)
                            pe.wait_ge(pt_done, n + 1)
                            pe.wait_ge(v_done, unit_pair + 1)
                            wait(pe, ot_done, n)
                            if two:
                                mm = accumulate(c_ps[0:VR, :], [(v_bd[par][:, b, q, :], pt[:, q, :]) for q in range(4)])
                            else:
                                mm = accumulate(c_ps[:, 0:T], [(v_bd[par][:, b, 8 * c + h, :], pt[:, h // 2, (h % 2) * T:(h % 2) * T + T])
                                                               for h in range(8)])
                            mm.then_inc(c_psum, 1)
                            if i == UNITS - 1:
                                pe.wait_ge(ot_done, n + 1)
                                wait(pe, x_done, unit_pair)
                                accumulate(o_ps[:, :], [(ot[:, q, :], wo[:, q, :]) for q in range(4 if two else 2)]).then_inc(o_psum, 1)
                skewed(pe, STEPS, body)

            @block.scalar
            def _(act):
                act.wait_ge(cols_psum, 1)
                act.activation(cols[:, :], c_ps[:, 0:8], ACT.Copy).then_inc(cols_done, 1)
                act.wait_ge(cols_done, 1)
                act.wait_ge(zeroed, 3)
                halves = [slice(0, 64), slice(64, P)]

                def body(j, front, back):
                    for half, i, prep, unit_pair, scores in pair_steps(j, front, back):
                        if unit_pair is not None:
                            n = UNITS * unit_pair + i
                            act.wait_ge(t_psum, n + 1)
                            act.activation(pt[:, :, :].rearrange("p q n -> p (q n)"), t_ps[:, :], ACT.Copy).then_inc(pt_done, 1)
                        if scores:
                            n = UNITS * scores[0] + scores[1]
                            act.wait_ge(shifted, n + 1)
                            tile = soft[scores[1] % 2]
                            act.activation(tile[:, :, :], tile[:, :, :], ACT.Exp).then_inc(exp_done, 1)
                        if prep is not None and i == 0 and two:
                            act.wait_ge(q_psum, prep + 1)
                            for c in range(2):
                                for h in halves:
                                    a = act.activation(q_bd[half][h, c, :, h], q_ps[h, c, :].rearrange("p (b q) -> p b q", b=2),
                                                       ACT.Identity, bias=cols[h, c:c + 1])
                            a.then_inc(q_done, 1)
                        if prep is not None and i == 0 and not two:
                            act.wait_ge(k_psum, prep + 1)
                            for c in range(2):
                                a = act.activation(k_bd[half][:, c, :], k_ps[:, c, :, :].rearrange("p b t -> p (b t)"),
                                                   ACT.Identity, bias=cols[:, 2 + c:3 + c])
                            a.then_inc(k_done, 1)
                        if prep is not None and i == 1:
                            act.wait_ge(v_psum, prep + 1)
                            for b in range(2):
                                if two:
                                    for u, h in enumerate(halves):
                                        dst_ = v_bd[half][h, b, :, :].rearrange("p q c -> p (q c)")
                                        for q in range(4):
                                            o = (2 * q + u) * 8
                                            a = act.activation(dst_[:, 64 * q + o:64 * q + o + 8], v_ps[h, b, o:o + 8], ACT.Copy)
                                else:
                                    for c in range(2):
                                        for h in range(8):
                                            a = act.activation(v_bd[half][:, b, 8 * c + h, 16 * h:16 * h + 16],
                                                               v_ps[:, b, P * c + 16 * h:P * c + 16 * h + 16], ACT.Copy)
                            a.then_inc(v_done, 1)
                        if unit_pair is not None:
                            n, b, c = UNITS * unit_pair + i, i // 2, i % 2
                            act.wait_ge(c_psum, n + 1)
                            if two:
                                act.activation(ot[:, 2 * c:2 * c + 2, b * T:(b + 1) * T], c_ps[0:VR, :].rearrange("p (g q) -> p g q", g=2),
                                               ACT.Identity, bias=cols[0:VR, 4:5]).then_inc(ot_done, 1)
                            else:
                                act.activation(ot[:, c, b * T:(b + 1) * T], c_ps[:, 0:T],
                                               ACT.Identity, bias=cols[:, 4 + c:5 + c]).then_inc(ot_done, 1)
                skewed(act, STEPS, body)

            @block.vector
            def _(dve):
                dve.memset(rows[:, :], 0.0).then_inc(zeroed, 1)
                for n in range(2):
                    dve.memset(q_bd[n][:, :, :, :], 0.0)
                    dve.memset(v_bd[n][:, :, :, :], 0.0).then_inc(zeroed, 1)
                dve.wait_ge(w_in, 16 * len(w_loads))
                for k in range(KT):
                    if two:
                        src = wq_raw[:, k, :].rearrange("p (v g d) -> p g v d", v=8, g=4)
                        pairs = [(wq_hi[:, k, :].rearrange("p (g v d) -> p g v d", g=4, v=8), wq_lo[:, k, :].rearrange("p (g v d) -> p g v d", g=4, v=8), src)]
                        keys = wkv_raw[:, k, 0, :].unsqueeze(1).to_broadcast([P, 2, 64])
                        values = wkv_raw[:, k, 1, :]
                        dve.tensor_copy(wk_f[:, k, :].rearrange("p (g c) -> p g c", g=2), keys)
                    else:
                        pairs = [(wq_hi[:, k, :], wq_lo[:, k, :], wq_raw[:, k, :])]
                        kv = wkv_raw[:, k, :].rearrange("p (c w) -> p w c", w=2)
                        values = kv[:, 1, :]
                        dve.tensor_copy(wk_f[:, k, :], kv[:, 0, :])
                    dve.tensor_copy(wv[:, k, :], values)
                    for hi, lo, src in pairs:
                        dve.tensor_copy(hi, src).then_inc(w_hi, 1)
                        dve.wait_ge(w_hi, 2 * k + 1)
                        dve.tensor_tensor(lo, src, hi.bitcast(F32), ALU.subtract).then_inc(w_ready, 1)
                    dve.wait_ge(w_ready, 1)
                    dve.tensor_copy(wk_hi[:, k, :], wk_f[:, k, :]).then_inc(w_hi, 1)
                    dve.wait_ge(w_hi, 2 * k + 2)
                    lo_ = dve.tensor_tensor(wk_lo[:, k, :], wk_f[:, k, :], wk_hi[:, k, :].bitcast(F32), ALU.subtract)
                lo_.then_inc(w_ready, 1)
                dve.wait_ge(mask_in, 16 * (1 + len(mask_loads)))
                if not two:
                    dve.memset(mask[:, :, T:2 * T], 0.0)
                    dve.tensor_scalar(mask[:, :, 0:T], mask_int[:, :].rearrange("p (b t) -> p b t", b=B), 0, eps_mask,
                                      ALU.is_equal, ALU.mult).then_inc(mask_done, 1)
                    dve.wait_ge(mask_done, 1)
                for p in range(PAIRS):
                    dve.tensor_tensor(G.x_res[:, p, :] if two else dst[:, p, :], G.x_res[:, p, :], o_bias[:, :], ALU.add).then_inc(o_bias_added, 1)
                dve.wait_ge(o_bias_added, PAIRS)
                dve.wait_ge(spread_made, 5 if two else 3)
                dve.wait_ge(cols_done, 1)

                def body(j, front, back):
                    for half, i, prep, unit_pair, scores in pair_steps(j, front, back):
                        if scores:
                            pair, c_i = scores
                            n, b, tile = UNITS * pair + c_i, c_i // 2, soft[c_i % 2]
                            s3 = s_ps[c_i % 2][:, :].rearrange("p (g t) -> p g t", g=GR)
                            dve.wait_ge(s_psum, n + 1)
                            wait(dve, prob_ready, n - 1)
                            dve.scalar_tensor_tensor(tile[:, :, :], s3, score_scale,
                                                     mask[:, ds(2 * pair + b, 1), :].to_broadcast([P, GR, NK]),
                                                     ALU.mult, ALU.add).then_inc(masked, 1)
                            dve.wait_ge(masked, n + 1)
                            dve.tensor_reduce(rmax[:, :], tile[:, :, :], X_AXIS, ALU.max).then_inc(max_done, 1)
                            dve.wait_ge(max_done, n + 1)
                            dve.tensor_tensor(tile[:, :, :], tile[:, :, :], rmax[:, :].unsqueeze(2).to_broadcast([P, GR, NK]),
                                              ALU.subtract).then_inc(shifted, 1)
                        if prep is not None and i == 0:
                            if two:
                                dve.wait_ge(k_psum, prep + 1)
                                dve.scalar_tensor_tensor(k_bd[half][:, :, :], k_ps[:, :].unsqueeze(1).to_broadcast([P, 8, P]),
                                                         cols[:, 2:3], spread[:, :].unsqueeze(2).to_broadcast([P, 8, P]),
                                                         ALU.add, ALU.mult).then_inc(k_done, 1)
                            else:
                                dve.wait_ge(q_psum, prep + 1)
                                for c in range(2):
                                    for b_ in range(2):
                                        q = dve.scalar_tensor_tensor(
                                            q_bd[half][:, c, b_, :].rearrange("p (h t) -> p h t", h=8),
                                            q_ps[:, c, b_ * T:(b_ + 1) * T].unsqueeze(1).to_broadcast([P, 8, T]),
                                            cols[:, c:c + 1], spread[:, :].unsqueeze(2).to_broadcast([P, 8, T]),
                                            ALU.add, ALU.mult)
                                q.then_inc(q_done, 1)
                        if scores:
                            dve.wait_ge(exp_done, n + 1)
                            dve.tensor_reduce(rsum[:, :], tile[:, :, :], X_AXIS, ALU.add).then_inc(sum_done, 1)
                            dve.wait_ge(sum_done, n + 1)
                            wait(dve, prob_ready, n)
                            dve.reciprocal(rinv[:, :], rsum[:, :]).then_inc(inv_done, 1)
                        if unit_pair is not None and i == UNITS - 1:
                            dve.wait_ge(o_psum, unit_pair + 1)
                            x = (G.x_res if two else dst)[:, ds(unit_pair, 1), :]
                            dve.tensor_tensor(x, o_ps[:, :], x, ALU.add).then_inc(x_done, 1)
                skewed(dve, STEPS, body)


class Global:
    pass


def build(nc, A, out, stage="L3"):
    G = Global()
    with Mem(nc, "g") as m:
        G.psum = m.stack.enter_context(nc.psum_tensor("psum", [P, PSUM_BANKS * BANK], F32))
        G.x_res = m.sb("x_res", [P, PAIRS, D])
        G.ctx_hi = m.sb("ctx_hi", [P, KT, TOK], F32R)
        G.ctx_lo = m.sb("ctx_lo", [P, KT, TOK], F32R)
        G.ident = m.sb("ident", [P, P])
        G.minus_half = m.sb("minus_half", [P, 2 * PAIRS])
        with Mem(nc, "c") as mc:
            G.ctx_tok = mc.sb("ctx_tok", [P, PAIRS, D])
            phase_setup(nc, A, G)
            phase_layer0(nc, A, G)
        if stage == "L0":
            return phase_store(nc, G.x_res, out)
        with Mem(nc, "one") as m1:
            G.cols = m1.sb("cols", [P, 2, 5 * H1])
            G.bias_k_hi = m1.sb("bias_k_hi", [P, 2, H1], F32R)
            G.bias_k_lo = m1.sb("bias_k_lo", [P, 2, H1], F32R)
            G.bvo = m1.sb("bvo", [H1 + 1, 2, D])
            G.bias_prob = m1.sb("bias_prob", [P, PAIRS, H1 + 1])
            G.feat_hi = m1.sb("feat_hi", [P, KT, TOK], F32R)
            G.feat_lo = m1.sb("feat_lo", [P, KT, TOK], F32R)
            phase_layer1_constants(nc, A, G)
            for i in (1, 2):
                phase_features(nc, G, f"ln{i}", G.x_res, G.feat_hi, G.feat_lo, "ln", 1e-5,
                               A[f"L1_xattn_ln{i}_scale"], A[f"L1_xattn_ln{i}_offset"])
                phase_layer1_attention(nc, A, G, i)
                if stage == f"A{i}p":
                    return phase_store(nc, G.x_res, out)
                phase_bias_token(nc, G, i)
                if stage == f"A{i}":
                    return phase_store(nc, G.x_res, out)
        with Mem(nc, "rest") as m2:
            G.feat_hi = m2.sb("feat_hi", [P, KT, TOK], F32R)
            G.feat_lo = m2.sb("feat_lo", [P, KT, TOK], F32R)
            phase_features(nc, G, "ln3", G.x_res, G.feat_hi, G.feat_lo, "ln", 1e-5,
                           A["L1_xattn_ln_mlp_scale"], A["L1_xattn_ln_mlp_offset"])
            phase_mlp(nc, A, G, "mlp1", *(A[f"L1_xattn_{n}"] for n in ("w_fc1", "b_fc1", "w_fc2", "b_fc2")), ACT.Gelu)
            if stage == "M1":
                return phase_store(nc, G.x_res, out)
            phase_features(nc, G, "ft2", G.x_res, G.feat_hi, G.feat_lo, "plain")
            phase_narrow_attention(nc, A, G, 2, G.x_res)
            phase_features(nc, G, "ln4", G.x_res, G.feat_hi, G.feat_lo, "ln", 1e-6,
                           A["L2_xattn_gamma"], A["L2_xattn_beta"], update=True)
            if stage == "L2":
                return phase_store(nc, G.x_res, out)
            with Mem(nc, "res") as m3:
                attn_out = m3.sb("attn_out", [P, PAIRS, D])
                phase_narrow_attention(nc, A, G, 3, attn_out)
                if stage == "L3a":
                    return phase_store(nc, attn_out, out)
                phase_features(nc, G, "rms", attn_out, G.feat_hi, G.feat_lo, "rms", 1e-6, A["L3_xattn_postnorm_w"])
            phase_mlp(nc, A, G, "mlp3", *(A[f"L3_xattn_{n}"] for n in ("mlp_w1", "mlp_b1", "mlp_w2", "mlp_b2")),
                      ACT.Gelu_apprx_tanh)
        phase_store(nc, G.x_res, out)


def phase_store(nc, src, out):
    with Mem(nc, "st") as m:
        stored = m.sem("stored")
        with nc.Block() as block:
            @block.sync
            def _(sp):
                sp.dma_start(out.rearrange("(p b) t d -> (b t) p d", b=2), src[:, :, :]).then_inc(stored, 16)
                sp.wait_ge(stored, 16)


def kernel(**inputs):
    import numpy as _np
    import concourse.bacc as _bacc
    from concourse import mybir as _mybir
    from concourse.bass_utils import run_bass_kernel_spmd as _run

    nc = _bacc.Bacc("TRN2", target_bir_lowering=False, num_devices=1)
    arrays, args = {}, {}
    for name, value in inputs.items():
        a = _np.ascontiguousarray(value)
        arrays[f"in_{name}"] = a
        args[name] = nc.dram_tensor(f"in_{name}", a.shape, _mybir.dt.from_np(a.dtype), kind="ExternalInput").ap()
    out = nc.dram_tensor("out_0", (B, T, D), F32, kind="ExternalOutput").ap()
    build(nc, args, out)
    r = _run(nc, [arrays], core_ids=[0])
    return r.results[0]["out_0"]
```

```python
import concourse.bass as bass
from concourse import mybir
from contextlib import ExitStack
import numpy as np

F32 = mybir.dt.float32
F32R = mybir.dt.float32r
I32 = mybir.dt.int32
ALU = mybir.AluOpType
ACT = mybir.ActivationFunctionType
X_AXIS = mybir.AxisListType.X

B, T, D = 32, 64, 256
P = 128
PAIRS = B * T // P
KT = D // P
TOK = B * T
BLK = 512
NBLK = TOK // BLK
PPB = BLK // P
H1, K1 = 16, 128
HG = 4
NG = H1 // HG
FF = 1024
FT = FF // P
BANK, PSUM_BANKS = 512, 8
ds = bass.ds


class Mem:

    def __init__(self, nc, tag, psum=None):
        self.nc, self.tag, self.psum, self.stack, self.banks, self.sems = nc, tag, psum, ExitStack(), 0, []

    def __enter__(self):
        self.stack.__enter__()
        return self

    def __exit__(self, *a):
        numbers = sorted(s.num for s in self.sems)
        while numbers:
            run = [n for i, n in enumerate(numbers) if n == numbers[0] + i]
            self.nc.sync.sem_clear(range(run[0], run[-1] + 1))
            numbers = numbers[len(run):]
        return self.stack.__exit__(*a)

    def sb(self, name, shape, dt=F32):
        return self.stack.enter_context(self.nc.sbuf_tensor(f"{self.tag}_{name}", shape, dt))

    def ps(self, name, shape=(P, 512)):
        size, at = int(np.prod(shape[1:])), self.banks * BANK
        self.banks += -(-size // BANK)
        assert self.banks <= PSUM_BANKS, name
        view = self.psum[0:shape[0], at:at + size]
        dims = " ".join(f"d{n}" for n in range(len(shape) - 1))
        sizes = {f"d{n}": s for n, s in enumerate(shape[1:])}
        return view.rearrange(f"p ({dims}) -> p {dims}", **sizes) if len(shape) > 2 else view

    def sem(self, name):
        self.sems.append(self.stack.enter_context(self.nc.semaphore(f"{self.tag}_{name}")))
        return self.sems[-1]


def split_products(lhs_hi, lhs_lo, rhs_hi, rhs_lo):
    return [(lhs_hi, rhs_hi), (lhs_hi, rhs_lo), (lhs_lo, rhs_hi)]


def skewed(eng, n, body):
    body(0, True, False)
    with eng.Fori(1, n) as j:
        body(j, True, True)
    body(n, False, True)


def phase_setup(nc, A, G):
    with Mem(nc, "su", G.psum) as m:
        ctx_psum = [m.ps(f"ctx_psum{i}", (P, KT, P)) for i in range(2)]
        x_in, ctx_in = m.sem("x_in"), m.sem("ctx_in")
        ident_zero, ident_made = m.sem("ident_zero"), m.sem("ident_made")
        transposed, hi_done, lo_done = m.sem("transposed"), m.sem("hi_done"), m.sem("lo_done")
        x_dram = A["x"].rearrange("(p b) t d -> (b t) p d", b=2)
        c_dram = A["ctx_2048"].rearrange("(p b) t d -> (b t) p d", b=2)
        with nc.Block() as block:
            @block.sync
            def _(sp):
                for q in range(4):
                    sp.dma_start(G.ctx_tok[:, 4 * q:4 * q + 4, :], c_dram[:, 4 * q:4 * q + 4, :]).then_inc(ctx_in, 16)
                for q in range(4):
                    sp.dma_start(G.x_res[:, 4 * q:4 * q + 4, :], x_dram[:, 4 * q:4 * q + 4, :]).then_inc(x_in, 16)
                sp.wait_ge(x_in, 64)

            @block.gpsimd
            def _(pool):
                pool.memset(G.ident[:, :], 0.0).then_inc(ident_zero, 1)
                pool.wait_ge(ident_zero, 1)
                pool.affine_select(out=G.ident[:, :], in_=G.ident[:, :], compare_op=ALU.not_equal, fill=1.0,
                                   base=0, pattern=[[-1, P]], channel_multiplier=1).then_inc(ident_made, 1)
                pool.memset(G.minus_half[:, :], -0.5)

            @block.tensor
            def _(pe):
                pe.wait_ge(ident_made, 1)
                pe.wait_ge(ctx_in, 64)
                for p in range(PAIRS):
                    if p >= 2:
                        pe.wait_ge(lo_done, p - 1)
                    for k in range(KT):
                        mm = pe.transpose(ctx_psum[p % 2][:, k, :], G.ctx_tok[:, p, k * P:(k + 1) * P], G.ident[:, :])
                    mm.then_inc(transposed, 1)

            @block.scalar
            def _(act):
                for p in range(PAIRS):
                    act.wait_ge(transposed, p + 1)
                    act.activation(G.ctx_hi[:, :, p * P:(p + 1) * P], ctx_psum[p % 2][:, :, :], ACT.Copy).then_inc(hi_done, 1)

            @block.vector
            def _(dve):
                for p in range(PAIRS):
                    dve.wait_ge(hi_done, p + 1)
                    dve.tensor_tensor(G.ctx_lo[:, :, p * P:(p + 1) * P], ctx_psum[p % 2][:, :, :],
                                      G.ctx_hi[:, :, p * P:(p + 1) * P].bitcast(F32), ALU.subtract).then_inc(lo_done, 1)


def phase_layer0(nc, A, G):
    with Mem(nc, "l0", G.psum) as m:
        w_nat = m.sb("w_nat", [P, 4, P])
        w_t = m.sb("w_t", [P, 4, P])
        bias = m.sb("bias", [P, 4])
        obias = m.sb("obias", [P, 1])
        stats = m.sb("stats", [P, 2 * PAIRS, 6])
        mv = m.sb("mv", [P, 2 * PAIRS, 2])
        rstd = m.sb("rstd", [P, 2 * PAIRS])
        xn = m.sb("xn", [P, 2 * PAIRS, D])
        c_fix = [m.sb(f"c_fix{i}", [P, D]) for i in range(2)]
        mix = m.sb("mix", [P, 2, D])
        prob = [m.sb(f"prob{i}", [P, 2, 2, D]) for i in range(2)]
        prob_t = m.sb("prob_t", [P, 2, 2, D])
        y_sb = [m.sb(f"y{i}", [P, 2, P]) for i in range(2)]
        nmax = m.sb("nmax", [P, 2, 2])
        ssum = m.sb("ssum", [P, 2, 4])
        rsum = m.sb("rsum", [P, 4])
        mix_ps = m.ps("mix_ps", (P, 2, D))
        y_ps = m.ps("y_ps", (P, 2, P))
        s_ps = [m.ps(f"s_ps{i}", (P, 2, D)) for i in range(2)]
        t_ps = [m.ps(f"t_ps{i}", (P, 2, D)) for i in range(2)]
        o_ps = m.ps("o_ps", (P, D))
        w_zero, w_in, w_turned, w_kept = m.sem("w_zero"), m.sem("w_in"), m.sem("w_turned"), m.sem("w_kept")
        g_psum, w_ready = m.sem("g_psum"), m.sem("w_ready")
        stats_done, mv_done, eps_added, rstd_done, xn_done = (m.sem(n) for n in
            ("stats_done", "mv_done", "eps_added", "rstd_done", "xn_done"))
        c_fixed, mix_psum, mix_done, s_psum = (m.sem(n) for n in ("c_fixed", "mix_psum", "mix_done", "s_psum"))
        max_done, exp_done, rsum_done, prob_done = (m.sem(n) for n in ("max_done", "exp_done", "rsum_done", "prob_done"))
        t_psum, t_act, t_dve = (m.sem(n) for n in ("t_psum", "t_act", "t_dve"))
        y_psum, y_done, o_psum, x_done = (m.sem(n) for n in ("y_psum", "y_done", "o_psum", "x_done"))
        STEPS = PAIRS // 2
        with nc.Block() as block:
            @block.sync
            def _(sp):
                sp.wait_ge(w_zero, 1)
                for i, n in enumerate(("Wn", "Wm", "Wl", "Wo")):
                    for b in range(2):
                        sp.dma_start(w_nat[64 * b:64 * b + 64, i, 64 * b:64 * b + 64], A[f"L0_xattn_{n}"]).then_inc(w_in, 16)
                for i, n in enumerate(("bn", "bm", "bl", "bo")):
                    for b in range(2):
                        sp.dma_start(bias[64 * b:64 * b + 64, i:i + 1],
                                     A[f"L0_xattn_{n}"].rearrange("(p o) -> p o", o=1)).then_inc(w_in, 16)

            @block.gpsimd
            def _(pool):
                pool.wait_ge(mv_done, 2 * PAIRS)
                pool.tensor_scalar(rstd[:, :], mv[:, :, 1], 1e-5, None, ALU.add).then_inc(eps_added, 1)
                pool.wait_ge(eps_added, 1)
                pool.tensor_tensor(rstd[:, :], rstd[:, :], G.minus_half[:, 0:2 * PAIRS], ALU.pow).then_inc(rstd_done, 1)

                def body(j, front, back):
                    for q in range(2):
                        if front:
                            u = 2 * j + q
                            if back:
                                pool.wait_ge(y_psum, u - 1)
                            pool.tensor_copy(c_fix[q][:, :], G.ctx_tok[:, ds(u, 1), :]).then_inc(c_fixed, 1)
                body(0, True, False)
                with pool.Fori(1, STEPS) as j:
                    body(j, True, True)

            @block.tensor
            def _(pe):
                pe.wait_ge(w_in, 16 * 16)
                for i, src in enumerate((0, 1, 3)):
                    mm = pe.transpose(mix_ps[:, i // 2, (i % 2) * P:(i % 2) * P + P], w_nat[:, src, :], G.ident[:, :])
                mm.then_inc(w_turned, 1)
                pe.wait_ge(w_kept, 1)
                pe.matmul(y_ps[:, 0, :], w_nat[:, 2, :], w_t[:, 3, :], start=True, stop=True)
                pe.matmul(y_ps[:, 1, 0:1], w_t[:, 3, :], bias[:, 2:3], start=True, stop=True).then_inc(g_psum, 1)
                pe.wait_ge(w_ready, 2)
                pe.wait_ge(xn_done, 2 * PAIRS)

                def body(j, front, back):
                    for q in range(2):
                        u = 2 * j + q
                        if back:
                            r = u - 2
                            pe.wait_ge(prob_done, r + 1)
                            pe.wait_ge(t_act, r + 1)
                            pe.wait_ge(t_dve, r + 1)
                            for b in range(2):
                                for sh in range(2):
                                    for th in range(2):
                                        mm = pe.transpose(t_ps[b][:, sh, th * P:th * P + P],
                                                          prob[q][:, b, th, sh * P:sh * P + P], G.ident[:, :])
                                mm.then_inc(t_psum, 1)
                        if front:
                            if back or q:
                                pe.wait_ge(mix_done, u)
                            for i in range(2):
                                mm = pe.matmul(mix_ps[:, i, :], w_t[:, i, :], xn[:, ds(i * PAIRS + u, 1), :],
                                               start=True, stop=True)
                            mm.then_inc(mix_psum, 1)
                            pe.wait_ge(mix_done, u + 1)
                            if back or q:
                                pe.wait_ge(exp_done, 4 * u)
                            for b in range(2):
                                for th in range(2):
                                    mm = pe.matmul(s_ps[b][:, th, :], mix[64 * b:64 * b + 64, 0, th * P:th * P + P],
                                                   mix[64 * b:64 * b + 64, 1, :], start=True, stop=True)
                                mm.then_inc(s_psum, 1)
                        if back:
                            pe.wait_ge(t_act, r + 2)
                            pe.wait_ge(t_dve, r + 2)
                            pe.wait_ge(x_done, r + 1)
                            for b in range(2):
                                for sh in range(2):
                                    mm = pe.matmul(o_ps[64 * b:64 * b + 64, :], y_sb[q][:, sh, 64 * b:64 * b + 64],
                                                   prob_t[:, b, sh, :], start=(sh == 0), stop=(sh == 1))
                            mm.then_inc(o_psum, 1)
                        if front:
                            pe.wait_ge(c_fixed, u + 1)
                            if back or q:
                                pe.wait_ge(y_done, u)
                            for sh in range(2):
                                mm = pe.matmul(y_ps[:, sh, :], c_fix[q][:, sh * P:sh * P + P], w_t[:, 2, :],
                                               start=True, stop=True)
                            mm.then_inc(y_psum, 1)
                skewed(pe, STEPS, body)

            @block.scalar
            def _(act):
                def body(j, front, back):
                    for q in range(2):
                        u = 2 * j + q
                        if back:
                            r = u - 2
                            act.wait_ge(t_psum, 2 * r + 1)
                            act.activation(prob_t[:, 0, :, :], t_ps[0][:, :, :], ACT.Copy).then_inc(t_act, 1)
                        if front:
                            act.wait_ge(mix_psum, u + 1)
                            act.activation(mix[:, 0, :], mix_ps[:, 0, :], ACT.Identity, bias=bias[:, 0:1])
                            act.activation(mix[:, 1, :], mix_ps[:, 1, :], ACT.Identity, bias=bias[:, 1:2]).then_inc(mix_done, 1)
                            for b in range(2):
                                act.wait_ge(max_done, 2 * u + b + 1)
                                for th in range(2):
                                    act.activation(prob[q][:, b, th, :], s_ps[b][:, th, :], ACT.Exp,
                                                   bias=nmax[:, b, th:th + 1],
                                                   accum_out=ssum[:, q, 2 * b + th:2 * b + th + 1]).then_inc(exp_done, 1)
                act.wait_ge(w_in, 16 * 16)
                skewed(act, STEPS, body)

            @block.vector
            def _(dve):
                dve.memset(w_nat[:, :, :], 0.0).then_inc(w_zero, 1)
                dve.memset(nmax[:, :, :], 0.0).then_inc(t_act, 1)
                dve.memset(rsum[:, :], 0.0).then_inc(t_dve, 1)
                dve.memset(obias[:, :], 0.0).then_inc(x_done, 1)
                dve.wait_ge(w_turned, 1)
                dve.tensor_copy(w_t[:, 0:2, :], mix_ps[:, 0, :])
                dve.tensor_copy(w_t[:, 3, :], mix_ps[:, 1, 0:P]).then_inc(w_kept, 1)
                dve.wait_ge(g_psum, 1)
                dve.tensor_copy(w_t[:, 2, :], y_ps[:, 0, :]).then_inc(w_ready, 1)
                dve.wait_ge(x_done, 1)
                dve.tensor_tensor(obias[:, :], y_ps[:, 1, 0:1], bias[:, 3:4], ALU.add).then_inc(w_ready, 1)
                for i in range(2 * PAIRS):
                    src = G.x_res if i < PAIRS else G.ctx_tok
                    dve.bn_stats(stats[:, i, :], src[:, i % PAIRS, :]).then_inc(stats_done, 1)
                for i in range(2 * PAIRS):
                    dve.wait_ge(stats_done, i + 1)
                    dve.bn_aggr(mv[:, i, :], stats[:, i, :]).then_inc(mv_done, 1)
                dve.wait_ge(rstd_done, 1)
                dve.wait_ge(mv_done, 2 * PAIRS)
                for i in range(2 * PAIRS):
                    src = G.x_res if i < PAIRS else G.ctx_tok
                    dve.tensor_scalar(xn[:, i, :], src[:, i % PAIRS, :], mv[:, i, 0:1], rstd[:, i:i + 1],
                                      ALU.subtract, ALU.mult).then_inc(xn_done, 1)
                dve.wait_ge(w_ready, 2)
                dve.wait_ge(t_dve, 1)

                def body(j, front, back):
                    for q in range(2):
                        u = 2 * j + q
                        if back:
                            r = u - 2
                            dve.wait_ge(t_psum, 2 * r + 2)
                            dve.tensor_copy(prob_t[:, 1, :, :], t_ps[1][:, :, :]).then_inc(t_dve, 1)
                        if front:
                            if back or q:
                                dve.wait_ge(exp_done, 4 * u)
                            for b in range(2):
                                dve.wait_ge(s_psum, 2 * u + b + 1)
                                dve.tensor_reduce(nmax[:, b, :], s_ps[b][:, :, :], X_AXIS, ALU.max, negate=True).then_inc(max_done, 1)
                        if back:
                            dve.wait_ge(o_psum, r + 1)
                            dve.scalar_tensor_tensor(G.x_res[:, ds(r, 1), :], o_ps[:, :], obias[:, 0:1],
                                                     G.x_res[:, ds(r, 1), :], ALU.add, ALU.add).then_inc(x_done, 1)
                        if front:
                            dve.wait_ge(exp_done, 4 * u + 4)
                            if back or q:
                                dve.wait_ge(prob_done, u)
                            dve.reciprocal(rsum[:, :], ssum[:, q, :]).then_inc(rsum_done, 1)
                            dve.wait_ge(rsum_done, u + 1)
                            for i in range(4):
                                sc = dve.tensor_scalar(prob[q][:, i // 2, i % 2, :], prob[q][:, i // 2, i % 2, :],
                                                       rsum[:, i:i + 1], None, ALU.mult)
                            sc.then_inc(prob_done, 1)
                            dve.wait_ge(y_psum, u + 1)
                            dve.tensor_copy(y_sb[q][:, :, :], y_ps[:, :, :]).then_inc(y_done, 1)
                skewed(dve, STEPS, body)


def phase_features(nc, G, tag, src, dst_hi, dst_lo, kind, eps=0.0, scale=None, offset=None,
                   update=False):
    with Mem(nc, tag, G.psum) as m:
        affine = m.sb("affine", [P, 2, KT])
        row_in = m.sb("row_in", [2 * KT, P])
        stats = m.sb("stats", [P, PAIRS, 6])
        mv = m.sb("mv", [P, PAIRS, 2])
        rstd = m.sb("rstd", [P, PAIRS])
        normed = m.sb("normed", [P, PAIRS, D])
        raw = [m.sb(f"raw{i}", [P, BLK]) for i in range(2)]
        feat_ps = [m.ps(f"feat_ps{i}", (P, BLK)) for i in range(3)]
        affine_in, stats_done, mv_done, eps_added, rstd_done, normed_done = (m.sem(n) for n in
            ("affine_in", "stats_done", "mv_done", "eps_added", "rstd_done", "normed_done"))
        feat_psum, raw_done, hi_done, lo_done = (m.sem(n) for n in ("feat_psum", "raw_done", "hi_done", "lo_done"))
        affine_ps = m.ps("affine_ps", (P, 2 * KT))
        affine_psum, affine_done, rows_zero = m.sem("affine_psum"), m.sem("affine_done"), m.sem("rows_zero")
        if update:
            spread_affine = m.sb("spread_affine", [P, 2, D])
            spread_in, scaled = m.sem("spread_in"), m.sem("scaled")
        normalized = src if kind == "plain" else normed
        with nc.Block() as block:
            @block.sync
            def _(sp):
                if scale is not None:
                    sp.wait_ge(rows_zero, 1)
                    sp.dma_start(row_in[0:KT, :], scale.rearrange("(k p) -> k p", p=P)).then_inc(affine_in, 16)
                    if offset is not None:
                        sp.dma_start(row_in[KT:2 * KT, :], offset.rearrange("(k p) -> k p", p=P)).then_inc(affine_in, 16)
                if update:
                    for n, v in enumerate((scale, offset)):
                        sp.dma_start(spread_affine[:, n, :], v.rearrange("(o n) -> o n", o=1).partition_broadcast(P)).then_inc(spread_in, 16)

            @block.gpsimd
            def _(pool):
                if kind != "plain":
                    pool.wait_ge(mv_done, PAIRS)
                    if kind == "rms":
                        pool.tensor_tensor(rstd[:, :], mv[:, :, 0], mv[:, :, 0], ALU.mult).then_inc(eps_added, 1)
                        pool.wait_ge(eps_added, 1)
                        pool.tensor_tensor(rstd[:, :], rstd[:, :], mv[:, :, 1], ALU.add).then_inc(eps_added, 1)
                        pool.wait_ge(eps_added, 2)
                        pool.tensor_scalar(rstd[:, :], rstd[:, :], eps, None, ALU.add).then_inc(eps_added, 1)
                    else:
                        pool.tensor_scalar(rstd[:, :], mv[:, :, 1], eps, None, ALU.add).then_inc(eps_added, 3)
                    pool.wait_ge(eps_added, 3)
                    pool.tensor_tensor(rstd[:, :], rstd[:, :], G.minus_half[:, 0:PAIRS], ALU.pow).then_inc(rstd_done, 1)

            @block.tensor
            def _(pe):
                if scale is not None:
                    pe.wait_ge(affine_in, 16 if offset is None else 32)
                    pe.transpose(affine_ps[:, :], row_in[:, :], G.ident[0:2 * KT, 0:2 * KT]).then_inc(affine_psum, 1)
                for n in range(NBLK * KT):
                    b, k = n // KT, n % KT
                    if kind != "plain":
                        pe.wait_ge(normed_done, PPB * (b + 1))
                    if n >= 3:
                        pe.wait_ge(raw_done, n - 2)
                    for i in range(PPB):
                        mm = pe.transpose(feat_ps[n % 3][:, i * P:(i + 1) * P],
                                          normalized[:, PPB * b + i, k * P:(k + 1) * P], G.ident[:, :])
                    mm.then_inc(feat_psum, 1)

            @block.scalar
            def _(act):
                if scale is not None:
                    act.wait_ge(affine_psum, 1)
                    act.activation(affine[:, :, :].rearrange("p a k -> p (a k)"), affine_ps[:, :], ACT.Copy).then_inc(affine_done, 1)
                    act.wait_ge(affine_done, 1)
                for n in range(NBLK * KT):
                    k = n % KT
                    act.wait_ge(feat_psum, n + 1)
                    to = raw[n % 2][:, :]
                    if dst_lo is None:
                        to = dst_hi[:, k, (n // KT) * BLK:(n // KT + 1) * BLK]
                    elif n >= 2:
                        act.wait_ge(lo_done, n - 1)
                    if scale is not None:
                        act.activation(to, feat_ps[n % 3][:, :], ACT.Identity,
                                       bias=affine[:, 1, k:k + 1], scale=affine[:, 0, k:k + 1]).then_inc(raw_done, 1)
                    else:
                        act.activation(to, feat_ps[n % 3][:, :], ACT.Copy).then_inc(raw_done, 1)

            @block.vector
            def _(dve):
                dve.memset(row_in[:, :], 0.0).then_inc(rows_zero, 1)
                if kind != "plain":
                    for i in range(PAIRS):
                        dve.bn_stats(stats[:, i, :], src[:, i, :]).then_inc(stats_done, 1)
                    for i in range(PAIRS):
                        dve.wait_ge(stats_done, i + 1)
                        dve.bn_aggr(mv[:, i, :], stats[:, i, :]).then_inc(mv_done, 1)
                    dve.wait_ge(rstd_done, 1)
                    dve.wait_ge(mv_done, PAIRS)
                    for i in range(PAIRS):
                        if kind == "ln":
                            dve.tensor_scalar(normed[:, i, :], src[:, i, :], mv[:, i, 0:1], rstd[:, i:i + 1],
                                              ALU.subtract, ALU.mult).then_inc(normed_done, 1)
                        else:
                            dve.tensor_scalar(normed[:, i, :], src[:, i, :], rstd[:, i:i + 1], None,
                                              ALU.mult).then_inc(normed_done, 1)
                for n in range(NBLK * KT if dst_lo is not None else 0):
                    b, k = n // KT, n % KT
                    hi, lo = dst_hi[:, k, b * BLK:(b + 1) * BLK], dst_lo[:, k, b * BLK:(b + 1) * BLK]
                    dve.wait_ge(raw_done, n + 1)
                    dve.tensor_copy(hi, raw[n % 2][:, :]).then_inc(hi_done, 1)
                    dve.wait_ge(hi_done, n + 1)
                    dve.tensor_tensor(lo, raw[n % 2][:, :], hi.bitcast(F32), ALU.subtract).then_inc(lo_done, 1)
                if update:
                    dve.wait_ge(spread_in, 32)
                    dve.wait_ge(normed_done, PAIRS)
                    for p in range(PAIRS):
                        dve.tensor_tensor(src[:, p, :], normed[:, p, :], spread_affine[:, 0, :], ALU.mult).then_inc(scaled, 1)
                    for p in range(PAIRS):
                        dve.wait_ge(scaled, p + 1)
                        dve.tensor_tensor(src[:, p, :], src[:, p, :], spread_affine[:, 1, :], ALU.add)



CONST_ROWS = ("bq", "bk", "bias_k", "bias_v", "bv")


def phase_layer1_constants(nc, A, G):
    with Mem(nc, "l1c", G.psum) as m:
        rows = m.sb("rows", [5 * H1, 2, P])
        wo = [m.sb(f"wo{i}", [P, H1, D]) for i in range(2)]
        lhs = m.sb("lhs", [P, 2, H1, H1 + 1])
        unit = m.sb("unit", [1, H1 + 1])
        bo = m.sb("bo", [1, 2, D])
        cols_ps = m.ps("cols_ps", (P, 2, 5 * H1))
        bvo_ps = m.ps("bvo_ps", (H1 + 1, 2, D))
        rows_in, wo_in, cleared, unit_zero = (m.sem(n) for n in ("rows_in", "wo_in", "cleared", "unit_zero"))
        cols_psum, cols_done, lhs_done, bvo_psum = (m.sem(n) for n in
            ("cols_psum", "cols_done", "lhs_done", "bvo_psum"))
        with nc.Block() as block:
            @block.sync
            def _(sp):
                for i in range(2):
                    for n, name in enumerate(CONST_ROWS):
                        src = A[f"L1_xattn_{name}{i + 1}"]
                        src = src.rearrange("a b h d -> (a b h) d") if len(src.shape) == 4 else src.rearrange("(h d) -> h d", d=K1)
                        sp.dma_start(rows[n * H1:(n + 1) * H1, i, :], src).then_inc(rows_in, 16)
                    sp.dma_start(bo[:, i, :], A[f"L1_xattn_bo{i + 1}"].rearrange("(o n) -> o n", o=1)).then_inc(rows_in, 16)
                for i in range(2):
                    sp.dma_start(wo[i][:, :, :], A[f"L1_xattn_wo{i + 1}"].rearrange("(h d) n -> d h n", d=K1)).then_inc(wo_in, 16)
                    sp.wait_ge(wo_in, 16 * (i + 1))

            @block.gpsimd
            def _(pool):
                pool.memset(lhs[:, :, :, :], 0.0).then_inc(cleared, 1)
                pool.memset(unit[:, :], 0.0).then_inc(unit_zero, 1)
                pool.wait_ge(unit_zero, 1)
                pool.memset(unit[:, H1:H1 + 1], 1.0).then_inc(cleared, 1)

            @block.tensor
            def _(pe):
                pe.wait_ge(rows_in, 16 * 12)
                for i in range(2):
                    mm = pe.transpose(cols_ps[:, i, :], rows[:, i, :], G.ident[0:5 * H1, 0:5 * H1])
                mm.then_inc(cols_psum, 1)
                pe.wait_ge(lhs_done, 2)
                pe.wait_ge(cleared, 2)
                for i in range(2):
                    pe.wait_ge(wo_in, 16 * (i + 1))
                    for h in range(H1):
                        pe.matmul(bvo_ps[:, i, :], lhs[:, i, h, :], wo[i][:, h, :], start=(h == 0), stop=False)
                    mm = pe.matmul(bvo_ps[:, i, :], unit[:, :], bo[:, i, :], start=False, stop=True)
                mm.then_inc(bvo_psum, 1)

            @block.vector
            def _(dve):
                dve.wait_ge(cols_psum, 1)
                dve.tensor_copy(G.cols[:, :, :], cols_ps[:, :, :]).then_inc(cols_done, 1)
                dve.wait_ge(cols_done, 1)
                bias_v, bv = (G.cols[:, :, n * H1:(n + 1) * H1] for n in (3, 4))
                dve.wait_ge(cleared, 2)
                diagonal = lhs[:, :, :, :].rearrange("p i h c -> p i (h c)")[:, :, 0:H1 * (H1 + 1):H1 + 2]
                dve.tensor_tensor(diagonal, bias_v, bv, ALU.subtract).then_inc(lhs_done, 1)
                dve.tensor_copy(lhs[:, :, :, H1], bv).then_inc(lhs_done, 1)
                dve.wait_ge(bvo_psum, 1)
                dve.tensor_copy(G.bvo[:, :, :], bvo_ps[:, :, :])


def phase_layer1_attention(nc, A, G, i):
    tag = f"att{i}"
    NI = NG * NBLK
    KP = T + 1
    name = lambda n: A[f"L1_xattn_{n}{i}"]
    q_scale = float(K1) ** -0.5
    with Mem(nc, tag, G.psum) as m:
        q_sb = m.sb("q_sb", [P, HG, BLK])
        k_sb = m.sb("k_sb", [P, HG, 2 * PPB, KP])
        v_sb = m.sb("v_sb", [P, PPB, HG * K1])
        pt = m.sb("pt", [P, BLK])
        ot_hi, ot_lo = (m.sb(n, [P, HG, BLK], F32R) for n in ("ot_hi", "ot_lo"))
        wqk_hi, wqk_lo = (m.sb(n, [P, HG, 2, KT, K1], F32R) for n in ("wqk_hi", "wqk_lo"))
        wv_hi, wv_lo = (m.sb(n, [P, KT, HG * K1], F32R) for n in ("wv_hi", "wv_lo"))
        wo_hi, wo_lo = (m.sb(n, [P, HG, D], F32R) for n in ("wo_hi", "wo_lo"))
        cf_hi, cf_lo = (m.sb(n, [P, KT, BLK], F32R) for n in ("cf_hi", "cf_lo"))
        stage_qk = m.sb("stage_qk", [P, 2, 2, KT, K1])
        stage_vo = m.sb("stage_vo", [P, KT * HG * K1])
        soft = m.sb("soft", [P, PPB, KP])
        prob = m.sb("prob", [P, PPB, P])
        rmax = m.sb("rmax", [P, PPB])
        rsum = m.sb("rsum", [P, PPB])
        rinv = m.sb("rinv", [P, PPB])
        q_ps, k_ps = m.ps("q_ps"), m.ps("k_ps")
        s_ps = m.ps("s_ps", (P, PPB, 2 * P))
        t_ps, c_ps = m.ps("t_ps"), m.ps("c_ps")
        o_ps = [m.ps(f"o_ps{n}", (P, 2, D)) for n in range(2)]
        v_ps = [q_ps, k_ps]
        qk_in = [m.sem(f"qk_in{n}") for n in range(2)]
        vo_in, w_hi, wqk_ready, wv_ready, wo_ready, cf_ready, kb_ready = (m.sem(n) for n in
            ("vo_in", "w_hi", "wqk_ready", "wv_ready", "wo_ready", "cf_ready", "kb_ready"))
        q_psum, k_psum, v_psum, s_psum, t_psum, c_psum, o_psum = (m.sem(n) for n in
            ("q_psum", "k_psum", "v_psum", "s_psum", "t_psum", "c_psum", "o_psum"))
        q_ready, k_ready, pt_ready, ot_high, ot_ready, x_added = (m.sem(n) for n in
            ("q_ready", "k_ready", "pt_ready", "ot_high", "ot_ready", "x_added"))
        v_ready = [m.sem("v_ready_act"), m.sem("v_ready_dve")]
        max_done, shifted, exp_done, sum_done, inv_done, prob_ready = (m.sem(n) for n in
            ("max_done", "shifted", "exp_done", "sum_done", "inv_done", "prob_ready"))

        qk_dram = [name(w).rearrange("(k p) n -> p k n", p=P) for w in ("wq", "wk")]
        v_dram = name("wv").rearrange("(k p) n -> p k n", p=P)
        o_dram = name("wo").rearrange("(h d) n -> d h n", d=K1)

        def score_item(j, h, front, back):
            if h < HG - 1:
                return (j - 1, h + 1) if back else None
            return (j, 0) if front else None

        with nc.Block() as block:
            @block.sync
            def _(sp):
                def group(g, first):
                    for h in range(HG):
                        if not (first and h < 2):
                            sp.wait_ge(wqk_ready, HG * g + h - 1)
                        for w in range(2):
                            sp.dma_start(stage_qk[:, h % 2, w, :, :],
                                         qk_dram[w][:, :, ds((HG * g + h) * K1, K1)]).then_inc(qk_in[h % 2], 16)
                    if not first:
                        sp.wait_ge(wo_ready, g)
                    sp.dma_start(stage_vo[:, :].rearrange("p (k n) -> p k n", k=KT),
                                 v_dram[:, :, ds(HG * K1 * g, HG * K1)]).then_inc(vo_in, 16)
                    sp.wait_ge(wv_ready, g + 1)
                    sp.dma_start(stage_vo[:, :].rearrange("p (h n) -> p h n", h=HG),
                                 o_dram[:, ds(HG * g, HG), :]).then_inc(vo_in, 16)
                group(0, True)
                with sp.Fori(1, NG) as g:
                    group(g, False)

            @block.gpsimd
            def _(pool):
                SPLITS = HG + 2

                def split(count, hi, lo, raw, ready):
                    pool.tensor_copy(hi, raw).then_inc(w_hi, 1)
                    pool.wait_ge(w_hi, count)
                    pool.tensor_tensor(lo, raw, hi.bitcast(F32), ALU.subtract).then_inc(ready, 1)

                def context_block(g, b, first):
                    if not (first and b == 0):
                        pool.wait_ge(v_psum, PPB * (NBLK * g + b))
                    pool.tensor_copy(cf_hi[:, :, :], G.ctx_hi[:, :, b * BLK:(b + 1) * BLK].bitcast(F32))
                    pool.tensor_copy(cf_lo[:, :, :], G.ctx_lo[:, :, b * BLK:(b + 1) * BLK].bitcast(F32)).then_inc(cf_ready, 1)

                def key_bias(g, b, first):
                    for h in range(HG):
                        pool.wait_ge(k_psum, HG * (NBLK * g + b) + h + 1)
                        pool.tensor_copy(k_sb[:, h, :, T:KP], G.cols[:, i - 1, ds(2 * H1 + HG * g + h, 1)]
                                         .unsqueeze(1).to_broadcast([P, 2 * PPB, 1])).then_inc(kb_ready, 1)

                def group(g, first):
                    for h in range(HG):
                        pool.wait_ge(qk_in[h % 2], 32 * (HG // 2 * g + h // 2 + 1))
                        if not first:
                            pool.wait_ge(k_psum, HG * NBLK * g - HG + h + 1)
                        split(SPLITS * g + h + 1, wqk_hi[:, h, :, :, :], wqk_lo[:, h, :, :, :],
                              stage_qk[:, h % 2, :, :, :], wqk_ready)
                    pool.wait_ge(vo_in, 32 * g + 16)
                    if not first:
                        pool.wait_ge(v_psum, PPB * NBLK * g)
                    split(SPLITS * g + HG + 1, wv_hi[:, :, :], wv_lo[:, :, :],
                          stage_vo[:, :].rearrange("p (k n) -> p k n", k=KT), wv_ready)
                    context_block(g, 0, first)
                    key_bias(g, 0, first)
                    context_block(g, 1, first)
                    pool.wait_ge(vo_in, 32 * g + 32)
                    if not first:
                        pool.wait_ge(o_psum, 2 * NBLK * g)
                    split(SPLITS * g + HG + 2, wo_hi[:, :, :], wo_lo[:, :, :],
                          stage_vo[:, :].rearrange("p (h n) -> p h n", h=HG), wo_ready)
                    key_bias(g, 1, first)
                    for b in (2, 3):
                        context_block(g, b, first)
                        key_bias(g, b, first)
                for g in range(NG):
                    group(g, g == 0)

            @block.tensor
            def _(pe):
                def body(j, front, back):
                    if front:
                        g, off = j // NBLK, (j % NBLK) * BLK
                    for h in range(HG):
                        item = score_item(j, h, front, back)
                        if item:
                            js, hs = item
                            n = HG * js + hs
                            pe.wait_ge(q_ready, n + 1)
                            pe.wait_ge(k_ready, n + 1)
                            pe.wait_ge(kb_ready, n + 1)
                            if back:
                                pe.wait_ge(shifted, 2 * n)
                            for p in range(PPB):
                                cols = slice(p * P, (p + 1) * P)
                                mm = pe.matmul(s_ps[:, p, 0:2 * KP], q_sb[:, hs, cols], k_sb[:, hs, 2 * p:2 * p + 2, :],
                                               start=True, stop=True)
                            mm.then_inc(s_psum, 1)
                        if back:
                            n = HG * (j - 1) + h
                            pe.wait_ge(prob_ready, 3 * n + 3)
                            pe.wait_ge(pt_ready, n + 1)
                            for p in range(PPB):
                                mm = pe.transpose(t_ps[:, p * P:(p + 1) * P], prob[:, p, :], G.ident[:, :])
                            mm.then_inc(t_psum, 1)
                        if front:
                            n = HG * j + h
                            pe.wait_ge(wqk_ready, HG * g + h + 1)
                            if back or h:
                                pe.wait_ge(q_ready, n)
                                pe.wait_ge(k_ready, n)
                            if back and h == 0:
                                for copied in v_ready:
                                    pe.wait_ge(copied, 2 * j)
                            for w, dst, x_hi, x_lo, done in ((0, q_ps, G.feat_hi, G.feat_lo, q_psum),
                                                             (1, k_ps, G.ctx_hi, G.ctx_lo, k_psum)):
                                for k in range(KT):
                                    prods = split_products(wqk_hi[:, h, w, k, :], wqk_lo[:, h, w, k, :],
                                                           x_hi[:, k, ds(off, BLK)], x_lo[:, k, ds(off, BLK)])
                                    for t, (a, b) in enumerate(prods):
                                        mm = pe.matmul(dst[:, :], a, b, start=(k == 0 and t == 0),
                                                       stop=(k == KT - 1 and t == 2))
                                mm.then_inc(done, 1)
                        if back:
                            n = HG * (j - 1) + h
                            pe.wait_ge(pt_ready, n + 2)
                            pe.wait_ge(ot_ready, n + 1)
                            for copied in v_ready:
                                pe.wait_ge(copied, 2 * j)
                            for p in range(PPB):
                                cols, head = slice(p * P, (p + 1) * P), slice(h * K1, (h + 1) * K1)
                                mm = pe.matmul(c_ps[:, cols], v_sb[:, p, head], pt[:, cols], start=True, stop=True)
                            mm.then_inc(c_psum, 1)
                    if front:
                        pe.wait_ge(wv_ready, g + 1)
                        pe.wait_ge(cf_ready, j + 1)
                        pe.wait_ge(q_ready, HG * j + HG)
                        pe.wait_ge(k_ready, HG * j + HG)
                        for p in range(PPB):
                            if p >= 2:
                                pe.wait_ge(v_ready[p % 2], 2 * j + 1)
                            for k in range(KT):
                                cols = slice(p * P, (p + 1) * P)
                                for t, (a, b) in enumerate(split_products(cf_hi[:, k, cols], cf_lo[:, k, cols],
                                                                          wv_hi[:, k, :], wv_lo[:, k, :])):
                                    mm = pe.matmul(v_ps[p % 2][:, :], a, b, start=(k == 0 and t == 0),
                                                   stop=(k == KT - 1 and t == 2))
                            mm.then_inc(v_psum, 1)
                    if back:
                        pe.wait_ge(ot_ready, HG * j + 1)
                        pe.wait_ge(wo_ready, (j - 1) // NBLK + 1)
                        pe.wait_ge(x_added, 2 * (j - 1) + 1)
                        for p in range(PPB):
                            cols = slice(p * P, (p + 1) * P)
                            for h in range(HG):
                                for t, (a, b) in enumerate(split_products(ot_hi[:, h, cols], ot_lo[:, h, cols],
                                                                          wo_hi[:, h, :], wo_lo[:, h, :])):
                                    mm = pe.matmul(o_ps[p // 2][:, p % 2, :], a, b, start=(h == 0 and t == 0),
                                                   stop=(h == HG - 1 and t == 2))
                            if p % 2:
                                mm.then_inc(o_psum, 1)
                skewed(pe, NI, body)

            @block.scalar
            def _(act):
                def body(j, front, back):
                    for h in range(HG):
                        if back:
                            n = HG * (j - 1) + h
                            act.wait_ge(t_psum, n + 1)
                            act.activation(pt[:, :], t_ps[:, :], ACT.Copy).then_inc(pt_ready, 1)
                        item = score_item(j, h, front, back)
                        if item:
                            n = HG * item[0] + item[1]
                            act.wait_ge(shifted, 2 * n + 2)
                            act.activation(soft[:, :, :], soft[:, :, :], ACT.Exp, scale=q_scale).then_inc(exp_done, 1)
                        if front:
                            n, head = HG * j + h, HG * (j // NBLK) + h
                            act.wait_ge(q_psum, n + 1)
                            act.activation(q_sb[:, h, :], q_ps[:, :], ACT.Identity,
                                           bias=G.cols[:, i - 1, ds(head, 1)]).then_inc(q_ready, 1)
                            act.wait_ge(k_psum, n + 1)
                            act.activation(k_sb[:, h, :, 0:T], k_ps[:, :].rearrange("p (b t) -> p b t", t=T), ACT.Identity,
                                           bias=G.cols[:, i - 1, ds(H1 + head, 1)]).then_inc(k_ready, 1)
                        if back:
                            act.wait_ge(c_psum, HG * (j - 1) + h + 1)
                            act.activation(ot_hi[:, h, :], c_ps[:, :], ACT.Copy).then_inc(ot_high, 1)
                    if front:
                        for p in (0, 2):
                            act.wait_ge(v_psum, PPB * j + p + 1)
                            act.activation(v_sb[:, p, :], v_ps[0][:, :], ACT.Copy).then_inc(v_ready[0], 1)
                skewed(act, NI, body)

            @block.vector
            def _(dve):
                dve.memset(prob[:, :, :], 0.0).then_inc(pt_ready, 1)
                dve.memset(G.bias_prob[:, :, H1:H1 + 1], 1.0).then_inc(ot_ready, 1)
                dve.memset(rmax[:, :], 0.0).then_inc(x_added, 1)
                dve.wait_ge(pt_ready, 1)
                dve.wait_ge(x_added, 1)
                halves = [slice(0, T), slice(T, 2 * T)]

                def body(j, front, back):
                    for h in range(HG):
                        item = score_item(j, h, front, back)
                        if item:
                            js, hs = item
                            n = HG * js + hs
                            dve.wait_ge(s_psum, n + 1)
                            for u, half in enumerate(halves):
                                dve.tensor_reduce(rmax[half, :], s_ps[half, :, u * KP:(u + 1) * KP], X_AXIS, ALU.max).then_inc(max_done, 1)
                            if back:
                                dve.wait_ge(prob_ready, 3 * n)
                            for u, half in enumerate(halves):
                                dve.wait_ge(max_done, 2 * n + u + 1)
                                dve.tensor_tensor(soft[half, :, :], s_ps[half, :, u * KP:(u + 1) * KP],
                                                  rmax[half, :].unsqueeze(2).to_broadcast([T, PPB, KP]), ALU.subtract).then_inc(shifted, 1)
                            dve.wait_ge(exp_done, n + 1)
                            dve.tensor_reduce(rsum[:, :], soft[:, :, :], X_AXIS, ALU.add).then_inc(sum_done, 1)
                            dve.wait_ge(sum_done, n + 1)
                            dve.reciprocal(rinv[:, :], rsum[:, :]).then_inc(inv_done, 1)
                            dve.wait_ge(inv_done, n + 1)
                            if back:
                                dve.wait_ge(t_psum, n)
                            for half in halves:
                                dve.tensor_tensor(prob[half, :, half], soft[half, :, 0:T],
                                                  rinv[half, :].unsqueeze(2).to_broadcast([T, PPB, T]), ALU.mult).then_inc(prob_ready, 1)
                            dve.tensor_tensor(G.bias_prob[:, ds(PPB * (js % NBLK), PPB), ds(HG * (js // NBLK) + hs, 1)],
                                              soft[:, :, T:KP], rinv[:, :].unsqueeze(2), ALU.mult).then_inc(prob_ready, 1)
                        if back:
                            dve.wait_ge(ot_high, HG * (j - 1) + h + 1)
                            dve.tensor_tensor(ot_lo[:, h, :], c_ps[:, :], ot_hi[:, h, :].bitcast(F32),
                                              ALU.subtract).then_inc(ot_ready, 1)
                    if front:
                        for p in (1, 3):
                            dve.wait_ge(v_psum, PPB * j + p + 1)
                            dve.tensor_copy(v_sb[:, p, :], v_ps[1][:, :]).then_inc(v_ready[1], 1)
                    if back:
                        for p in range(2):
                            dve.wait_ge(o_psum, 2 * (j - 1) + p + 1)
                            x = G.x_res[:, ds(PPB * ((j - 1) % NBLK) + 2 * p, 2), :]
                            dve.tensor_tensor(x, o_ps[p][:, :, :], x, ALU.add).then_inc(x_added, 1)
                skewed(dve, NI, body)


def phase_bias_token(nc, G, i):
    with Mem(nc, f"bt{i}", G.psum) as m:
        bp_t = [m.sb(f"bp_t{n}", [H1 + 1, P]) for n in range(2)]
        t_ps = [m.ps(f"t_ps{n}", (H1 + 1, P)) for n in range(2)]
        o_ps = [m.ps(f"o_ps{n}", (P, D)) for n in range(2)]
        t_psum, t_done, o_psum, x_done = (m.sem(n) for n in ("t_psum", "t_done", "o_psum", "x_done"))
        with nc.Block() as block:
            @block.tensor
            def _(pe):
                for p in range(PAIRS + 1):
                    if p < PAIRS:
                        if p >= 2:
                            pe.wait_ge(t_done, p - 1)
                        pe.transpose(t_ps[p % 2][:, :], G.bias_prob[:, p, :], G.ident[:, :]).then_inc(t_psum, 1)
                    if p:
                        pe.wait_ge(t_done, p)
                        if p >= 3:
                            pe.wait_ge(x_done, p - 2)
                        pe.matmul(o_ps[(p - 1) % 2][:, :], bp_t[(p - 1) % 2][:, :], G.bvo[:, i - 1, :], start=True, stop=True).then_inc(o_psum, 1)

            @block.scalar
            def _(act):
                for p in range(PAIRS):
                    act.wait_ge(t_psum, p + 1)
                    if p >= 2:
                        act.wait_ge(o_psum, p - 1)
                    act.activation(bp_t[p % 2][:, :], t_ps[p % 2][:, :], ACT.Copy).then_inc(t_done, 1)

            @block.vector
            def _(dve):
                for p in range(PAIRS):
                    dve.wait_ge(o_psum, p + 1)
                    dve.tensor_tensor(G.x_res[:, p, :], o_ps[p % 2][:, :], G.x_res[:, p, :], ALU.add).then_inc(x_done, 1)


def phase_mlp(nc, A, G, tag, feat_hi, feat_lo, w1_dram, b1_dram, w2_dram, b2_dram, func, join_context=False):
    LAG, RING = 2, 4
    with Mem(nc, tag, G.psum) as m:
        w1_raw, w2_raw = m.sb("w1_raw", [P, KT, FF]), m.sb("w2_raw", [P, FT, D])
        w1_hi, w1_lo = (m.sb(n, [P, KT, FF], F32R) for n in ("w1_hi", "w1_lo"))
        w2_hi, w2_lo = (m.sb(n, [P, FT, D], F32R) for n in ("w2_hi", "w2_lo"))
        b1_rows, b1 = m.sb("b1_rows", [FT, P]), m.sb("b1", [P, FT])
        b2 = m.sb("b2", [P, D])
        act_raw = [m.sb(f"act_raw{n}", [P, BLK]) for n in range(2)]
        act_hi = [m.sb(f"act_hi{n}", [P, BLK], F32R) for n in range(RING)]
        act_lo = [m.sb(f"act_lo{n}", [P, BLK], F32R) for n in range(RING)]
        hid_ps = [m.ps(f"hid_ps{n}", (P, BLK)) for n in range(RING)]
        out_ps = [m.ps(f"out_ps{n}", (P, D)) for n in range(PPB)]
        w1_in, w2_in, b1_in, b2_in = (m.sem(n) for n in ("w1_in", "w2_in", "b1_in", "b2_in"))
        b1_psum, b1_done, b2_added, w_hi, w_ready = (m.sem(n) for n in ("b1_psum", "b1_done", "b2_added", "w_hi", "w_ready"))
        hid_psum, raw_done, hi_done, act_ready, out_psum, x_done = (m.sem(n) for n in
            ("hid_psum", "raw_done", "hi_done", "act_ready", "out_psum", "x_done"))
        with nc.Block() as block:
            @block.sync
            def _(sp):
                sp.dma_start(b1_rows[:, :], b1_dram.rearrange("(f p) -> f p", p=P)).then_inc(b1_in, 16)
                sp.dma_start(w1_raw[:, :, :], w1_dram.rearrange("(k p) n -> p k n", p=P)).then_inc(w1_in, 16)
                sp.dma_start(w2_raw[:, :, :], w2_dram.rearrange("(f p) n -> p f n", p=P)).then_inc(w2_in, 16)
                sp.dma_start(b2[:, :], b2_dram.rearrange("(o n) -> o n", o=1).partition_broadcast(P)).then_inc(b2_in, 16)

            @block.gpsimd
            def _(pool):
                pool.wait_ge(b2_in, 16)
                for p in range(PAIRS):
                    pool.tensor_tensor(G.x_res[:, p, :], G.x_res[:, p, :], b2[:, :], ALU.add).then_inc(b2_added, 1)
                if join_context:
                    for k in range(KT):
                        for q in range(NBLK):
                            whole, hi, lo = (t[:, k, q * BLK:(q + 1) * BLK] for t in (G.ctx_f, G.ctx_hi, G.ctx_lo))
                            pool.tensor_tensor(whole, hi.bitcast(F32), lo.bitcast(F32), ALU.add)

            @block.tensor
            def _(pe):
                pe.wait_ge(b1_in, 16)
                pe.transpose(hid_ps[0][:, 0:FT], b1_rows[:, :], G.ident[0:FT, 0:FT]).then_inc(b1_psum, 1)
                pe.wait_ge(b1_done, 1)

                def up(j, f, first):
                    n = FT * j + f
                    if first:
                        pe.wait_ge(w_ready, min(f, 1) + 1)
                    if not first or f >= RING:
                        pe.wait_ge(raw_done, n - RING + 1)
                    for k in range(KT):
                        cols = slice(f * P, (f + 1) * P)
                        for t, (a, b) in enumerate(split_products(w1_hi[:, k, cols], w1_lo[:, k, cols],
                                                                  feat_hi[:, k, ds(j * BLK, BLK)],
                                                                  feat_lo[:, k, ds(j * BLK, BLK)])):
                            mm = pe.matmul(hid_ps[f % RING][:, :], a, b, start=(k == 0 and t == 0),
                                           stop=(k == KT - 1 and t == 2))
                    mm.then_inc(hid_psum, 1)

                def down(j, f, first):
                    pe.wait_ge(act_ready, FT * j + f + 1)
                    for p in range(PPB):
                        if f == 0 and not first:
                            pe.wait_ge(x_done, PPB * (j - 1) + p + 1)
                        cols = slice(p * P, (p + 1) * P)
                        for t, (a, b) in enumerate(split_products(act_hi[f % RING][:, cols], act_lo[f % RING][:, cols],
                                                                  w2_hi[:, f, :], w2_lo[:, f, :])):
                            mm = pe.matmul(out_ps[p][:, :], a, b, start=(f == 0 and t == 0), stop=(f == FT - 1 and t == 2))
                        if f == FT - 1:
                            mm.then_inc(out_psum, 1)

                def block_of_tokens(j, first):
                    for f in range(FT):
                        up(j, f, first)
                        if f >= LAG:
                            down(j, f - LAG, first)
                    for f in range(FT - LAG, FT):
                        down(j, f, first)
                block_of_tokens(0, True)
                with pe.Fori(1, NBLK) as j:
                    block_of_tokens(j, False)

            @block.scalar
            def _(act):
                act.wait_ge(b1_psum, 1)
                act.activation(b1[:, :], hid_ps[0][:, 0:FT], ACT.Copy).then_inc(b1_done, 1)
                act.wait_ge(b1_done, 1)

                def block_of_tokens(j, first):
                    for f in range(FT):
                        n = FT * j + f
                        act.wait_ge(hid_psum, n + 1)
                        if not first or f >= 2:
                            act.wait_ge(act_ready, n - 1)
                        act.activation(act_raw[f % 2][:, :], hid_ps[f % RING][:, :], func, bias=b1[:, f:f + 1]).then_inc(raw_done, 1)
                block_of_tokens(0, True)
                with act.Fori(1, NBLK) as j:
                    block_of_tokens(j, False)

            @block.vector
            def _(dve):
                for n, (got, raw, hi, lo) in enumerate(((w1_in, w1_raw, w1_hi, w1_lo), (w2_in, w2_raw, w2_hi, w2_lo))):
                    dve.wait_ge(got, 16)
                    dve.tensor_copy(hi[:, :, :], raw[:, :, :]).then_inc(w_hi, 1)
                    dve.wait_ge(w_hi, n + 1)
                    dve.tensor_tensor(lo[:, :, :], raw[:, :, :], hi[:, :, :].bitcast(F32), ALU.subtract).then_inc(w_ready, 1)

                def block_of_tokens(j, first):
                    for f in range(FT):
                        n = FT * j + f
                        dve.wait_ge(raw_done, n + 1)
                        dve.tensor_copy(act_hi[f % RING][:, :], act_raw[f % 2][:, :]).then_inc(hi_done, 1)
                        dve.wait_ge(hi_done, n + 1)
                        dve.tensor_tensor(act_lo[f % RING][:, :], act_raw[f % 2][:, :], act_hi[f % RING][:, :].bitcast(F32),
                                          ALU.subtract).then_inc(act_ready, 1)
                    if first:
                        dve.wait_ge(b2_added, PAIRS)
                    for p in range(PPB):
                        dve.wait_ge(out_psum, PPB * j + p + 1)
                        x = G.x_res[:, ds(PPB * j + p, 1), :]
                        dve.tensor_tensor(x, out_ps[p][:, :], x, ALU.add).then_inc(x_done, 1)
                block_of_tokens(0, True)
                with dve.Fori(1, NBLK) as j:
                    block_of_tokens(j, False)


UNITS = 4


def wait(eng, sem, value):
    if not (isinstance(value, int) and value <= 0):
        eng.wait_ge(sem, value)


MAKE_V, SCORE, EXP, NORMALIZE, TURN, VALUES, OUTPUT, ADD = 2, 2, 3, 4, 5, 6, 7, 8


def unit_slots(j, front, back):
    for slot in range(2 * UNITS):
        def at(lag, slot=slot):
            ahead, t = divmod(slot - lag, UNITS)
            return (2 * j + ahead, t, ahead % 2) if (front if ahead >= 0 else back) else None
        yield slot % UNITS, at


def phase_narrow_attention(nc, A, G, layer, dst):
    two = layer == 2
    GR, NK = (8, 64) if two else (4, 128)
    HD = 8 if two else 16
    score_scale = float(HD) ** -0.5 if two else 1.0 / HD
    dropped = -1e30
    VR = 64 if two else P
    SKEW = 80 if two else 160
    with Mem(nc, f"l{layer}", G.psum) as m:
        wq_raw = m.sb("wq_raw", [P, KT, D])
        kv_cols = 64 if two else D
        wkv_raw = m.sb("wkv_raw", [P, KT, 2, kv_cols] if two else [P, KT, 2 * D])
        KC = P if two else D
        wq = m.sb("wq", [P, KT, D]) if two else wq_raw
        wk = m.sb("wk", [P, KT, KC])
        wv = m.sb("wv", [P, KT, kv_cols])
        wo = m.sb("wo", [P, KT, D])
        rows = m.sb("rows", [8, P])
        cols = m.sb("cols", [P, 8])
        o_bias = m.sb("o_bias", [P, D])
        mask = m.sb("mask", [P, B, NK])
        mask_int = None if two else m.sb("mask_int", [P, B * T], I32)
        spread = m.sb("spread", [P, 8])
        odd_even = m.sb("odd_even", [P, 2])
        q_bd = [m.sb(f"q_bd{n}", [P, 2, 2, P] if two else [P, 2, 2, 8 * T]) for n in range(2)]
        k_bd = [m.sb(f"k_bd{n}", [P, 8, P] if two else [P, 2, 2 * P]) for n in range(2)]
        v_bd = [m.sb(f"v_bd{n}", [P, 2, 4 * SKEW] if two else [P, 2, 2, 4 * SKEW]) for n in range(2)]
        vx = m.sb("vx", [P, KT, 2, 2, T])
        soft = [m.sb(f"soft{n}", [P, GR, NK]) for n in range(UNITS)]
        prob = [m.sb(f"prob{n}", [P, GR, NK]) for n in range(2)]
        pt = [m.sb(f"pt{n}", [P, 4, P]) for n in range(2)]
        ot = m.sb("ot", [P, 2, P])
        even_part = m.sb("even_part", [P, T])
        rmax, rsum, rinv = ([m.sb(f"{n}{r}", [P, GR]) for r in range(2)] for n in ("rmax", "rsum", "rinv"))
        s_ps = [m.ps(f"s_ps{n}") for n in range(2)]
        t_ps, c_ps, o_ps = m.ps("t_ps"), m.ps("c_ps", (P, P)), m.ps("o_ps", (P, D))
        q_ps = m.ps("q_ps", (P, 2, P))
        k_ps = m.ps("k_ps", (P, P) if two else (P, 2, 2, P))
        v_ps = m.ps("v_ps", (P, 2, kv_cols))
        w_in, row_in, mask_in, o_bias_in, spread_made, rows_zero, q_zero, v_zero = (m.sem(n) for n in
            ("w_in", "row_in", "mask_in", "o_bias_in", "spread_made", "rows_zero", "q_zero", "v_zero"))
        w_ready, cols_psum, cols_done, mask_done, o_bias_added = (m.sem(n) for n in
            ("w_ready", "cols_psum", "cols_done", "mask_done", "o_bias_added"))
        vx_ready, q_psum, k_psum, v_psum, q_done, k_done, v_done = (m.sem(n) for n in
            ("vx_ready", "q_psum", "k_psum", "v_psum", "q_done", "k_done", "v_done"))
        s_psum, masked, max_done, shifted, exp_done, sum_done, inv_done, prob_ready = (m.sem(n) for n in
            ("s_psum", "masked", "max_done", "shifted", "exp_done", "sum_done", "inv_done", "prob_ready"))
        t_psum, pt_done, c_psum, even_done, ot_done, o_psum, x_done = (m.sem(n) for n in
            ("t_psum", "pt_done", "c_psum", "even_done", "ot_done", "o_psum", "x_done"))
        STEPS = PAIRS // 2
        if two:
            name = lambda n: A[f"L2_xattn_{n}"]
            w_loads = [(wq_raw[:, :, :], name("Wq").rearrange("(k p) n -> p k n", p=P)),
                       (wkv_raw[:, :, 0, :], name("Wk").rearrange("(k p) n -> p k n", p=P)),
                       (wkv_raw[:, :, 1, :], name("Wv").rearrange("(k p) n -> p k n", p=P))] + \
                      [(wo[64 * g + 8 * v:64 * g + 8 * v + 8, :, :],
                        name("Wo")[32 * v:32 * v + 32, :].rearrange("(c g d) n -> g d c n", c=2, g=2)[g]) for v in range(8) for g in range(2)]
            q_bias = name("bq").rearrange("(v c g d) -> c g v d", v=8, c=2, g=2)
            row_loads = [(rows[c:c + 1, 64 * g:64 * g + 64].rearrange("o (v d) -> o v d", d=8), q_bias[c:c + 1, g]) for c in range(2) for g in range(2)] + \
                        [(rows[r:r + 1, 64 * g:64 * g + 64], name(n).rearrange("(o n) -> o n", o=1)) for r, n in ((2, "bk"), (4, "bv")) for g in range(2)]
            o_bias_dram = name("bo")
            mask_dram = A["mask_Bx1xSxS2_ff0"].rearrange("b o q t -> q (b o) t")
            mask_loads = [(mask[64 * g:64 * g + 64, :, :], mask_dram) for g in range(2)]
        else:
            name = lambda n: A[f"L3_xattn_{n}"]
            w_loads = [(wq_raw[:, :, :], name("q_w").rearrange("(k p) n -> p k n", p=P)),
                       (wkv_raw[:, :, :], name("kv_w").rearrange("(k p) n -> p k n", p=P)),
                       (wo[:, :, :], name("out_w").rearrange("(k p) n -> p k n", p=P))]
            kv_bias = name("kv_b").rearrange("(c p w) -> w c p", c=2, w=2)
            row_loads = [(rows[0:2, :], name("q_b").rearrange("(c p) -> c p", p=P)),
                         (rows[2:4, :], kv_bias[0]), (rows[4:6, :], kv_bias[1])]
            o_bias_dram = name("out_b")
            mask_loads = [(mask_int[:, :], A["mask_BxS2_ik0"].rearrange("(o b) t -> o (b t)", o=1).partition_broadcast(P))]

        def number(unit):
            return UNITS * unit[0] + unit[1]

        with nc.Block() as block:
            @block.sync
            def _(sp):
                sp.dma_start(o_bias[:, :], o_bias_dram.rearrange("(o n) -> o n", o=1).partition_broadcast(P)).then_inc(o_bias_in, 16)
                for dst_, src in w_loads:
                    sp.dma_start(dst_, src).then_inc(w_in, 16)
                sp.wait_ge(rows_zero, 1)
                with nc.allow_non_contiguous_dma(reason="biases of interleaved keys and values: 512 words"):
                    for dst_, src in row_loads:
                        sp.dma_start(dst_, src).then_inc(row_in, 16)
                for dst_, src in mask_loads:
                    sp.dma_start(dst_, src).then_inc(mask_in, 16)

            @block.gpsimd
            def _(pool):
                pool.memset(spread[:, :], 1.0).then_inc(spread_made, 1)
                n = 1
                for base, width in ((0, 8 * HD), (64, 64))[:2 if two else 1]:
                    for cm, b0, pat in ((1, -base, -HD), (-1, base + HD - 1, HD)):
                        pool.wait_ge(spread_made, n)
                        rows_ = slice(base, base + (64 if two else P))
                        pool.affine_select(out=spread[rows_, :], in_=spread[rows_, :], compare_op=ALU.is_ge, fill=0.0,
                                           base=b0 + cm * base, pattern=[[pat, 8]], channel_multiplier=cm).then_inc(spread_made, 1)
                        n += 1
                pool.wait_ge(spread_made, n)
                for n in range(2):
                    pool.memset(v_bd[n][:, :, :] if two else v_bd[n][:, :, :, :], 0.0).then_inc(v_zero, 1)

                def body(j, front, back):
                    for i, at in unit_slots(j, front, back):
                        if at(NORMALIZE):
                            n, t = number(at(NORMALIZE)), at(NORMALIZE)[1]
                            pool.wait_ge(inv_done, n + 1)
                            wait(pool, t_psum, n - 1)
                            pool.tensor_tensor(prob[t % 2][:, :, :], soft[t][:, :, :],
                                               rinv[t % 2][:, :].unsqueeze(2).to_broadcast([P, GR, NK]), ALU.mult).then_inc(prob_ready, 1)
                        if at(SCORE):
                            n, t = number(at(SCORE)), at(SCORE)[1]
                            pool.wait_ge(max_done, n + 1)
                            pool.tensor_tensor(soft[t][:, :, :], soft[t][:, :, :],
                                               rmax[t % 2][:, :].unsqueeze(2).to_broadcast([P, GR, NK]), ALU.subtract).then_inc(shifted, 1)
                skewed(pool, STEPS, body)

            @block.tensor
            def _(pe):
                pe.wait_ge(row_in, 16 * len(row_loads))
                pe.transpose(c_ps[:, 0:8], rows[:, :], G.ident[0:8, 0:8]).then_inc(cols_psum, 1)
                pe.wait_ge(cols_done, 1)
                pe.wait_ge(w_ready, 1)

                def accumulate(out, products):
                    for n, (a, b) in enumerate(products):
                        mm = pe.matmul(out, a, b, start=(n == 0), stop=(n == len(products) - 1))
                    return mm

                def body(j, front, back):
                    for i, at in unit_slots(j, front, back):
                        if at(TURN):
                            n, t = number(at(TURN)), at(TURN)[1]
                            pe.wait_ge(prob_ready, n + 1)
                            wait(pe, pt_done, n)
                            for q in range(4):
                                mm = pe.transpose(t_ps[:, q * P:(q + 1) * P],
                                                  prob[t % 2][:, :, :].rearrange("p g t -> p (g t)")[:, q * P:(q + 1) * P], G.ident[:, :])
                            mm.then_inc(t_psum, 1)
                        if at(SCORE):
                            pair, t, par = at(SCORE)
                            n, b, c = UNITS * pair + t, t // 2, t % 2
                            pe.wait_ge(q_done, pair + 1)
                            pe.wait_ge(k_done, pair + 1)
                            wait(pe, masked, n - 1)
                            out = s_ps[t % 2]
                            if two:
                                mm = accumulate(out[:, :], [(q_bd[par][:, c, b, :], k_bd[par][:, :, b * T:(b + 1) * T])])
                            else:
                                for h2 in range(4):
                                    mm = accumulate(out[:, h2 * P:(h2 + 1) * P],
                                                    [(q_bd[par][:, c, b, h2 * P:(h2 + 1) * P], k_bd[par][:, c, b * P:(b + 1) * P])])
                            mm.then_inc(s_psum, 1)
                        if i == 0 and at(0):
                            pair = at(0)[0]
                            x_new, ctx = (t[:, :, ds(pair * P, P)] for t in (G.feat_f, G.ctx_f))
                            wait(pe, q_done, pair)
                            for c in range(2):
                                mm = accumulate(q_ps[:, c, :], [(wq[:, k, c * P:(c + 1) * P], x_new[:, k]) for k in range(KT)])
                            mm.then_inc(q_psum, 1)
                            wait(pe, k_done, pair)
                            if two:
                                mm = accumulate(k_ps[:, :], [(wk[:, k, :], ctx[:, k]) for k in range(KT)])
                            else:
                                for c in range(2):
                                    for s, tokens in enumerate((ctx, x_new)):
                                        mm = accumulate(k_ps[:, c, :, s * T:(s + 1) * T],
                                                        [(wk[:, k, c * P:(c + 1) * P], tokens[:, k]) for k in range(KT)])
                            mm.then_inc(k_psum, 1)
                        if i == MAKE_V and at(MAKE_V):
                            pair = at(MAKE_V)[0]
                            pe.wait_ge(vx_ready, pair + 1)
                            wait(pe, v_done, pair)
                            for b in range(2):
                                mm = accumulate(v_ps[:, b, :], [(vx[:, k, b, :, :], wv[:, k, :]) for k in range(KT)])
                            mm.then_inc(v_psum, 1)
                        if at(OUTPUT) and at(OUTPUT)[1] == UNITS - 1:
                            pair = at(OUTPUT)[0]
                            pe.wait_ge(ot_done, UNITS * (pair + 1))
                            wait(pe, x_done, pair)
                            accumulate(o_ps[:, :], [(ot[:, c, :], wo[:, c, :]) for c in range(KT)]).then_inc(o_psum, 1)
                        if at(VALUES):
                            pair, t, par = at(VALUES)
                            n, b, c = UNITS * pair + t, t // 2, t % 2
                            pe.wait_ge(pt_done, n + 1)
                            pe.wait_ge(v_done, pair + 1)
                            wait(pe, ot_done, n)
                            v = v_bd[par][:, b, :] if two else v_bd[par][:, b, c, :]
                            accumulate(c_ps[0:VR, :], [(v[:, VR * q:VR * (q + 1)], pt[t % 2][:, q, :]) for q in range(4)]).then_inc(c_psum, 1)
                skewed(pe, STEPS, body)

            @block.scalar
            def _(act):
                act.wait_ge(cols_psum, 1)
                act.activation(cols[:, :], c_ps[:, 0:8], ACT.Copy).then_inc(cols_done, 1)
                act.wait_ge(cols_done, 1)
                if two:
                    act.wait_ge(q_zero, 2)
                act.wait_ge(v_zero, 2)
                halves = [slice(0, 64), slice(64, P)]

                def body(j, front, back):
                    for i, at in unit_slots(j, front, back):
                        if at(EXP):
                            act.wait_ge(shifted, number(at(EXP)) + 1)
                            tile = soft[at(EXP)[1]]
                            act.activation(tile[:, :, :], tile[:, :, :], ACT.Exp).then_inc(exp_done, 1)
                        if at(TURN):
                            act.wait_ge(t_psum, number(at(TURN)) + 1)
                            act.activation(pt[at(TURN)[1] % 2][:, :, :].rearrange("p q n -> p (q n)"), t_ps[:, :], ACT.Copy).then_inc(pt_done, 1)
                        prep, half = (at(0)[0], at(0)[2]) if at(0) else (None, None)
                        if prep is not None and i == 0 and two:
                            act.wait_ge(q_psum, prep + 1)
                            for c in range(2):
                                for h in halves:
                                    a = act.activation(q_bd[half][h, c, :, h], q_ps[h, c, :].rearrange("p (b q) -> p b q", b=2),
                                                       ACT.Identity, bias=cols[h, c:c + 1])
                            a.then_inc(q_done, 1)
                        if prep is not None and i == 0 and not two:
                            act.wait_ge(k_psum, prep + 1)
                            for c in range(2):
                                a = act.activation(k_bd[half][:, c, :], k_ps[:, c, :, :].rearrange("p b t -> p (b t)"),
                                                   ACT.Identity, bias=cols[:, 2 + c:3 + c])
                            a.then_inc(k_done, 1)
                        if prep is not None and i == MAKE_V:
                            act.wait_ge(v_psum, prep + 1)
                            for n in range(2):
                                if two:
                                    a = act.activation(
                                        v_bd[half][halves[n], :, :].rearrange("p b (q x) -> p b q x", x=SKEW)[:, :, :, 8 * n:8 * n + 8],
                                        v_ps[halves[n], :, :].rearrange("p b (q u d) -> p b q u d", q=4, u=2)[:, :, :, n, :], ACT.Copy)
                                else:
                                    a = act.activation(
                                        v_bd[half][:, n, :, :].rearrange("p c (h x) -> p c h x", x=SKEW)[:, :, :, 0:2 * HD],
                                        v_ps[:, n, :].rearrange("p (c h x) -> p c h x", c=2, h=4), ACT.Copy)
                            a.then_inc(v_done, 1)
                        if at(VALUES):
                            n, b, c = number(at(VALUES)), at(VALUES)[1] // 2, at(VALUES)[1] % 2
                            act.wait_ge(c_psum, n + 1)
                            if two:
                                for g, h in enumerate(halves):
                                    a = act.activation(ot[h, c, b * T:(b + 1) * T], c_ps[0:VR, g * T:(g + 1) * T],
                                                       ACT.Identity, bias=cols[0:VR, 4:5])
                                a.then_inc(ot_done, 1)
                            else:
                                act.activation(even_part[:, :], c_ps[:, 0:T], ACT.Identity, bias=cols[:, 4 + c:5 + c],
                                               scale=odd_even[:, 0:1]).then_inc(even_done, 1)
                skewed(act, STEPS, body)

            @block.vector
            def _(dve):
                dve.memset(rows[:, :], 0.0).then_inc(rows_zero, 1)
                if two:
                    for n in range(2):
                        dve.memset(q_bd[n][:, :, :, :], 0.0).then_inc(q_zero, 1)
                dve.wait_ge(o_bias_in, 16)
                for p in range(PAIRS):
                    dve.tensor_tensor(G.x_res[:, p, :] if two else dst[:, p, :], G.x_res[:, p, :], o_bias[:, :], ALU.add).then_inc(o_bias_added, 1)
                dve.wait_ge(w_in, 16 * len(w_loads))
                for k in range(KT):
                    if two:
                        keys = wkv_raw[:, k, 0, :].unsqueeze(1).to_broadcast([P, 2, 64])
                        values = wkv_raw[:, k, 1, :]
                        dve.tensor_copy(wk[:, k, :].rearrange("p (g c) -> p g c", g=2), keys)
                        dve.tensor_copy(wq[:, k, :].rearrange("p (g v d) -> p g v d", g=4, v=8),
                                        wq_raw[:, k, :].rearrange("p (v g d) -> p g v d", v=8, g=4))
                    else:
                        kv = wkv_raw[:, k, :].rearrange("p (c w) -> p w c", w=2)
                        values = kv[:, 1, :]
                        dve.tensor_copy(wk[:, k, :], kv[:, 0, :])
                    w = dve.tensor_copy(wv[:, k, :], values)
                w.then_inc(w_ready, 1)
                if not two:
                    dve.wait_ge(spread_made, 3)
                    dve.tensor_reduce(odd_even[:, :], spread[:, :].rearrange("p (h e) -> p e h", e=2), X_AXIS, ALU.add).then_inc(mask_done, 1)
                    dve.memset(mask[:, :, T:2 * T], 0.0)
                dve.wait_ge(mask_in, 16 * len(mask_loads))
                if not two:
                    dve.tensor_scalar(mask[:, :, 0:T], mask_int[:, :].rearrange("p (b t) -> p b t", b=B), 0, dropped,
                                      ALU.is_equal, ALU.mult).then_inc(mask_done, 1)
                    dve.wait_ge(mask_done, 2)
                dve.wait_ge(o_bias_added, PAIRS)
                dve.wait_ge(spread_made, 5 if two else 3)
                dve.wait_ge(cols_done, 1)

                def make_vx(prep):
                    wait(dve, v_psum, prep)
                    for k in range(KT):
                        for s, src in enumerate((G.ctx_f, G.ctx_f if two else G.feat_f)):
                            v = dve.tensor_copy(vx[:, k, :, s, :],
                                                src[:, k, ds(prep * P, P)].rearrange("p (b t) -> p b t", b=2))
                    v.then_inc(vx_ready, 1)

                def add_output(pair):
                    dve.wait_ge(o_psum, pair + 1)
                    x = (G.x_res if two else dst)[:, ds(pair, 1), :]
                    dve.tensor_tensor(x, o_ps[:, :], x, ALU.add).then_inc(x_done, 1)

                def body(j, front, back):
                    for i, at in unit_slots(j, front, back):
                        prep, half = (at(0)[0], at(0)[2]) if at(0) else (None, None)
                        if at(NORMALIZE):
                            n, t = number(at(NORMALIZE)), at(NORMALIZE)[1]
                            dve.wait_ge(exp_done, n + 1)
                            dve.tensor_reduce(rsum[t % 2][:, :], soft[t][:, :, :], X_AXIS, ALU.add).then_inc(sum_done, 1)
                            dve.wait_ge(sum_done, n + 1)
                            wait(dve, prob_ready, n - 1)
                            dve.reciprocal(rinv[t % 2][:, :], rsum[t % 2][:, :]).then_inc(inv_done, 1)
                        if prep is not None and i == 0:
                            make_vx(prep)
                        if at(SCORE):
                            pair, t, _ = at(SCORE)
                            n, b = UNITS * pair + t, t // 2
                            s3 = s_ps[t % 2][:, :].rearrange("p (g t) -> p g t", g=GR)
                            dve.wait_ge(s_psum, n + 1)
                            wait(dve, prob_ready, n - 3)
                            dve.scalar_tensor_tensor(soft[t][:, :, :], s3, score_scale,
                                                     mask[:, ds(2 * pair + b, 1), :].to_broadcast([P, GR, NK]),
                                                     ALU.mult, ALU.add).then_inc(masked, 1)
                            dve.wait_ge(masked, n + 1)
                            wait(dve, shifted, n - 1)
                            dve.tensor_reduce(rmax[t % 2][:, :], soft[t][:, :, :], X_AXIS, ALU.max).then_inc(max_done, 1)
                        if prep is not None and i == 0:
                            if two:
                                dve.wait_ge(k_psum, prep + 1)
                                dve.scalar_tensor_tensor(k_bd[half][:, :, :], k_ps[:, :].unsqueeze(1).to_broadcast([P, 8, P]),
                                                         cols[:, 2:3], spread[:, :].unsqueeze(2).to_broadcast([P, 8, P]),
                                                         ALU.add, ALU.mult).then_inc(k_done, 1)
                            else:
                                dve.wait_ge(q_psum, prep + 1)
                                for c in range(2):
                                    for b in range(2):
                                        q = dve.scalar_tensor_tensor(
                                            q_bd[half][:, c, b, :].rearrange("p (h t) -> p h t", h=8),
                                            q_ps[:, c, b * T:(b + 1) * T].unsqueeze(1).to_broadcast([P, 8, T]),
                                            cols[:, c:c + 1], spread[:, :].unsqueeze(2).to_broadcast([P, 8, T]),
                                            ALU.add, ALU.mult)
                                q.then_inc(q_done, 1)
                        if at(ADD) and at(ADD)[1] == UNITS - 1:
                            add_output(at(ADD)[0])
                        if at(VALUES) and not two:
                            n, b, c = number(at(VALUES)), at(VALUES)[1] // 2, at(VALUES)[1] % 2
                            dve.wait_ge(even_done, n + 1)
                            dve.scalar_tensor_tensor(ot[:, c, b * T:(b + 1) * T], c_ps[:, T:2 * T], odd_even[:, 1:2],
                                                     even_part[:, :], ALU.mult, ALU.add).then_inc(ot_done, 1)
                skewed(dve, STEPS, body)


class Global:
    pass


def build(nc, A, out, stage="L3"):
    G = Global()
    with Mem(nc, "g") as m:
        G.psum = m.stack.enter_context(nc.psum_tensor("psum", [P, PSUM_BANKS * BANK], F32))
        G.x_res = m.sb("x_res", [P, PAIRS, D])
        G.ctx_hi = m.sb("ctx_hi", [P, KT, TOK], F32R)
        G.ctx_lo = m.sb("ctx_lo", [P, KT, TOK], F32R)
        G.ident = m.sb("ident", [P, P])
        G.minus_half = m.sb("minus_half", [P, 2 * PAIRS])
        with Mem(nc, "c") as mc:
            G.ctx_tok = mc.sb("ctx_tok", [P, PAIRS, D])
            phase_setup(nc, A, G)
            phase_layer0(nc, A, G)
        if stage == "L0":
            return phase_store(nc, G.x_res, out)
        with Mem(nc, "one") as m1:
            G.cols = m1.sb("cols", [P, 2, 5 * H1])
            G.bvo = m1.sb("bvo", [H1 + 1, 2, D])
            G.bias_prob = m1.sb("bias_prob", [P, PAIRS, H1 + 1])
            G.feat_hi = m1.sb("feat_hi", [P, KT, TOK], F32R)
            G.feat_lo = m1.sb("feat_lo", [P, KT, TOK], F32R)
            phase_layer1_constants(nc, A, G)
            for i in (1, 2):
                phase_features(nc, G, f"ln{i}", G.x_res, G.feat_hi, G.feat_lo, "ln", 1e-5,
                               A[f"L1_xattn_ln{i}_scale"], A[f"L1_xattn_ln{i}_offset"])
                phase_layer1_attention(nc, A, G, i)
                if stage == f"A{i}p":
                    return phase_store(nc, G.x_res, out)
                phase_bias_token(nc, G, i)
                if stage == f"A{i}":
                    return phase_store(nc, G.x_res, out)
        with Mem(nc, "rest") as m2:
            G.ctx_f = m2.sb("ctx_f", [P, KT, TOK])
            with Mem(nc, "two") as m3:
                feat = [m3.sb(n, [P, KT, TOK], F32R) for n in ("feat_hi", "feat_lo")]
                phase_features(nc, G, "ln3", G.x_res, *feat, "ln", 1e-5,
                               A["L1_xattn_ln_mlp_scale"], A["L1_xattn_ln_mlp_offset"])
                phase_mlp(nc, A, G, "mlp1", *feat, *(A[f"L1_xattn_{n}"] for n in ("w_fc1", "b_fc1", "w_fc2", "b_fc2")), ACT.Gelu,
                          join_context=True)
            if stage == "M1":
                return phase_store(nc, G.x_res, out)
            attn_out = m2.sb("attn_out", [P, PAIRS, D])
            with Mem(nc, "narrow") as m3:
                G.feat_f = m3.sb("feat_f", [P, KT, TOK])
                phase_features(nc, G, "ft2", G.x_res, G.feat_f, None, "plain")
                phase_narrow_attention(nc, A, G, 2, G.x_res)
                phase_features(nc, G, "ln4", G.x_res, G.feat_f, None, "ln", 1e-6,
                               A["L2_xattn_gamma"], A["L2_xattn_beta"], update=True)
                if stage == "L2":
                    return phase_store(nc, G.x_res, out)
                phase_narrow_attention(nc, A, G, 3, attn_out)
            with Mem(nc, "three") as m3:
                feat = [m3.sb(n, [P, KT, TOK], F32R) for n in ("feat_hi", "feat_lo")]
                phase_features(nc, G, "rms", attn_out, *feat, "rms", 1e-6, A["L3_xattn_postnorm_w"])
                phase_mlp(nc, A, G, "mlp3", *feat, *(A[f"L3_xattn_{n}"] for n in ("mlp_w1", "mlp_b1", "mlp_w2", "mlp_b2")),
                          ACT.Gelu_apprx_tanh)
        phase_store(nc, G.x_res, out)


def phase_store(nc, src, out):
    with Mem(nc, "st") as m:
        stored = m.sem("stored")
        with nc.Block() as block:
            @block.sync
            def _(sp):
                sp.dma_start(out.rearrange("(p b) t d -> (b t) p d", b=2), src[:, :, :]).then_inc(stored, 16)
                sp.wait_ge(stored, 16)


def kernel(**inputs):
    import numpy as _np
    import concourse.bacc as _bacc
    from concourse import mybir as _mybir
    from concourse.bass_utils import run_bass_kernel_spmd as _run

    nc = _bacc.Bacc("TRN2", target_bir_lowering=False, num_devices=1)
    arrays, args = {}, {}
    for name, value in inputs.items():
        a = _np.ascontiguousarray(value)
        arrays[f"in_{name}"] = a
        args[name] = nc.dram_tensor(f"in_{name}", a.shape, _mybir.dt.from_np(a.dtype), kind="ExternalInput").ap()
    out = nc.dram_tensor("out_0", (B, T, D), F32, kind="ExternalOutput").ap()
    build(nc, args, out)
    r = _run(nc, [arrays], core_ids=[0])
    return r.results[0]["out_0"]
```

```python
import concourse.bass as bass
from concourse import mybir
from contextlib import ExitStack
import numpy as np

F32 = mybir.dt.float32
F32R = mybir.dt.float32r
I32 = mybir.dt.int32
ALU = mybir.AluOpType
ACT = mybir.ActivationFunctionType
X_AXIS = mybir.AxisListType.X

B, T, D = 32, 64, 256
P = 128
PAIRS = B * T // P
KT = D // P
TOK = B * T
BLK = 512
NBLK = TOK // BLK
PPB = BLK // P
H1, K1 = 16, 128
HG = 4
NG = H1 // HG
FF = 1024
FT = FF // P
BANK, PSUM_BANKS = 512, 8
ds = bass.ds


class Mem:

    def __init__(self, nc, tag, psum=None):
        self.nc, self.tag, self.psum, self.stack, self.banks, self.sems = nc, tag, psum, ExitStack(), 0, []

    def __enter__(self):
        self.stack.__enter__()
        return self

    def __exit__(self, *a):
        numbers = sorted(s.num for s in self.sems)
        while numbers:
            run = [n for i, n in enumerate(numbers) if n == numbers[0] + i]
            self.nc.sync.sem_clear(range(run[0], run[-1] + 1))
            numbers = numbers[len(run):]
        return self.stack.__exit__(*a)

    def sb(self, name, shape, dt=F32):
        return self.stack.enter_context(self.nc.sbuf_tensor(f"{self.tag}_{name}", shape, dt))

    def ps(self, name, shape=(P, 512)):
        size, at = int(np.prod(shape[1:])), self.banks * BANK
        self.banks += -(-size // BANK)
        assert self.banks <= PSUM_BANKS, name
        view = self.psum[0:shape[0], at:at + size]
        dims = " ".join(f"d{n}" for n in range(len(shape) - 1))
        sizes = {f"d{n}": s for n, s in enumerate(shape[1:])}
        return view.rearrange(f"p ({dims}) -> p {dims}", **sizes) if len(shape) > 2 else view

    def sem(self, name):
        self.sems.append(self.stack.enter_context(self.nc.semaphore(f"{self.tag}_{name}")))
        return self.sems[-1]


def split_products(lhs_hi, lhs_lo, rhs_hi, rhs_lo):
    return [(lhs_hi, rhs_hi), (lhs_hi, rhs_lo), (lhs_lo, rhs_hi)]


def skewed(eng, n, body):
    body(0, True, False)
    with eng.Fori(1, n) as j:
        body(j, True, True)
    body(n, False, True)


def load(nc, sp, loads, arrived):
    if not loads:
        return
    with nc.allow_non_contiguous_dma(reason="biases of interleaved keys and values: 512 words"):
        for dst, src in loads:
            sp.dma_start(dst, src).then_inc(arrived, 16)
    sp.wait_ge(arrived, 16 * len(loads))


CONST_ROWS = ("bq", "bk", "bias_k", "bias_v", "bv")


def phase_setup(nc, A, G):
    with Mem(nc, "su", G.psum) as m:
        w_nat = m.sb("w_nat", [P, 4, P])
        stats = [m.sb(f"stats{n}", [P, PAIRS, 6]) for n in range(2)]
        mv = [m.sb(f"mv{n}", [P, PAIRS, 2]) for n in range(2)]
        rstd = [m.sb(f"rstd{n}", [P, PAIRS]) for n in range(2)]
        shift = m.sb("shift", [P, PAIRS])
        rows = m.sb("rows", [5 * H1, 2, P])
        ctx_psum = [m.ps(f"ctx_psum{i}", (P, KT, P)) for i in range(3)]
        turn_ps = m.ps("turn_ps", (P, 3, P))
        y_ps = m.ps("y_ps", (P, 2, P))
        cols_ps = m.ps("cols_ps", (P, 2, 5 * H1))
        x_in, ctx_in = [m.sem(f"x_in{q}") for q in range(4)], [m.sem(f"ctx_in{q}") for q in range(4)]
        ident_zero, ident_made, half_made = m.sem("ident_zero"), m.sem("ident_made"), m.sem("half_made")
        transposed, hi_done, lo_done = m.sem("transposed"), m.sem("hi_done"), m.sem("lo_done")
        w_zero, w_in, w_turned, w_kept = m.sem("w_zero"), m.sem("w_in"), m.sem("w_turned"), m.sem("w_kept")
        g_psum = m.sem("g_psum")
        stats_done, mv_done, eps_added, rstd_done = ([m.sem(f"{n}{t}") for t in range(2)] for n in
            ("stats_done", "mv_done", "eps_added", "rstd_done"))
        shift_done = m.sem("shift_done")
        rows_in, cols_psum = m.sem("rows_in"), m.sem("cols_psum")
        x_dram = A["x"].rearrange("(p b) t d -> (b t) p d", b=2)
        c_dram = A["ctx_2048"].rearrange("(p b) t d -> (b t) p d", b=2)
        small_in = 16 * 16
        with nc.Block() as block:
            @block.sync
            def _(sp):
                for q in range(4):
                    sp.dma_start(G.ctx_tok[:, 4 * q:4 * q + 4, :], c_dram[:, 4 * q:4 * q + 4, :]).then_inc(ctx_in[q], 16)
                for q in range(4):
                    sp.dma_start(G.x_res[:, 4 * q:4 * q + 4, :], x_dram[:, 4 * q:4 * q + 4, :]).then_inc(x_in[q], 16)
                sp.wait_ge(w_zero, 1)
                for i, n in enumerate(("Wn", "Wm", "Wl", "Wo")):
                    for b in range(2):
                        sp.dma_start(w_nat[64 * b:64 * b + 64, i, 64 * b:64 * b + 64], A[f"L0_xattn_{n}"]).then_inc(w_in, 16)
                for i, n in enumerate(("bn", "bm", "bl", "bo")):
                    for b in range(2):
                        sp.dma_start(G.bias0[64 * b:64 * b + 64, i:i + 1],
                                     A[f"L0_xattn_{n}"].rearrange("(p o) -> p o", o=1)).then_inc(w_in, 16)
                for i in range(2):
                    for n, name in enumerate(CONST_ROWS):
                        src = A[f"L1_xattn_{name}{i + 1}"]
                        src = src.rearrange("a b h d -> (a b h) d") if len(src.shape) == 4 else src.rearrange("(h d) -> h d", d=K1)
                        sp.dma_start(rows[n * H1:(n + 1) * H1, i, :], src).then_inc(rows_in, 16)

            @block.gpsimd
            def _(pool):
                pool.memset(G.ident[:, :], 0.0).then_inc(ident_zero, 1)
                pool.wait_ge(ident_zero, 1)
                pool.affine_select(out=G.ident[:, :], in_=G.ident[:, :], compare_op=ALU.not_equal, fill=1.0,
                                   base=0, pattern=[[-1, P]], channel_multiplier=1).then_inc(ident_made, 1)
                pool.memset(G.minus_half[:, :], -0.5).then_inc(half_made, 1)
                pool.wait_ge(half_made, 1)
                for t in range(2):
                    for half in range(2):
                        ps = slice(half * PAIRS // 2, (half + 1) * PAIRS // 2)
                        pool.wait_ge(mv_done[t], ps.stop)
                        pool.tensor_scalar(rstd[t][:, ps], mv[t][:, ps, 1], 1e-5, None, ALU.add).then_inc(eps_added[t], 1)
                        pool.wait_ge(eps_added[t], half + 1)
                        pool.tensor_tensor(rstd[t][:, ps], rstd[t][:, ps], G.minus_half[:, 0:PAIRS // 2], ALU.pow).then_inc(rstd_done[t], 1)

            @block.tensor
            def _(pe):
                pe.wait_ge(ident_made, 1)
                for p in range(PAIRS):
                    pe.wait_ge(ctx_in[p // 4], 16)
                    if p >= 3:
                        pe.wait_ge(lo_done, p - 2)
                    for k in range(KT):
                        mm = pe.transpose(ctx_psum[p % 3][:, k, :], G.ctx_tok[:, p, k * P:(k + 1) * P], G.ident[:, :])
                    mm.then_inc(transposed, 1)
                pe.wait_ge(w_in, small_in)
                for i, src in enumerate((0, 1, 3)):
                    mm = pe.transpose(turn_ps[:, i, :], w_nat[:, src, :], G.ident[:, :])
                mm.then_inc(w_turned, 1)
                pe.wait_ge(rows_in, 16 * 2 * len(CONST_ROWS))
                for i in range(2):
                    mm = pe.transpose(cols_ps[:, i, :], rows[:, i, :], G.ident[0:5 * H1, 0:5 * H1])
                mm.then_inc(cols_psum, 1)
                pe.wait_ge(w_kept, 1)
                pe.matmul(y_ps[:, 0, :], w_nat[:, 2, :], G.w_t[:, 3, :], start=True, stop=True)
                pe.matmul(y_ps[:, 1, 0:1], G.w_t[:, 3, :], G.bias0[:, 2:3], start=True, stop=True).then_inc(g_psum, 1)

            @block.scalar
            def _(act):
                for p in range(PAIRS):
                    act.wait_ge(transposed, p + 1)
                    act.activation(G.ctx_hi[:, :, p * P:(p + 1) * P], ctx_psum[p % 3][:, :, :], ACT.Copy).then_inc(hi_done, 1)
                act.wait_ge(shift_done, 1)
                for p in range(PAIRS):
                    act.activation(G.xn[:, PAIRS + p, :], G.ctx_tok[:, p, :], ACT.Identity,
                                   bias=shift[:, p:p + 1], scale=rstd[0][:, p:p + 1])

            @block.vector
            def _(dve):
                dve.memset(w_nat[:, :, :], 0.0).then_inc(w_zero, 1)
                for p in range(PAIRS):
                    dve.wait_ge(ctx_in[p // 4], 16)
                    dve.bn_stats(stats[0][:, p, :], G.ctx_tok[:, p, :]).then_inc(stats_done[0], 1)
                    dve.wait_ge(hi_done, p + 1)
                    dve.tensor_tensor(G.ctx_lo[:, :, p * P:(p + 1) * P], ctx_psum[p % 3][:, :, :],
                                      G.ctx_hi[:, :, p * P:(p + 1) * P].bitcast(F32), ALU.subtract).then_inc(lo_done, 1)

                def aggregate(t):
                    for p in range(PAIRS):
                        dve.wait_ge(stats_done[t], p + 1)
                        dve.bn_aggr(mv[t][:, p, :], stats[t][:, p, :]).then_inc(mv_done[t], 1)
                aggregate(0)
                for p in range(PAIRS):
                    dve.wait_ge(x_in[p // 4], 16)
                    dve.bn_stats(stats[1][:, p, :], G.x_res[:, p, :]).then_inc(stats_done[1], 1)
                    if p == PAIRS - 3:
                        dve.wait_ge(rstd_done[0], 2)
                        dve.wait_ge(mv_done[0], PAIRS)
                        dve.scalar_tensor_tensor(shift[:, :], mv[0][:, :, 0], -1.0, rstd[0][:, :], ALU.mult, ALU.mult).then_inc(shift_done, 1)
                aggregate(1)
                dve.wait_ge(w_turned, 1)
                dve.tensor_copy(G.w_t[:, 0:2, :], turn_ps[:, 0:2, :])
                dve.tensor_copy(G.w_t[:, 3, :], turn_ps[:, 2, :]).then_inc(w_kept, 1)
                dve.wait_ge(cols_psum, 1)
                dve.tensor_copy(G.cols[:, :, :], cols_ps[:, :, :])
                dve.wait_ge(g_psum, 1)
                dve.tensor_copy(G.w_t[:, 2, :], y_ps[:, 0, :])
                dve.tensor_tensor(G.obias[:, :], y_ps[:, 1, 0:1], G.bias0[:, 3:4], ALU.add)
                dve.wait_ge(mv_done[1], PAIRS)
                for p in range(PAIRS):
                    if p % (PAIRS // 2) == 0:
                        dve.wait_ge(rstd_done[1], 1 + p // (PAIRS // 2))
                    dve.tensor_scalar(G.xn[:, p, :], G.x_res[:, p, :], mv[1][:, p, 0:1], rstd[1][:, p:p + 1],
                                      ALU.subtract, ALU.mult)


def phase_layer0(nc, A, G):
    with Mem(nc, "l0", G.psum) as m:
        c_fix = [m.sb(f"c_fix{i}", [P, D]) for i in range(2)]
        mix = m.sb("mix", [P, 2, D])
        prob = [m.sb(f"prob{i}", [P, 2, 2, D]) for i in range(2)]
        prob_t = m.sb("prob_t", [P, 2, 2, D])
        y_sb = [m.sb(f"y{i}", [P, 2, P]) for i in range(2)]
        nmax = m.sb("nmax", [P, 2, 2])
        ssum = m.sb("ssum", [P, 2, 4])
        rsum = m.sb("rsum", [P, 4])
        mix_ps = m.ps("mix_ps", (P, 2, D))
        y_ps = m.ps("y_ps", (P, 2, P))
        s_ps = [m.ps(f"s_ps{i}", (P, 2, D)) for i in range(2)]
        t_ps = [m.ps(f"t_ps{i}", (P, 2, D)) for i in range(2)]
        o_ps = m.ps("o_ps", (P, D))
        c_fixed, mix_psum, mix_done, s_psum = (m.sem(n) for n in ("c_fixed", "mix_psum", "mix_done", "s_psum"))
        max_done, exp_done, rsum_done, prob_done = (m.sem(n) for n in ("max_done", "exp_done", "rsum_done", "prob_done"))
        t_psum, t_act, t_dve = (m.sem(n) for n in ("t_psum", "t_act", "t_dve"))
        y_psum, y_done, o_psum, x_done = (m.sem(n) for n in ("y_psum", "y_done", "o_psum", "x_done"))
        STEPS = PAIRS // 2
        with nc.Block() as block:
            @block.gpsimd
            def _(pool):
                def body(j, front, back):
                    for q in range(2):
                        if front:
                            u = 2 * j + q
                            if back:
                                pool.wait_ge(y_psum, u - 1)
                            pool.tensor_copy(c_fix[q][:, :], G.ctx_tok[:, ds(u, 1), :]).then_inc(c_fixed, 1)
                body(0, True, False)
                with pool.Fori(1, STEPS) as j:
                    body(j, True, True)

            @block.tensor
            def _(pe):
                def body(j, front, back):
                    for q in range(2):
                        u = 2 * j + q
                        if front:
                            if back or q:
                                pe.wait_ge(mix_done, u)
                            for i in range(2):
                                mm = pe.matmul(mix_ps[:, i, :], G.w_t[:, i, :], G.xn[:, ds(i * PAIRS + u, 1), :],
                                               start=True, stop=True)
                            mm.then_inc(mix_psum, 1)
                        if back:
                            r = u - 2
                            pe.wait_ge(prob_done, r + 1)
                            pe.wait_ge(t_act, r + 1)
                            pe.wait_ge(t_dve, r + 1)
                            for b in range(2):
                                for sh in range(2):
                                    for th in range(2):
                                        mm = pe.transpose(t_ps[b][:, sh, th * P:th * P + P],
                                                          prob[q][:, b, th, sh * P:sh * P + P], G.ident[:, :])
                                mm.then_inc(t_psum, 1)
                        if front:
                            pe.wait_ge(mix_done, u + 1)
                            if back or q:
                                pe.wait_ge(exp_done, 4 * u)
                            for b in range(2):
                                for th in range(2):
                                    mm = pe.matmul(s_ps[b][:, th, :], mix[64 * b:64 * b + 64, 0, th * P:th * P + P],
                                                   mix[64 * b:64 * b + 64, 1, :], start=True, stop=True)
                                mm.then_inc(s_psum, 1)
                        if back:
                            pe.wait_ge(t_act, r + 2)
                            pe.wait_ge(t_dve, r + 2)
                            pe.wait_ge(x_done, r + 1)
                            for b in range(2):
                                for sh in range(2):
                                    mm = pe.matmul(o_ps[64 * b:64 * b + 64, :], y_sb[q][:, sh, 64 * b:64 * b + 64],
                                                   prob_t[:, b, sh, :], start=(sh == 0), stop=(sh == 1))
                            mm.then_inc(o_psum, 1)
                        if front:
                            pe.wait_ge(c_fixed, u + 1)
                            if back or q:
                                pe.wait_ge(y_done, u)
                            for sh in range(2):
                                mm = pe.matmul(y_ps[:, sh, :], c_fix[q][:, sh * P:sh * P + P], G.w_t[:, 2, :],
                                               start=True, stop=True)
                            mm.then_inc(y_psum, 1)
                skewed(pe, STEPS, body)

            @block.scalar
            def _(act):
                def body(j, front, back):
                    for q in range(2):
                        u = 2 * j + q
                        if front:
                            act.wait_ge(mix_psum, u + 1)
                            act.activation(mix[:, 0, :], mix_ps[:, 0, :], ACT.Identity, bias=G.bias0[:, 0:1])
                            act.activation(mix[:, 1, :], mix_ps[:, 1, :], ACT.Identity, bias=G.bias0[:, 1:2]).then_inc(mix_done, 1)
                        if back:
                            r = u - 2
                            act.wait_ge(t_psum, 2 * r + 1)
                            act.activation(prob_t[:, 0, :, :], t_ps[0][:, :, :], ACT.Copy).then_inc(t_act, 1)
                        if front:
                            for b in range(2):
                                act.wait_ge(max_done, 2 * u + b + 1)
                                for th in range(2):
                                    act.activation(prob[q][:, b, th, :], s_ps[b][:, th, :], ACT.Exp,
                                                   bias=nmax[:, b, th:th + 1],
                                                   accum_out=ssum[:, q, 2 * b + th:2 * b + th + 1]).then_inc(exp_done, 1)
                skewed(act, STEPS, body)

            @block.vector
            def _(dve):
                dve.memset(nmax[:, :, :], 0.0).then_inc(t_act, 1)
                dve.memset(rsum[:, :], 0.0).then_inc(t_dve, 1)
                dve.memset(ssum[:, :, :], 0.0).then_inc(x_done, 1)
                dve.wait_ge(x_done, 1)
                dve.wait_ge(t_dve, 1)

                def body(j, front, back):
                    for q in range(2):
                        u = 2 * j + q
                        if back:
                            r = u - 2
                            dve.wait_ge(t_psum, 2 * r + 2)
                            dve.tensor_copy(prob_t[:, 1, :, :], t_ps[1][:, :, :]).then_inc(t_dve, 1)
                        if front:
                            if back or q:
                                dve.wait_ge(exp_done, 4 * u)
                            for b in range(2):
                                dve.wait_ge(s_psum, 2 * u + b + 1)
                                dve.tensor_reduce(nmax[:, b, :], s_ps[b][:, :, :], X_AXIS, ALU.max, negate=True).then_inc(max_done, 1)
                        if back:
                            dve.wait_ge(o_psum, r + 1)
                            dve.scalar_tensor_tensor(G.x_res[:, ds(r, 1), :], o_ps[:, :], G.obias[:, 0:1],
                                                     G.x_res[:, ds(r, 1), :], ALU.add, ALU.add).then_inc(x_done, 1)
                            dve.wait_ge(x_done, r + 2)
                            dve.bn_stats(G.stats[:, ds(r, 1), :].rearrange("p o s -> p (o s)"),
                                         G.x_res[:, ds(r, 1), :].rearrange("p o d -> p (o d)"))
                        if front:
                            dve.wait_ge(exp_done, 4 * u + 4)
                            if back or q:
                                dve.wait_ge(prob_done, u)
                            dve.reciprocal(rsum[:, :], ssum[:, q, :]).then_inc(rsum_done, 1)
                            dve.wait_ge(rsum_done, u + 1)
                            for i in range(4):
                                sc = dve.tensor_scalar(prob[q][:, i // 2, i % 2, :], prob[q][:, i // 2, i % 2, :],
                                                       rsum[:, i:i + 1], None, ALU.mult)
                            sc.then_inc(prob_done, 1)
                            dve.wait_ge(y_psum, u + 1)
                            dve.tensor_copy(y_sb[q][:, :, :], y_ps[:, :, :]).then_inc(y_done, 1)
                skewed(dve, STEPS, body)


def phase_features(nc, G, tag, src, dst_hi, dst_lo, kind, eps=0.0, scale=None, offset=None,
                   update=False, mlp=None, loads=(), have_stats=True,
                   attention=None):
    with Mem(nc, tag, G.psum) as m:
        affine = m.sb("affine", [P, 2, KT])
        row_in = m.sb("row_in", [2 * KT, P])
        stats = G.stats if have_stats else m.sb("stats", [P, PAIRS, 6])
        mv = m.sb("mv", [P, PAIRS, 2])
        rstd = m.sb("rstd", [P, PAIRS])
        normed = m.sb("normed", [P, PAIRS, D])
        raw = [m.sb(f"raw{i}", [P, BLK]) for i in range(2)]
        feat_ps = [m.ps(f"feat_ps{i}", (P, BLK)) for i in range(3)]
        affine_ps = m.ps("affine_ps", (P, 2 * KT))
        affine_in, stats_done, mv_done, eps_added, rstd_done, normed_done = (m.sem(n) for n in
            ("affine_in", "stats_done", "mv_done", "eps_added", "rstd_done", "normed_done"))
        feat_psum, raw_done, hi_done, lo_done = (m.sem(n) for n in ("feat_psum", "raw_done", "hi_done", "lo_done"))
        affine_psum, affine_done, rows_zero = m.sem("affine_psum"), m.sem("affine_done"), m.sem("rows_zero")
        if update:
            spread_affine = m.sb("spread_affine", [P, 2, D])
            spread_in, scaled = m.sem("spread_in"), m.sem("scaled")
        arrived = m.sem("arrived")
        if attention:
            i_att, wo_dram, bo_dram = attention
            wo, bo = m.sb("wo", [P, H1, D]), m.sb("bo", [1, D])
            lhs, unit = m.sb("lhs", [P, H1, H1 + 1]), m.sb("unit", [1, H1 + 1])
            bvo_ps = m.ps("bvo_ps", (H1 + 1, D))
            wo_in, cleared, unit_zero, lhs_done, bvo_psum = (m.sem(n) for n in
                ("wo_in", "cleared", "unit_zero", "lhs_done", "bvo_psum"))
        if mlp:
            w_in, w_high = [m.sem(f"w_in{n}") for n in range(2)], m.sem("w_high")
            small_in = m.sem("small_in")
        normalized = src if kind == "plain" else normed
        with nc.Block() as block:
            @block.sync
            def _(sp):
                if scale is not None:
                    sp.wait_ge(rows_zero, 1)
                    sp.dma_start(row_in[0:KT, :], scale.rearrange("(k p) -> k p", p=P)).then_inc(affine_in, 16)
                    if offset is not None:
                        sp.dma_start(row_in[KT:2 * KT, :], offset.rearrange("(k p) -> k p", p=P)).then_inc(affine_in, 16)
                if update:
                    for n, v in enumerate((scale, offset)):
                        sp.dma_start(spread_affine[:, n, :], v.rearrange("(o n) -> o n", o=1).partition_broadcast(P)).then_inc(spread_in, 16)
                if attention:
                    sp.dma_start(wo[:, :, :], wo_dram.rearrange("(h d) n -> d h n", d=K1)).then_inc(wo_in, 16)
                    sp.dma_start(bo[:, :], bo_dram.rearrange("(o n) -> o n", o=1)).then_inc(wo_in, 16)
                if mlp and not mlp.loaded:
                    for (to, of), w_arrived in zip(mlp.w_loads, w_in):
                        sp.dma_start(to, of).then_inc(w_arrived, 16)
                    load(nc, sp, mlp.small_loads, small_in)
                load(nc, sp, loads, arrived)

            @block.gpsimd
            def _(pool):
                if attention:
                    pool.memset(lhs[:, :, :], 0.0).then_inc(cleared, 1)
                    pool.memset(unit[:, :], 0.0).then_inc(unit_zero, 1)
                    pool.wait_ge(unit_zero, 1)
                    pool.memset(unit[:, H1:H1 + 1], 1.0).then_inc(cleared, 1)
                    pool.wait_ge(cleared, 2)

                def scales(b):
                    for p in range(PPB * b, PPB * (b + 1)):
                        pool.wait_ge(normed_done, p + 1)
                        pool.tensor_tensor(src[:, p, :], normed[:, p, :], spread_affine[:, 0, :], ALU.mult).then_inc(scaled, 1)
                if update:
                    pool.wait_ge(spread_in, 32)
                for b in range(NBLK if kind != "plain" else 0):
                    ps = slice(PPB * b, PPB * (b + 1))
                    pool.wait_ge(mv_done, PPB * (b + 1))
                    if kind == "rms":
                        pool.tensor_tensor(rstd[:, ps], mv[:, ps, 0], mv[:, ps, 0], ALU.mult).then_inc(eps_added, 1)
                        pool.wait_ge(eps_added, 3 * b + 1)
                        pool.tensor_tensor(rstd[:, ps], rstd[:, ps], mv[:, ps, 1], ALU.add).then_inc(eps_added, 1)
                        pool.wait_ge(eps_added, 3 * b + 2)
                        pool.tensor_scalar(rstd[:, ps], rstd[:, ps], eps, None, ALU.add).then_inc(eps_added, 1)
                    else:
                        pool.tensor_scalar(rstd[:, ps], mv[:, ps, 1], eps, None, ALU.add).then_inc(eps_added, 3)
                    pool.wait_ge(eps_added, 3 * b + 3)
                    pool.tensor_tensor(rstd[:, ps], rstd[:, ps], G.minus_half[:, 0:PPB], ALU.pow).then_inc(rstd_done, 1)
                    if update and b:
                        scales(b - 1)
                if update:
                    scales(NBLK - 1)
                if mlp:
                    for n, (raw_w, hi_w, lo_w) in enumerate(mlp.splits):
                        pool.wait_ge(w_high, n + 1)
                        pool.tensor_tensor(lo_w, raw_w, hi_w.bitcast(F32), ALU.subtract)

            @block.tensor
            def _(pe):
                def feature_block(b):
                    if kind != "plain":
                        pe.wait_ge(normed_done, PPB * (b + 1))
                    for k in range(KT):
                        n = KT * b + k
                        if n >= 3:
                            pe.wait_ge(raw_done, n - 2)
                        for i in range(PPB):
                            mm = pe.transpose(feat_ps[n % 3][:, i * P:(i + 1) * P],
                                              normalized[:, PPB * b + i, k * P:(k + 1) * P], G.ident[:, :])
                        mm.then_inc(feat_psum, 1)
                if scale is not None:
                    pe.wait_ge(affine_in, 16 if offset is None else 32)
                    pe.transpose(affine_ps[:, :], row_in[:, :], G.ident[0:2 * KT, 0:2 * KT]).then_inc(affine_psum, 1)
                for b in range(NBLK):
                    feature_block(b)
                    if attention and b:
                        if b == 1:
                            pe.wait_ge(lhs_done, 2)
                            pe.wait_ge(cleared, 2)
                            pe.wait_ge(wo_in, 32)
                        for h in range(H1 * (b - 1) // (NBLK - 1), H1 * b // (NBLK - 1)):
                            pe.matmul(bvo_ps[:, :], lhs[:, h, :], wo[:, h, :], start=(h == 0), stop=False)
                if attention:
                    pe.matmul(bvo_ps[:, :], unit[:, :], bo[:, :], start=False, stop=True).then_inc(bvo_psum, 1)

            @block.scalar
            def _(act):
                if scale is not None:
                    act.wait_ge(affine_psum, 1)
                    act.activation(affine[:, :, :].rearrange("p a k -> p (a k)"), affine_ps[:, :], ACT.Copy).then_inc(affine_done, 1)
                    act.wait_ge(affine_done, 1)
                for b in range(1, NBLK + 1):
                    for n in range(KT * (b - 1), KT * b):
                        k, cols = n % KT, slice((b - 1) * BLK, b * BLK)
                        act.wait_ge(feat_psum, n + 1)
                        to = raw[n % 2][:, :]
                        if dst_lo is None:
                            to = dst_hi[:, k, cols]
                        elif n >= 2:
                            act.wait_ge(lo_done, n - 1)
                        if scale is not None:
                            act.activation(to, feat_ps[n % 3][:, :], ACT.Identity,
                                           bias=affine[:, 1, k:k + 1], scale=affine[:, 0, k:k + 1]).then_inc(raw_done, 1)
                        else:
                            act.activation(to, feat_ps[n % 3][:, :], ACT.Copy).then_inc(raw_done, 1)
                        if dst_lo is not None:
                            act.wait_ge(raw_done, n + 1)
                            act.activation(dst_hi[:, k, cols], raw[n % 2][:, :], ACT.Copy).then_inc(hi_done, 1)
                    for n in ((), (0, 1), (2,), (3,), ())[b] if mlp else ():
                        raw_w, hi_w, _ = mlp.splits[n]
                        if not mlp.loaded:
                            act.wait_ge(w_in[n // 2], 16)
                        act.activation(hi_w, raw_w, ACT.Copy).then_inc(w_high, 1)

            @block.vector
            def _(dve):
                dve.memset(row_in[:, :], 0.0).then_inc(rows_zero, 1)
                if attention:
                    bias_v, bv = (G.cols[:, i_att - 1, n * H1:(n + 1) * H1] for n in (3, 4))
                    dve.wait_ge(cleared, 2)
                    diagonal = lhs[:, :, :].rearrange("p h c -> p (h c)")[:, 0:H1 * (H1 + 1):H1 + 2]
                    dve.tensor_tensor(diagonal, bias_v, bv, ALU.subtract).then_inc(lhs_done, 1)
                    dve.tensor_copy(lhs[:, :, H1], bv).then_inc(lhs_done, 1)

                def statistics(b):
                    ps = range(PPB * b, PPB * (b + 1))
                    for p in ps if not have_stats else ():
                        dve.bn_stats(stats[:, p, :], src[:, p, :]).then_inc(stats_done, 1)
                    for p in ps:
                        if not have_stats:
                            dve.wait_ge(stats_done, p + 1)
                        dve.bn_aggr(mv[:, p, :], stats[:, p, :]).then_inc(mv_done, 1)

                def normalize(b):
                    dve.wait_ge(rstd_done, b + 1)
                    dve.wait_ge(mv_done, PPB * (b + 1))
                    for p in range(PPB * b, PPB * (b + 1)):
                        if kind == "ln":
                            dve.tensor_scalar(normed[:, p, :], src[:, p, :], mv[:, p, 0:1], rstd[:, p:p + 1],
                                              ALU.subtract, ALU.mult).then_inc(normed_done, 1)
                        else:
                            dve.tensor_scalar(normed[:, p, :], src[:, p, :], rstd[:, p:p + 1], None,
                                              ALU.mult).then_inc(normed_done, 1)

                def low_parts(b):
                    for k in range(KT):
                        n, cols = KT * b + k, slice(b * BLK, (b + 1) * BLK)
                        dve.wait_ge(hi_done, n + 1)
                        dve.tensor_tensor(dst_lo[:, k, cols], raw[n % 2][:, :], dst_hi[:, k, cols].bitcast(F32),
                                          ALU.subtract).then_inc(lo_done, 1)

                def offsets(b):
                    for p in range(PPB * b, PPB * (b + 1)):
                        dve.wait_ge(scaled, p + 1)
                        dve.tensor_tensor(src[:, p, :], src[:, p, :], spread_affine[:, 1, :], ALU.add)
                if update:
                    dve.wait_ge(spread_in, 32)
                for b in range(NBLK if have_stats and kind != "plain" else 0):
                    statistics(b)
                for b in range(NBLK + 2 if kind != "plain" else 0):
                    if b < NBLK and not have_stats:
                        statistics(b)
                    if 1 <= b <= NBLK:
                        normalize(b - 1)
                    if b >= 2 and dst_lo is not None:
                        low_parts(b - 2)
                    if b >= 2 and update:
                        offsets(b - 2)
                if attention:
                    dve.wait_ge(bvo_psum, 1)
                    dve.tensor_copy(G.bvo[:, :], bvo_ps[:, :])


class Operands:
    pass


def attention_operands(m, A, i):
    w = Operands()
    w.stage_qk = m.sb("stage_qk", [P, 2, 2, KT, K1])
    w.stage_vo = m.sb("stage_vo", [P, KT * HG * K1])
    w.qk_dram = [A[f"L1_xattn_{n}{i}"].rearrange("(k p) n -> p k n", p=P) for n in ("wq", "wk")]
    w.v_dram = A[f"L1_xattn_wv{i}"].rearrange("(k p) n -> p k n", p=P)
    w.o_dram = A[f"L1_xattn_wo{i}"].rearrange("(h d) n -> d h n", d=K1)
    w.loads = [(w.stage_qk[:, h, n, :, :], w.qk_dram[n][:, :, h * K1:(h + 1) * K1]) for h in range(2) for n in range(2)] + \
              [(w.stage_vo[:, :].rearrange("p (k n) -> p k n", k=KT), w.v_dram[:, :, 0:HG * K1])]
    return w


def phase_layer1_attention(nc, A, G, i, w):
    tag = f"att{i}"
    NI = NG * NBLK
    KP = T + 1
    stage_qk, stage_vo = w.stage_qk, w.stage_vo
    q_scale = float(K1) ** -0.5
    with Mem(nc, tag, G.psum) as m:
        q_sb = m.sb("q_sb", [P, HG, BLK])
        k_sb = m.sb("k_sb", [P, HG, 2 * PPB, KP])
        v_sb = m.sb("v_sb", [P, PPB, HG * K1])
        pt = m.sb("pt", [P, BLK])
        ot_hi, ot_lo = (m.sb(n, [P, HG, BLK], F32R) for n in ("ot_hi", "ot_lo"))
        wqk_hi, wqk_lo = (m.sb(n, [P, HG, 2, KT, K1], F32R) for n in ("wqk_hi", "wqk_lo"))
        wv_hi, wv_lo = (m.sb(n, [P, KT, HG * K1], F32R) for n in ("wv_hi", "wv_lo"))
        wo_hi, wo_lo = (m.sb(n, [P, HG, D], F32R) for n in ("wo_hi", "wo_lo"))
        cf_hi, cf_lo = (m.sb(n, [P, KT, BLK], F32R) for n in ("cf_hi", "cf_lo"))
        soft = m.sb("soft", [P, PPB, KP])
        prob = m.sb("prob", [P, PPB, P])
        rmax = m.sb("rmax", [P, PPB])
        rsum = m.sb("rsum", [P, PPB])
        rinv = m.sb("rinv", [P, PPB])
        q_ps, k_ps = m.ps("q_ps"), m.ps("k_ps")
        s_ps = m.ps("s_ps", (P, PPB, 2 * P))
        t_ps, c_ps = m.ps("t_ps"), m.ps("c_ps")
        o_ps = [m.ps(f"o_ps{n}", (P, 2, D)) for n in range(2)]
        v_ps = [q_ps, k_ps]
        bp_t = m.sb("bp_t", [H1 + 1, PPB, P])
        bias_block = m.sb("bias_block", [P, PPB, H1 + 1])
        block_ready, bt_psum, bt_done = m.sem("block_ready"), m.sem("bt_psum"), m.sem("bt_done")
        w_hi_act, w_hi_dve = m.sem("w_hi_act"), m.sem("w_hi_dve")
        qk_in = [m.sem(f"qk_in{n}") for n in range(2)]
        vo_in, w_hi, wqk_ready, wv_ready, wo_ready, cf_ready, kb_ready = (m.sem(n) for n in
            ("vo_in", "w_hi", "wqk_ready", "wv_ready", "wo_ready", "cf_ready", "kb_ready"))
        q_psum, k_psum, v_psum, s_psum, t_psum, c_psum, o_psum = (m.sem(n) for n in
            ("q_psum", "k_psum", "v_psum", "s_psum", "t_psum", "c_psum", "o_psum"))
        q_ready, k_ready, pt_ready, ot_high, ot_ready, x_added = (m.sem(n) for n in
            ("q_ready", "k_ready", "pt_ready", "ot_high", "ot_ready", "x_added"))
        v_ready = [m.sem("v_ready_act"), m.sem("v_ready_dve")]
        max_done, shifted, exp_done, sum_done, inv_done, prob_ready = (m.sem(n) for n in
            ("max_done", "shifted", "exp_done", "sum_done", "inv_done", "prob_ready"))

        def items(eng, body):
            body(0, True, False, False)
            with eng.Fori(1, NI - NBLK + 1) as j:
                body(j, True, True, False)
            with eng.Fori(NI - NBLK + 1, NI) as j:
                body(j, True, True, True)
            body(NI, False, True, True)

        def score_item(j, h, front, back):
            if h < HG - 1:
                return (j - 1, h + 1) if back else None
            return (j, 0) if front else None

        with nc.Block() as block:
            @block.sync
            def _(sp):
                def group(g, first):
                    for h in range(2 if first else 0, HG):
                        sp.wait_ge(wqk_ready, HG * g + h - 1)
                        for n in range(2):
                            sp.dma_start(stage_qk[:, h % 2, n, :, :],
                                         w.qk_dram[n][:, :, ds((HG * g + h) * K1, K1)]).then_inc(qk_in[h % 2], 16)
                    if not first:
                        sp.wait_ge(wo_ready, g)
                        sp.dma_start(stage_vo[:, :].rearrange("p (k n) -> p k n", k=KT),
                                     w.v_dram[:, :, ds(HG * K1 * g, HG * K1)]).then_inc(vo_in, 16)
                    sp.wait_ge(wv_ready, g + 1)
                    sp.dma_start(stage_vo[:, :].rearrange("p (h n) -> p h n", h=HG),
                                 w.o_dram[:, ds(HG * g, HG), :]).then_inc(vo_in, 16)
                group(0, True)
                with sp.Fori(1, NG) as g:
                    group(g, False)

            @block.gpsimd
            def _(pool):
                SPLITS = HG + 2
                LESS = 3

                def split(count, hi, lo, raw, ready):
                    pool.tensor_copy(hi, raw).then_inc(w_hi, 1)
                    pool.wait_ge(w_hi, count)
                    pool.tensor_tensor(lo, raw, hi.bitcast(F32), ALU.subtract).then_inc(ready, 1)

                def context_block(g, b, first):
                    if not (first and b == 0):
                        pool.wait_ge(v_psum, PPB * (NBLK * g + b))
                    pool.tensor_copy(cf_hi[:, :, :], G.ctx_hi[:, :, b * BLK:(b + 1) * BLK].bitcast(F32))
                    pool.tensor_copy(cf_lo[:, :, :], G.ctx_lo[:, :, b * BLK:(b + 1) * BLK].bitcast(F32)).then_inc(cf_ready, 1)

                def key_bias(g, b, first):
                    for h in range(HG):
                        pool.wait_ge(k_psum, HG * (NBLK * g + b) + h + 1)
                        pool.tensor_copy(k_sb[:, h, :, T:KP], G.cols[:, i - 1, ds(2 * H1 + HG * g + h, 1)]
                                         .unsqueeze(1).to_broadcast([P, 2 * PPB, 1])).then_inc(kb_ready, 1)

                def group(g, first):
                    done = 0 if first else SPLITS * g - LESS
                    for h in range(HG):
                        hi, lo, raw = wqk_hi[:, h, :, :, :], wqk_lo[:, h, :, :, :], stage_qk[:, h % 2, :, :, :]
                        if first and h < 2:
                            pool.wait_ge(w_hi_act, h + 1)
                            pool.tensor_tensor(lo, raw, hi.bitcast(F32), ALU.subtract).then_inc(wqk_ready, 1)
                            continue
                        pool.wait_ge(qk_in[h % 2], 32 * (HG // 2 * g + h // 2))
                        if not first:
                            pool.wait_ge(k_psum, HG * NBLK * g - HG + h + 1)
                        done += 1
                        split(done, hi, lo, raw, wqk_ready)
                    if not first:
                        pool.wait_ge(vo_in, 32 * g)
                        pool.wait_ge(v_psum, PPB * NBLK * g)
                        done += 1
                        split(done, wv_hi[:, :, :], wv_lo[:, :, :],
                              stage_vo[:, :].rearrange("p (k n) -> p k n", k=KT), wv_ready)
                        context_block(g, 0, first)
                    key_bias(g, 0, first)
                    context_block(g, 1, first)
                    pool.wait_ge(vo_in, 32 * g + 16)
                    if not first:
                        pool.wait_ge(o_psum, 2 * NBLK * g)
                    split(done + 1, wo_hi[:, :, :], wo_lo[:, :, :],
                          stage_vo[:, :].rearrange("p (h n) -> p h n", h=HG), wo_ready)
                    key_bias(g, 1, first)
                    for b in (2, 3):
                        context_block(g, b, first)
                        key_bias(g, b, first)
                for g in range(NG):
                    group(g, g == 0)

            @block.tensor
            def _(pe):
                def body(j, front, back, last):
                    if front:
                        g, off = j // NBLK, (j % NBLK) * BLK
                    for h in range(HG):
                        item = score_item(j, h, front, back)
                        if item:
                            js, hs = item
                            n = HG * js + hs
                            pe.wait_ge(q_ready, n + 1)
                            pe.wait_ge(k_ready, n + 1)
                            pe.wait_ge(kb_ready, n + 1)
                            if back:
                                pe.wait_ge(shifted, 2 * n)
                            for p in range(PPB):
                                cols = slice(p * P, (p + 1) * P)
                                mm = pe.matmul(s_ps[:, p, 0:2 * KP], q_sb[:, hs, cols], k_sb[:, hs, 2 * p:2 * p + 2, :],
                                               start=True, stop=True)
                            mm.then_inc(s_psum, 1)
                        if back:
                            n = HG * (j - 1) + h
                            pe.wait_ge(prob_ready, 3 * n + 3)
                            pe.wait_ge(pt_ready, n + 1)
                            for p in range(PPB):
                                mm = pe.transpose(t_ps[:, p * P:(p + 1) * P], prob[:, p, :], G.ident[:, :])
                            mm.then_inc(t_psum, 1)
                        if back and last and h == HG - 1:
                            pe.wait_ge(x_added, 2 * (j - 1) + 1)
                            pe.wait_ge(block_ready, j - (NI - NBLK))
                            for p in range(PPB):
                                mm = pe.transpose(o_ps[1][0:H1 + 1, :, :].rearrange("p a d -> p (a d)")[:, p * P:(p + 1) * P],
                                                  bias_block[:, p, :], G.ident[:, :])
                            mm.then_inc(bt_psum, 1)
                        if front:
                            n = HG * j + h
                            pe.wait_ge(wqk_ready, HG * g + h + 1)
                            if back or h:
                                pe.wait_ge(q_ready, n)
                                pe.wait_ge(k_ready, n)
                            if back and h == 0:
                                for copied in v_ready:
                                    pe.wait_ge(copied, 2 * j)
                            for w, dst, x_hi, x_lo, done in ((0, q_ps, G.feat_hi, G.feat_lo, q_psum),
                                                             (1, k_ps, G.ctx_hi, G.ctx_lo, k_psum)):
                                for k in range(KT):
                                    prods = split_products(wqk_hi[:, h, w, k, :], wqk_lo[:, h, w, k, :],
                                                           x_hi[:, k, ds(off, BLK)], x_lo[:, k, ds(off, BLK)])
                                    for t, (a, b) in enumerate(prods):
                                        mm = pe.matmul(dst[:, :], a, b, start=(k == 0 and t == 0),
                                                       stop=(k == KT - 1 and t == 2))
                                mm.then_inc(done, 1)
                        if back:
                            n = HG * (j - 1) + h
                            pe.wait_ge(pt_ready, n + 2)
                            pe.wait_ge(ot_ready, n + 1)
                            for copied in v_ready:
                                pe.wait_ge(copied, 2 * j)
                            for p in range(PPB):
                                cols, head = slice(p * P, (p + 1) * P), slice(h * K1, (h + 1) * K1)
                                mm = pe.matmul(c_ps[:, cols], v_sb[:, p, head], pt[:, cols], start=True, stop=True)
                            mm.then_inc(c_psum, 1)
                    if front:
                        pe.wait_ge(wv_ready, g + 1)
                        pe.wait_ge(cf_ready, j + 1)
                        pe.wait_ge(q_ready, HG * j + HG)
                        pe.wait_ge(k_ready, HG * j + HG)
                        for p in range(PPB):
                            if p >= 2:
                                pe.wait_ge(v_ready[p % 2], 2 * j + 1)
                            for k in range(KT):
                                cols = slice(p * P, (p + 1) * P)
                                for t, (a, b) in enumerate(split_products(cf_hi[:, k, cols], cf_lo[:, k, cols],
                                                                          wv_hi[:, k, :], wv_lo[:, k, :])):
                                    mm = pe.matmul(v_ps[p % 2][:, :], a, b, start=(k == 0 and t == 0),
                                                   stop=(k == KT - 1 and t == 2))
                            mm.then_inc(v_psum, 1)
                    if back:
                        pe.wait_ge(ot_ready, HG * j + 1)
                        pe.wait_ge(wo_ready, (j - 1) // NBLK + 1)
                        pe.wait_ge(x_added, 2 * (j - 1) + 1)
                        if last:
                            pe.wait_ge(bt_done, j - (NI - NBLK))
                        for p in range(PPB):
                            cols = slice(p * P, (p + 1) * P)
                            for h in range(HG):
                                for t, (a, b) in enumerate(split_products(ot_hi[:, h, cols], ot_lo[:, h, cols],
                                                                          wo_hi[:, h, :], wo_lo[:, h, :])):
                                    mm = pe.matmul(o_ps[p // 2][:, p % 2, :], a, b, start=(h == 0 and t == 0),
                                                   stop=(not last and h == HG - 1 and t == 2))
                            if last:
                                mm = pe.matmul(o_ps[p // 2][:, p % 2, :], bp_t[:, p, :], G.bvo[:, :],
                                               start=False, stop=True)
                            if p % 2:
                                mm.then_inc(o_psum, 1)
                items(pe, body)

            @block.scalar
            def _(act):
                def body(j, front, back, last):
                    for h in range(HG):
                        if back:
                            n = HG * (j - 1) + h
                            act.wait_ge(t_psum, n + 1)
                            act.activation(pt[:, :], t_ps[:, :], ACT.Copy).then_inc(pt_ready, 1)
                        if back and last and h == HG - 1:
                            act.wait_ge(bt_psum, j - (NI - NBLK))
                            act.activation(bp_t[:, :, :].rearrange("p a q -> p (a q)"),
                                           o_ps[1][0:H1 + 1, :, :].rearrange("p a d -> p (a d)"), ACT.Copy).then_inc(bt_done, 1)
                        item = score_item(j, h, front, back)
                        if item:
                            n = HG * item[0] + item[1]
                            act.wait_ge(shifted, 2 * n + 2)
                            act.activation(soft[:, :, :], soft[:, :, :], ACT.Exp, scale=q_scale).then_inc(exp_done, 1)
                        if front:
                            n, head = HG * j + h, HG * (j // NBLK) + h
                            act.wait_ge(q_psum, n + 1)
                            act.activation(q_sb[:, h, :], q_ps[:, :], ACT.Identity,
                                           bias=G.cols[:, i - 1, ds(head, 1)]).then_inc(q_ready, 1)
                            act.wait_ge(k_psum, n + 1)
                            act.activation(k_sb[:, h, :, 0:T], k_ps[:, :].rearrange("p (b t) -> p b t", t=T), ACT.Identity,
                                           bias=G.cols[:, i - 1, ds(H1 + head, 1)]).then_inc(k_ready, 1)
                        if back:
                            act.wait_ge(c_psum, HG * (j - 1) + h + 1)
                            act.activation(ot_hi[:, h, :], c_ps[:, :], ACT.Copy).then_inc(ot_high, 1)
                    if front:
                        for p in (0, 2):
                            act.wait_ge(v_psum, PPB * j + p + 1)
                            act.activation(v_sb[:, p, :], v_ps[0][:, :], ACT.Copy).then_inc(v_ready[0], 1)
                for h in range(2):
                    act.activation(wqk_hi[:, h, :, :, :], stage_qk[:, h, :, :, :], ACT.Copy).then_inc(w_hi_act, 1)
                items(act, body)

            @block.vector
            def _(dve):
                dve.memset(prob[:, :, :], 0.0).then_inc(pt_ready, 1)
                dve.memset(G.bias_prob[:, :, H1:H1 + 1], 1.0).then_inc(ot_ready, 1)
                dve.memset(rmax[:, :], 0.0).then_inc(x_added, 1)
                dve.wait_ge(pt_ready, 1)
                dve.wait_ge(x_added, 1)
                raw = stage_vo[:, :].rearrange("p (k n) -> p k n", k=KT)
                dve.tensor_copy(wv_hi[:, :, :], raw).then_inc(w_hi_dve, 1)
                dve.wait_ge(w_hi_dve, 1)
                dve.tensor_tensor(wv_lo[:, :, :], raw, wv_hi[:, :, :].bitcast(F32), ALU.subtract).then_inc(wv_ready, 1)
                dve.tensor_copy(cf_hi[:, :, :], G.ctx_hi[:, :, 0:BLK].bitcast(F32))
                dve.tensor_copy(cf_lo[:, :, :], G.ctx_lo[:, :, 0:BLK].bitcast(F32)).then_inc(cf_ready, 1)
                halves = [slice(0, T), slice(T, 2 * T)]

                def body(j, front, back, last):
                    for h in range(HG):
                        item = score_item(j, h, front, back)
                        if item:
                            js, hs = item
                            n = HG * js + hs
                            dve.wait_ge(s_psum, n + 1)
                            for u, half in enumerate(halves):
                                dve.tensor_reduce(rmax[half, :], s_ps[half, :, u * KP:(u + 1) * KP], X_AXIS, ALU.max).then_inc(max_done, 1)
                            if back:
                                dve.wait_ge(prob_ready, 3 * n)
                            for u, half in enumerate(halves):
                                dve.wait_ge(max_done, 2 * n + u + 1)
                                dve.tensor_tensor(soft[half, :, :], s_ps[half, :, u * KP:(u + 1) * KP],
                                                  rmax[half, :].unsqueeze(2).to_broadcast([T, PPB, KP]), ALU.subtract).then_inc(shifted, 1)
                            dve.wait_ge(exp_done, n + 1)
                            dve.tensor_reduce(rsum[:, :], soft[:, :, :], X_AXIS, ALU.add).then_inc(sum_done, 1)
                            dve.wait_ge(sum_done, n + 1)
                            dve.reciprocal(rinv[:, :], rsum[:, :]).then_inc(inv_done, 1)
                            dve.wait_ge(inv_done, n + 1)
                            if back:
                                dve.wait_ge(t_psum, n)
                            for half in halves:
                                dve.tensor_tensor(prob[half, :, half], soft[half, :, 0:T],
                                                  rinv[half, :].unsqueeze(2).to_broadcast([T, PPB, T]), ALU.mult).then_inc(prob_ready, 1)
                            dve.tensor_tensor(G.bias_prob[:, ds(PPB * (js % NBLK), PPB), ds(HG * (js // NBLK) + hs, 1)],
                                              soft[:, :, T:KP], rinv[:, :].unsqueeze(2), ALU.mult).then_inc(prob_ready, 1)
                            if last and hs == HG - 1 and h < HG - 1:
                                dve.wait_ge(prob_ready, 3 * n + 3)
                                dve.tensor_copy(bias_block[:, :, :], G.bias_prob[:, ds(PPB * (js % NBLK), PPB), :]).then_inc(block_ready, 1)
                        if back:
                            dve.wait_ge(ot_high, HG * (j - 1) + h + 1)
                            dve.tensor_tensor(ot_lo[:, h, :], c_ps[:, :], ot_hi[:, h, :].bitcast(F32),
                                              ALU.subtract).then_inc(ot_ready, 1)
                    if front:
                        for p in (1, 3):
                            dve.wait_ge(v_psum, PPB * j + p + 1)
                            dve.tensor_copy(v_sb[:, p, :], v_ps[1][:, :]).then_inc(v_ready[1], 1)
                    if back:
                        for p in range(2):
                            dve.wait_ge(o_psum, 2 * (j - 1) + p + 1)
                            x = G.x_res[:, ds(PPB * ((j - 1) % NBLK) + 2 * p, 2), :]
                            dve.tensor_tensor(x, o_ps[p][:, :, :], x, ALU.add).then_inc(x_added, 1)
                            if last:
                                dve.wait_ge(x_added, 2 * (j - 1) + p + 2)
                                for q in range(2):
                                    dve.bn_stats(G.stats[:, ds(PPB * ((j - 1) % NBLK) + 2 * p + q, 1), :].rearrange("p o s -> p (o s)"),
                                                 G.x_res[:, ds(PPB * ((j - 1) % NBLK) + 2 * p + q, 1), :].rearrange("p o d -> p (o d)"))
                items(dve, body)


def mlp_operands(m, w1_dram, b1_dram, w2_dram, b2_dram):
    w = Operands()
    w.w1, w.w2 = m.sb("w1", [P, KT, FF]), m.sb("w2", [P, FT, D])
    w.b1_rows, w.b2 = m.sb("b1_rows", [FT, P]), m.sb("b2", [P, D])
    w.w_loads = [(w.w1[:, :, :], w1_dram.rearrange("(k p) n -> p k n", p=P)),
                 (w.w2[:, :, :], w2_dram.rearrange("(f p) n -> p f n", p=P))]
    w.small_loads = [(w.b1_rows[:, :], b1_dram.rearrange("(f p) -> f p", p=P)),
                     (w.b2[:, :], b2_dram.rearrange("(o n) -> o n", o=1).partition_broadcast(P))]
    return w


def mlp_split(m, w, loaded):
    w.w1_hi, w.w1_lo = (m.sb(n, [P, KT, FF], F32R) for n in ("w1_hi", "w1_lo"))
    w.w2_hi, w.w2_lo = (m.sb(n, [P, FT, D], F32R) for n in ("w2_hi", "w2_lo"))
    w.splits = [(w.w1[:, k, :], w.w1_hi[:, k, :], w.w1_lo[:, k, :]) for k in range(KT)] + \
               [tuple(t[:, f:f + FT // 2, :] for t in (w.w2, w.w2_hi, w.w2_lo)) for f in (0, FT // 2)]
    w.loaded = loaded
    return w


def phase_mlp(nc, G, tag, feat_hi, feat_lo, w, func, join_context=False, loads=()):
    LAG, RING = 2, 4
    with Mem(nc, tag, G.psum) as m:
        w1_hi, w1_lo, w2_hi, w2_lo = w.w1_hi, w.w1_lo, w.w2_hi, w.w2_lo
        b1 = m.sb("b1", [P, FT])
        act_raw = [m.sb(f"act_raw{n}", [P, BLK]) for n in range(2)]
        act_hi = [m.sb(f"act_hi{n}", [P, BLK], F32R) for n in range(RING)]
        act_lo = [m.sb(f"act_lo{n}", [P, BLK], F32R) for n in range(RING)]
        hid_ps = [m.ps(f"hid_ps{n}", (P, BLK)) for n in range(RING)]
        out_ps = [m.ps(f"out_ps{n}", (P, D)) for n in range(PPB)]
        arrived, b1_psum, b1_done, b2_added = (m.sem(n) for n in ("arrived", "b1_psum", "b1_done", "b2_added"))
        hid_psum, raw_done, hi_done, act_ready, out_psum, x_done = (m.sem(n) for n in
            ("hid_psum", "raw_done", "hi_done", "act_ready", "out_psum", "x_done"))
        with nc.Block() as block:
            @block.sync
            def _(sp):
                load(nc, sp, loads, arrived)

            @block.gpsimd
            def _(pool):
                for p in range(PAIRS):
                    pool.tensor_tensor(G.x_res[:, p, :], G.x_res[:, p, :], w.b2[:, :], ALU.add).then_inc(b2_added, 1)
                if join_context:
                    for k in range(KT):
                        for q in range(NBLK):
                            whole, hi, lo = (t[:, k, q * BLK:(q + 1) * BLK] for t in (G.ctx_f, G.ctx_hi, G.ctx_lo))
                            pool.tensor_tensor(whole, hi.bitcast(F32), lo.bitcast(F32), ALU.add)

            @block.tensor
            def _(pe):
                pe.transpose(hid_ps[0][:, 0:FT], w.b1_rows[:, :], G.ident[0:FT, 0:FT]).then_inc(b1_psum, 1)
                pe.wait_ge(b1_done, 1)

                def up(j, f, first):
                    n = FT * j + f
                    if not first or f >= RING:
                        pe.wait_ge(raw_done, n - RING + 1)
                    for k in range(KT):
                        cols = slice(f * P, (f + 1) * P)
                        for t, (a, b) in enumerate(split_products(w1_hi[:, k, cols], w1_lo[:, k, cols],
                                                                  feat_hi[:, k, ds(j * BLK, BLK)],
                                                                  feat_lo[:, k, ds(j * BLK, BLK)])):
                            mm = pe.matmul(hid_ps[f % RING][:, :], a, b, start=(k == 0 and t == 0),
                                           stop=(k == KT - 1 and t == 2))
                    mm.then_inc(hid_psum, 1)

                def down(j, f, first):
                    pe.wait_ge(act_ready, FT * j + f + 1)
                    for p in range(PPB):
                        if f == 0 and not first:
                            pe.wait_ge(x_done, PPB * (j - 1) + p + 1)
                        cols = slice(p * P, (p + 1) * P)
                        for t, (a, b) in enumerate(split_products(act_hi[f % RING][:, cols], act_lo[f % RING][:, cols],
                                                                  w2_hi[:, f, :], w2_lo[:, f, :])):
                            mm = pe.matmul(out_ps[p][:, :], a, b, start=(f == 0 and t == 0), stop=(f == FT - 1 and t == 2))
                        if f == FT - 1:
                            mm.then_inc(out_psum, 1)

                def block_of_tokens(j, first):
                    for f in range(FT):
                        up(j, f, first)
                        if f >= LAG:
                            down(j, f - LAG, first)
                    for f in range(FT - LAG, FT):
                        down(j, f, first)
                block_of_tokens(0, True)
                with pe.Fori(1, NBLK) as j:
                    block_of_tokens(j, False)

            @block.scalar
            def _(act):
                act.wait_ge(b1_psum, 1)
                act.activation(b1[:, :], hid_ps[0][:, 0:FT], ACT.Copy).then_inc(b1_done, 1)
                act.wait_ge(b1_done, 1)

                def block_of_tokens(j, first):
                    for f in range(FT):
                        n = FT * j + f
                        act.wait_ge(hid_psum, n + 1)
                        if not first or f >= 2:
                            act.wait_ge(act_ready, n - 1)
                        act.activation(act_raw[f % 2][:, :], hid_ps[f % RING][:, :], func, bias=b1[:, f:f + 1]).then_inc(raw_done, 1)
                block_of_tokens(0, True)
                with act.Fori(1, NBLK) as j:
                    block_of_tokens(j, False)

            @block.vector
            def _(dve):
                def block_of_tokens(j, first):
                    for f in range(FT):
                        n = FT * j + f
                        dve.wait_ge(raw_done, n + 1)
                        dve.tensor_copy(act_hi[f % RING][:, :], act_raw[f % 2][:, :]).then_inc(hi_done, 1)
                        dve.wait_ge(hi_done, n + 1)
                        dve.tensor_tensor(act_lo[f % RING][:, :], act_raw[f % 2][:, :], act_hi[f % RING][:, :].bitcast(F32),
                                          ALU.subtract).then_inc(act_ready, 1)
                    if first:
                        dve.wait_ge(b2_added, PAIRS)
                    for p in range(PPB):
                        dve.wait_ge(out_psum, PPB * j + p + 1)
                        x = G.x_res[:, ds(PPB * j + p, 1), :]
                        dve.tensor_tensor(x, out_ps[p][:, :], x, ALU.add).then_inc(x_done, 1)
                block_of_tokens(0, True)
                with dve.Fori(1, NBLK) as j:
                    block_of_tokens(j, False)


UNITS = 4


def wait(eng, sem, value):
    if not (isinstance(value, int) and value <= 0):
        eng.wait_ge(sem, value)


MAKE_V, SCORE, EXP, NORMALIZE, TURN, VALUES, OUTPUT, ADD = 3, 2, 3, 4, 5, 6, 7, 7


def unit_slots(j, front, back):
    for slot in range(2 * UNITS):
        def at(lag, slot=slot):
            ahead, t = divmod(slot - lag, UNITS)
            return (2 * j + ahead, t, ahead % 2) if (front if ahead >= 0 else back) else None
        yield slot % UNITS, at


def narrow_operands(m, A, layer):
    two = layer == 2
    w = Operands()
    w.wq = m.sb(f"wq{layer}", [P, KT, D])
    w.wkv = m.sb(f"wkv{layer}", [P, KT, 2, 64] if two else [P, KT, 2 * D])
    w.wo = m.sb(f"wo{layer}", [P, KT, D])
    w.rows = m.sb(f"rows{layer}", [4 if two else 6, P])
    w.o_bias = m.sb(f"o_bias{layer}", [P, D])
    if not two:
        w.mask = m.sb(f"mask{layer}", [P, B * T], I32)
    if two:
        name = lambda n: A[f"L2_xattn_{n}"]
        q_bias = name("bq").rearrange("(v c g d) -> c g v d", v=8, c=2, g=2)
        w.loads = [(w.rows[c:c + 1, 64 * g:64 * g + 64].rearrange("o (v d) -> o v d", d=8), q_bias[c:c + 1, g]) for c in range(2) for g in range(2)] + \
                  [(w.rows[r:r + 1, 64 * g:64 * g + 64], name(n).rearrange("(o n) -> o n", o=1)) for r, n in ((2, "bk"), (3, "bv")) for g in range(2)] + \
                  [(w.wq[:, :, :], name("Wq").rearrange("(k p) n -> p k n", p=P)),
                   (w.wkv[:, :, 0, :], name("Wk").rearrange("(k p) n -> p k n", p=P)),
                   (w.wkv[:, :, 1, :], name("Wv").rearrange("(k p) n -> p k n", p=P))] + \
                  [(w.wo[64 * g + 8 * v:64 * g + 8 * v + 8, :, :],
                    name("Wo")[32 * v:32 * v + 32, :].rearrange("(c g d) n -> g d c n", c=2, g=2)[g]) for v in range(8) for g in range(2)]
        bias = name("bo")
    else:
        name = lambda n: A[f"L3_xattn_{n}"]
        kv_bias = name("kv_b").rearrange("(c p w) -> w c p", c=2, w=2)
        w.loads = [(w.rows[0:2, :], name("q_b").rearrange("(c p) -> c p", p=P)),
                   (w.rows[2:4, :], kv_bias[0]), (w.rows[4:6, :], kv_bias[1]),
                   (w.wq[:, :, :], name("q_w").rearrange("(k p) n -> p k n", p=P)),
                   (w.wkv[:, :, :], name("kv_w").rearrange("(k p) n -> p k n", p=P)),
                   (w.wo[:, :, :], name("out_w").rearrange("(k p) n -> p k n", p=P)),
                   (w.mask[:, :], A["mask_BxS2_ik0"].rearrange("(o b) t -> o (b t)", o=1).partition_broadcast(P))]
        bias = name("out_b")
    w.loads.append((w.o_bias[:, :], bias.rearrange("(o n) -> o n", o=1).partition_broadcast(P)))
    return w


def phase_narrow_attention(nc, A, G, layer, w, dst, loads=()):
    two = layer == 2
    GR, NK = (8, 64) if two else (4, 128)
    HD = 8 if two else 16
    score_scale = float(HD) ** -0.5 if two else 1.0 / HD
    dropped = -1e30
    VR = 64 if two else P
    SKEW = 80 if two else 160
    with Mem(nc, f"l{layer}", G.psum) as m:
        kv_cols = 64 if two else D
        BV = 3 if two else 4
        KC = P if two else D
        wq = m.sb("wq", [P, KT, D]) if two else w.wq
        wk = m.sb("wk", [P, KT, KC])
        wv = m.sb("wv", [P, KT, kv_cols])
        wo = w.wo
        cols = m.sb("cols", [P, 8])
        mask = m.sb("mask", [P, B, NK])
        spread = m.sb("spread", [P, 8])
        odd_even = m.sb("odd_even", [P, 2])
        q_bd = [m.sb(f"q_bd{n}", [P, 2, 2, P] if two else [P, 2, 2, 8 * T]) for n in range(2)]
        k_bd = [m.sb(f"k_bd{n}", [P, 8, P] if two else [P, 2, 2 * P]) for n in range(2)]
        v_bd = [m.sb(f"v_bd{n}", [P, 2, 4 * SKEW] if two else [P, 2, 2, 4 * SKEW]) for n in range(2)]
        vx = m.sb("vx", [P, KT, 2 * T] if two else [P, KT, 2, 2, T])
        soft = [m.sb(f"soft{n}", [P, GR, NK]) for n in range(UNITS)]
        prob = [m.sb(f"prob{n}", [P, GR, NK]) for n in range(2)]
        pt = [m.sb(f"pt{n}", [P, 4, P]) for n in range(2)]
        ot = m.sb("ot", [P, 2, P])
        even_part = m.sb("even_part", [P, T])
        rmax, rsum, rinv = ([m.sb(f"{n}{r}", [P, GR]) for r in range(2)] for n in ("rmax", "rsum", "rinv"))
        s_ps = [m.ps(f"s_ps{n}") for n in range(2)]
        t_ps, c_ps, o_ps = m.ps("t_ps"), m.ps("c_ps", (P, P)), m.ps("o_ps", (P, D))
        q_ps = m.ps("q_ps", (P, 2, P))
        k_ps = m.ps("k_ps", (P, P) if two else (P, 2, 2, P))
        v_ps = m.ps("v_ps", (P, 1 if two else 2, kv_cols))
        mask_in, arrived, spread_made, q_zero, v_zero, bias_added = (m.sem(n) for n in
            ("mask_in", "arrived", "spread_made", "q_zero", "v_zero", "bias_added"))
        w_ready, cols_psum, cols_done, mask_done = (m.sem(n) for n in
            ("w_ready", "cols_psum", "cols_done", "mask_done"))
        vx_ready, q_psum, k_psum, v_psum, q_done, k_done, v_done = (m.sem(n) for n in
            ("vx_ready", "q_psum", "k_psum", "v_psum", "q_done", "k_done", "v_done"))
        s_psum, masked, max_done, shifted, exp_done, sum_done, inv_done, prob_ready = (m.sem(n) for n in
            ("s_psum", "masked", "max_done", "shifted", "exp_done", "sum_done", "inv_done", "prob_ready"))
        t_psum, pt_done, c_psum, even_done, ot_done, o_psum, x_done = (m.sem(n) for n in
            ("t_psum", "pt_done", "c_psum", "even_done", "ot_done", "o_psum", "x_done"))
        STEPS = PAIRS // 2

        def number(unit):
            return UNITS * unit[0] + unit[1]

        with nc.Block() as block:
            @block.sync
            def _(sp):
                if two:
                    for g in range(2):
                        sp.dma_start(mask[64 * g:64 * g + 64, :, :],
                                     A["mask_Bx1xSxS2_ff0"].rearrange("b o q t -> q (b o) t")).then_inc(mask_in, 16)
                load(nc, sp, loads, arrived)

            @block.gpsimd
            def _(pool):
                pool.memset(spread[:, :], 1.0).then_inc(spread_made, 1)
                n = 1
                for base in (0, 64) if two else (0,):
                    for cm, b0, pat in ((1, -base, -HD), (-1, base + HD - 1, HD)):
                        pool.wait_ge(spread_made, n)
                        rows_ = slice(base, base + (64 if two else P))
                        pool.affine_select(out=spread[rows_, :], in_=spread[rows_, :], compare_op=ALU.is_ge, fill=0.0,
                                           base=b0 + cm * base, pattern=[[pat, 8]], channel_multiplier=cm).then_inc(spread_made, 1)
                        n += 1
                pool.wait_ge(spread_made, n)
                for n in range(2):
                    pool.memset(v_bd[n][:, :, :] if two else v_bd[n][:, :, :, :], 0.0).then_inc(v_zero, 1)

                def body(j, front, back):
                    for i, at in unit_slots(j, front, back):
                        if at(NORMALIZE):
                            n, t = number(at(NORMALIZE)), at(NORMALIZE)[1]
                            pool.wait_ge(inv_done, n + 1)
                            wait(pool, t_psum, n - 1)
                            pool.tensor_tensor(prob[t % 2][:, :, :], soft[t][:, :, :],
                                               rinv[t % 2][:, :].unsqueeze(2).to_broadcast([P, GR, NK]), ALU.mult).then_inc(prob_ready, 1)
                        if at(SCORE):
                            n, t = number(at(SCORE)), at(SCORE)[1]
                            pool.wait_ge(max_done, n + 1)
                            pool.tensor_tensor(soft[t][:, :, :], soft[t][:, :, :],
                                               rmax[t % 2][:, :].unsqueeze(2).to_broadcast([P, GR, NK]), ALU.subtract).then_inc(shifted, 1)
                        if i == 1 and at(0):
                            pair = at(0)[0]
                            pool.tensor_tensor(dst[:, ds(pair, 1), :], G.x_res[:, ds(pair, 1), :],
                                               w.o_bias[:, :].unsqueeze(1), ALU.add).then_inc(bias_added, 1)
                skewed(pool, STEPS, body)

            @block.tensor
            def _(pe):
                n_rows = w.rows.shape[0]
                pe.transpose(c_ps[:, 0:n_rows], w.rows[:, :], G.ident[0:n_rows, 0:n_rows]).then_inc(cols_psum, 1)
                pe.wait_ge(cols_done, 1)
                pe.wait_ge(w_ready, 1)

                def accumulate(out, products):
                    for n, (a, b) in enumerate(products):
                        mm = pe.matmul(out, a, b, start=(n == 0), stop=(n == len(products) - 1))
                    return mm

                def body(j, front, back):
                    for i, at in unit_slots(j, front, back):
                        if at(TURN):
                            n, t = number(at(TURN)), at(TURN)[1]
                            pe.wait_ge(prob_ready, n + 1)
                            wait(pe, pt_done, n)
                            for q in range(4):
                                mm = pe.transpose(t_ps[:, q * P:(q + 1) * P],
                                                  prob[t % 2][:, :, :].rearrange("p g t -> p (g t)")[:, q * P:(q + 1) * P], G.ident[:, :])
                            mm.then_inc(t_psum, 1)
                        if at(SCORE):
                            pair, t, par = at(SCORE)
                            n, b, c = UNITS * pair + t, t // 2, t % 2
                            pe.wait_ge(q_done, 2 * pair + c + 1)
                            pe.wait_ge(k_done, pair + 1)
                            wait(pe, masked, n - 1)
                            out = s_ps[t % 2]
                            if two:
                                mm = accumulate(out[:, :], [(q_bd[par][:, c, b, :], k_bd[par][:, :, b * T:(b + 1) * T])])
                            else:
                                for h2 in range(4):
                                    mm = accumulate(out[:, h2 * P:(h2 + 1) * P],
                                                    [(q_bd[par][:, c, b, h2 * P:(h2 + 1) * P], k_bd[par][:, c, b * P:(b + 1) * P])])
                            mm.then_inc(s_psum, 1)
                        if i == 0 and at(0):
                            pair = at(0)[0]
                            x_new, ctx = (t[:, :, ds(pair * P, P)] for t in (G.feat_f, G.ctx_f))
                            wait(pe, q_done, 2 * pair)
                            for c in range(2):
                                mm = accumulate(q_ps[:, c, :], [(wq[:, k, c * P:(c + 1) * P], x_new[:, k]) for k in range(KT)])
                            mm.then_inc(q_psum, 1)
                            wait(pe, k_done, pair)
                            if two:
                                mm = accumulate(k_ps[:, :], [(wk[:, k, :], ctx[:, k]) for k in range(KT)])
                            else:
                                for c in range(2):
                                    for s, tokens in enumerate((ctx, x_new)):
                                        mm = accumulate(k_ps[:, c, :, s * T:(s + 1) * T],
                                                        [(wk[:, k, c * P:(c + 1) * P], tokens[:, k]) for k in range(KT)])
                            mm.then_inc(k_psum, 1)
                        if i == MAKE_V and at(MAKE_V):
                            pair = at(MAKE_V)[0]
                            pe.wait_ge(vx_ready, pair + 1)
                            wait(pe, v_done, pair)
                            for b in range(1 if two else 2):
                                mm = accumulate(v_ps[:, b, :], [(vx[:, k, :] if two else vx[:, k, b, :, :], wv[:, k, :])
                                                                for k in range(KT)])
                            mm.then_inc(v_psum, 1)
                        if at(OUTPUT) and at(OUTPUT)[1] == UNITS - 1:
                            pair = at(OUTPUT)[0]
                            pe.wait_ge(ot_done, UNITS * (pair + 1))
                            pe.wait_ge(x_done, pair + 1)
                            accumulate(o_ps[:, :], [(ot[:, c, :], wo[:, c, :]) for c in range(KT)]).then_inc(o_psum, 1)
                        if at(VALUES):
                            pair, t, par = at(VALUES)
                            n, b, c = UNITS * pair + t, t // 2, t % 2
                            pe.wait_ge(pt_done, n + 1)
                            pe.wait_ge(v_done, pair + 1)
                            wait(pe, ot_done, n)
                            v = v_bd[par][:, b, :] if two else v_bd[par][:, b, c, :]
                            accumulate(c_ps[0:VR, :], [(v[:, VR * q:VR * (q + 1)], pt[t % 2][:, q, :]) for q in range(4)]).then_inc(c_psum, 1)
                skewed(pe, STEPS, body)

            @block.scalar
            def _(act):
                act.wait_ge(cols_psum, 1)
                n_rows = w.rows.shape[0]
                act.activation(cols[:, 0:n_rows], c_ps[:, 0:n_rows], ACT.Copy).then_inc(cols_done, 1)
                act.wait_ge(cols_done, 1)
                if two:
                    act.wait_ge(q_zero, 2)
                act.wait_ge(v_zero, 2)
                halves = [slice(0, 64), slice(64, P)]

                def body(j, front, back):
                    for i, at in unit_slots(j, front, back):
                        if at(EXP):
                            act.wait_ge(shifted, number(at(EXP)) + 1)
                            tile = soft[at(EXP)[1]]
                            act.activation(tile[:, :, :], tile[:, :, :], ACT.Exp).then_inc(exp_done, 1)
                        if at(TURN):
                            act.wait_ge(t_psum, number(at(TURN)) + 1)
                            act.activation(pt[at(TURN)[1] % 2][:, :, :].rearrange("p q n -> p (q n)"), t_ps[:, :], ACT.Copy).then_inc(pt_done, 1)
                        prep, half = (at(0)[0], at(0)[2]) if at(0) else (None, None)
                        if prep is not None and i == 0 and two:
                            act.wait_ge(q_psum, prep + 1)
                            for c in range(2):
                                for h in halves:
                                    a = act.activation(q_bd[half][h, c, :, h], q_ps[h, c, :].rearrange("p (b q) -> p b q", b=2),
                                                       ACT.Identity, bias=cols[h, c:c + 1])
                                a.then_inc(q_done, 1)
                        if prep is not None and i == 0 and not two:
                            act.wait_ge(k_psum, prep + 1)
                            for c in range(2):
                                a = act.activation(k_bd[half][:, c, :], k_ps[:, c, :, :].rearrange("p b t -> p (b t)"),
                                                   ACT.Identity, bias=cols[:, 2 + c:3 + c])
                            a.then_inc(k_done, 1)
                        if prep is not None and i == MAKE_V:
                            act.wait_ge(v_psum, prep + 1)
                            for n in range(2):
                                if two:
                                    for u, h in enumerate(halves):
                                        a = act.activation(
                                            v_bd[half][h, n, :].rearrange("p (q x) -> p q x", x=SKEW)[:, :, 8 * u:8 * u + 8],
                                            v_ps[halves[n], 0, :].rearrange("p (q u d) -> p q u d", q=4, u=2)[:, :, u, :], ACT.Copy)
                                else:
                                    a = act.activation(
                                        v_bd[half][:, n, :, :].rearrange("p c (h x) -> p c h x", x=SKEW)[:, :, :, 0:2 * HD],
                                        v_ps[:, n, :].rearrange("p (c h x) -> p c h x", c=2, h=4), ACT.Copy)
                            a.then_inc(v_done, 1)
                        if at(VALUES):
                            n, b, c = number(at(VALUES)), at(VALUES)[1] // 2, at(VALUES)[1] % 2
                            act.wait_ge(c_psum, n + 1)
                            if two:
                                for g, h in enumerate(halves):
                                    a = act.activation(ot[h, c, b * T:(b + 1) * T], c_ps[0:VR, g * T:(g + 1) * T],
                                                       ACT.Identity, bias=cols[0:VR, BV:BV + 1])
                                a.then_inc(ot_done, 1)
                            else:
                                act.activation(even_part[:, :], c_ps[:, 0:T], ACT.Identity, bias=cols[:, BV + c:BV + c + 1],
                                               scale=odd_even[:, 0:1]).then_inc(even_done, 1)
                skewed(act, STEPS, body)

            @block.vector
            def _(dve):
                if two:
                    for n in range(2):
                        dve.memset(q_bd[n][:, :, :, :], 0.0).then_inc(q_zero, 1)
                for k in range(KT):
                    if two:
                        keys = w.wkv[:, k, 0, :].unsqueeze(1).to_broadcast([P, 2, 64])
                        values = w.wkv[:, k, 1, :]
                        dve.tensor_copy(wk[:, k, :].rearrange("p (g c) -> p g c", g=2), keys)
                        dve.tensor_copy(wq[:, k, :].rearrange("p (g v d) -> p g v d", g=4, v=8),
                                        w.wq[:, k, :].rearrange("p (v g d) -> p g v d", v=8, g=4))
                    else:
                        kv = w.wkv[:, k, :].rearrange("p (c w) -> p w c", w=2)
                        values = kv[:, 1, :]
                        dve.tensor_copy(wk[:, k, :], kv[:, 0, :])
                    copied = dve.tensor_copy(wv[:, k, :], values)
                copied.then_inc(w_ready, 1)
                dve.memset(rmax[0][:, :], 0.0).then_inc(x_done, 1)
                dve.wait_ge(x_done, 1)
                if not two:
                    dve.wait_ge(spread_made, 3)
                    dve.tensor_reduce(odd_even[:, :], spread[:, :].rearrange("p (h e) -> p e h", e=2), X_AXIS, ALU.add).then_inc(mask_done, 1)
                    dve.memset(mask[:, :, T:2 * T], 0.0)
                if two:
                    dve.wait_ge(mask_in, 32)
                else:
                    dve.tensor_scalar(mask[:, :, 0:T], w.mask[:, :].rearrange("p (b t) -> p b t", b=B), 0, dropped,
                                      ALU.is_equal, ALU.mult).then_inc(mask_done, 1)
                    dve.wait_ge(mask_done, 2)
                dve.wait_ge(spread_made, 5 if two else 3)
                dve.wait_ge(cols_done, 1)

                def make_vx(prep):
                    wait(dve, v_psum, prep)
                    for k in range(KT):
                        for s, src in enumerate((G.ctx_f,) if two else (G.ctx_f, G.feat_f)):
                            tokens = src[:, k, ds(prep * P, P)]
                            if two:
                                v = dve.tensor_copy(vx[:, k, :], tokens)
                            else:
                                v = dve.tensor_copy(vx[:, k, :, s, :], tokens.rearrange("p (b t) -> p b t", b=2))
                    v.then_inc(vx_ready, 1)

                def add_output(pair):
                    dve.wait_ge(o_psum, pair + 1)
                    dve.wait_ge(bias_added, pair + 1)
                    x = dst[:, ds(pair, 1), :]
                    dve.tensor_tensor(x, o_ps[:, :], x, ALU.add).then_inc(x_done, 1)

                def body(j, front, back):
                    for i, at in unit_slots(j, front, back):
                        prep, half = (at(0)[0], at(0)[2]) if at(0) else (None, None)
                        if at(NORMALIZE):
                            n, t = number(at(NORMALIZE)), at(NORMALIZE)[1]
                            dve.wait_ge(exp_done, n + 1)
                            dve.tensor_reduce(rsum[t % 2][:, :], soft[t][:, :, :], X_AXIS, ALU.add).then_inc(sum_done, 1)
                            dve.wait_ge(sum_done, n + 1)
                            wait(dve, prob_ready, n - 1)
                            dve.reciprocal(rinv[t % 2][:, :], rsum[t % 2][:, :]).then_inc(inv_done, 1)
                        if prep is not None and i == 2:
                            make_vx(prep)
                        if at(SCORE):
                            pair, t, _ = at(SCORE)
                            n, b = UNITS * pair + t, t // 2
                            s3 = s_ps[t % 2][:, :].rearrange("p (g t) -> p g t", g=GR)
                            dve.wait_ge(s_psum, n + 1)
                            wait(dve, prob_ready, n - 3)
                            dve.scalar_tensor_tensor(soft[t][:, :, :], s3, score_scale,
                                                     mask[:, ds(2 * pair + b, 1), :].to_broadcast([P, GR, NK]),
                                                     ALU.mult, ALU.add).then_inc(masked, 1)
                            dve.wait_ge(masked, n + 1)
                            wait(dve, shifted, n - 1)
                            dve.tensor_reduce(rmax[t % 2][:, :], soft[t][:, :, :], X_AXIS, ALU.max).then_inc(max_done, 1)
                        if prep is not None and i == 0 and two:
                            dve.wait_ge(k_psum, prep + 1)
                            dve.scalar_tensor_tensor(k_bd[half][:, :, :], k_ps[:, :].unsqueeze(1).to_broadcast([P, 8, P]),
                                                     cols[:, 2:3], spread[:, :].unsqueeze(2).to_broadcast([P, 8, P]),
                                                     ALU.add, ALU.mult).then_inc(k_done, 1)
                        if prep is not None and i < 2 and not two:
                            c = i
                            dve.wait_ge(q_psum, prep + 1)
                            for b in range(2):
                                q = dve.scalar_tensor_tensor(
                                    q_bd[half][:, c, b, :].rearrange("p (h t) -> p h t", h=8),
                                    q_ps[:, c, b * T:(b + 1) * T].unsqueeze(1).to_broadcast([P, 8, T]),
                                    cols[:, c:c + 1], spread[:, :].unsqueeze(2).to_broadcast([P, 8, T]),
                                    ALU.add, ALU.mult)
                            q.then_inc(q_done, 1)
                        if at(ADD) and at(ADD)[1] == UNITS - 1:
                            add_output(at(ADD)[0])
                        if at(VALUES) and not two:
                            n, b, c = number(at(VALUES)), at(VALUES)[1] // 2, at(VALUES)[1] % 2
                            dve.wait_ge(even_done, n + 1)
                            dve.scalar_tensor_tensor(ot[:, c, b * T:(b + 1) * T], c_ps[:, T:2 * T], odd_even[:, 1:2],
                                                     even_part[:, :], ALU.mult, ALU.add).then_inc(ot_done, 1)
                skewed(dve, STEPS, body)


class Global:
    pass


def build(nc, A, out):
    G = Global()
    with Mem(nc, "g") as m:
        G.psum = m.stack.enter_context(nc.psum_tensor("psum", [P, PSUM_BANKS * BANK], F32))
        G.x_res = m.sb("x_res", [P, PAIRS, D])
        G.ident = m.sb("ident", [P, P])
        G.minus_half = m.sb("minus_half", [P, 2 * PAIRS])
        G.stats = m.sb("stats", [P, PAIRS, 6])
        G.ctx_f = m.sb("ctx_f", [P, KT, TOK])
        layer2 = narrow_operands(m, A, 2)
        with Mem(nc, "split") as ms:
            G.ctx_hi = ms.sb("ctx_hi", [P, KT, TOK], F32R)
            G.ctx_lo = ms.sb("ctx_lo", [P, KT, TOK], F32R)
            G.cols = ms.sb("cols", [P, 2, 5 * H1])
            G.bvo = ms.sb("bvo", [H1 + 1, D])
            with Mem(nc, "c") as mc:
                G.ctx_tok = mc.sb("ctx_tok", [P, PAIRS, D])
                G.w_t = mc.sb("w_t", [P, 4, P])
                G.bias0 = mc.sb("bias0", [P, 4])
                G.obias = mc.sb("obias", [P, 1])
                G.xn = mc.sb("xn", [P, 2 * PAIRS, D])
                phase_setup(nc, A, G)
                phase_layer0(nc, A, G)
            G.bias_prob = ms.sb("bias_prob", [P, PAIRS, H1 + 1])
            feat = [ms.sb(n, [P, KT, TOK], F32R) for n in ("feat_hi", "feat_lo")]
            G.feat_hi, G.feat_lo = feat
            for i in (1, 2):
                with Mem(nc, f"w{i}") as mw:
                    w = attention_operands(mw, A, i)
                    phase_features(nc, G, f"ln{i}", G.x_res, *feat, "ln", 1e-5,
                                   A[f"L1_xattn_ln{i}_scale"], A[f"L1_xattn_ln{i}_offset"], loads=w.loads,
                                   attention=(i, A[f"L1_xattn_wo{i}"], A[f"L1_xattn_bo{i}"]))
                    phase_layer1_attention(nc, A, G, i, w)
            with Mem(nc, "m1") as mm:
                mlp = mlp_operands(mm, *(A[f"L1_xattn_{n}"] for n in ("w_fc1", "b_fc1", "w_fc2", "b_fc2")))
                mlp = mlp_split(mm, mlp, loaded=False)
                phase_features(nc, G, "ln3", G.x_res, *feat, "ln", 1e-5,
                               A["L1_xattn_ln_mlp_scale"], A["L1_xattn_ln_mlp_offset"], mlp=mlp)
                phase_mlp(nc, G, "mlp1", *feat, mlp, ACT.Gelu, join_context=True, loads=layer2.loads)
        attn_out = m.sb("attn_out", [P, PAIRS, D])
        mlp = mlp_operands(m, *(A[f"L3_xattn_{n}"] for n in ("mlp_w1", "mlp_b1", "mlp_w2", "mlp_b2")))
        with Mem(nc, "narrow") as mn:
            G.feat_f = mn.sb("feat_f", [P, KT, TOK])
            layer3 = narrow_operands(mn, A, 3)
            phase_features(nc, G, "ft2", G.x_res, G.feat_f, None, "plain")
            phase_narrow_attention(nc, A, G, 2, layer2, G.x_res, loads=layer3.loads)
            phase_features(nc, G, "ln4", G.x_res, G.feat_f, None, "ln", 1e-6,
                           A["L2_xattn_gamma"], A["L2_xattn_beta"], update=True, have_stats=False)
            phase_narrow_attention(nc, A, G, 3, layer3, attn_out, loads=mlp.w_loads + mlp.small_loads)
        with Mem(nc, "three") as mt:
            feat = [mt.sb(n, [P, KT, TOK], F32R) for n in ("feat_hi", "feat_lo")]
            mlp = mlp_split(mt, mlp, loaded=True)
            phase_features(nc, G, "rms", attn_out, *feat, "rms", 1e-6, A["L3_xattn_postnorm_w"], mlp=mlp, have_stats=False)
            phase_mlp(nc, G, "mlp3", *feat, mlp, ACT.Gelu_apprx_tanh)
        phase_store(nc, G.x_res, out)


def phase_store(nc, src, out):
    with Mem(nc, "st") as m:
        stored = m.sem("stored")
        with nc.Block() as block:
            @block.sync
            def _(sp):
                sp.dma_start(out.rearrange("(p b) t d -> (b t) p d", b=2), src[:, :, :]).then_inc(stored, 16)
                sp.wait_ge(stored, 16)


def kernel(**inputs):
    import numpy as _np
    import concourse.bacc as _bacc
    from concourse import mybir as _mybir
    from concourse.bass_utils import run_bass_kernel_spmd as _run

    nc = _bacc.Bacc("TRN2", target_bir_lowering=False, num_devices=1)
    arrays, args = {}, {}
    for name, value in inputs.items():
        a = _np.ascontiguousarray(value)
        arrays[f"in_{name}"] = a
        args[name] = nc.dram_tensor(f"in_{name}", a.shape, _mybir.dt.from_np(a.dtype), kind="ExternalInput").ap()
    out = nc.dram_tensor("out_0", (B, T, D), F32, kind="ExternalOutput").ap()
    build(nc, args, out)
    r = _run(nc, [arrays], core_ids=[0])
    return r.results[0]["out_0"]
```
